# Optimizing a Trainium2 kernel written in Bass

```python
import numpy as np
import jax
import jax.numpy as jnp

def _softmax(x, axis=-1):
    return jax.nn.softmax(x, axis=axis)

def _gelu(x):
    return jax.nn.gelu(x, approximate=True)

def _silu(x):
    return jax.nn.silu(x)

def _sigmoid(x):
    return jax.nn.sigmoid(x)

def _layernorm(x, axis=-1, eps=1e-05):
    m = jnp.mean(x, axis=axis, keepdims=True)
    v = jnp.var(x, axis=axis, keepdims=True)
    return (x - m) / jnp.sqrt(v + eps)

def _scatter_add(tgt, idx, src, axis=0):
    return tgt.at[idx].add(src)

def _segment_sum(src, seg, n):
    return jax.ops.segment_sum(src, seg, n)
kernel_name = 'mk_gnn_ffn_d2_gnn_r32_20dd61'

def setup_inputs(seed: int=0):
    np.random.seed(seed)
    _w = jnp.asarray

    def _rec_inputs():
        import jax
        import jax.numpy as jnp
        _gk = jax.random.key(seed)
        x = -0.0002117 + 1 * jax.random.normal(jax.random.fold_in(_gk, 1), (3125, 256), jnp.float32)
        _s = jax.random.randint(jax.random.fold_in(_gk, 2), (25000,), 0, 3125, jnp.int32)
        _d = jax.random.randint(jax.random.fold_in(_gk, 3), (25000,), 0, 3125, jnp.int32)
        _loop = jnp.arange(3125, dtype=jnp.int32)
        src = jnp.concatenate([_s, _d, _loop])
        dst = jnp.concatenate([_d, _s, _loop])
        _o = jnp.argsort(dst, stable=True)
        src = src[_o]
        dst = dst[_o]
        edge_attr_4 = 0.00117183 + 1.0004 * jax.random.normal(jax.random.fold_in(_gk, 12), (53125, 4), jnp.float32)
        edge_attr_8 = -0.000615933 + 0.999959 * jax.random.normal(jax.random.fold_in(_gk, 13), (53125, 8), jnp.float32)
        node_vec1 = jax.random.uniform(jax.random.fold_in(_gk, 14), (3125, 1), jnp.float32, 0.0, 1)
        return (x, src, dst, edge_attr_4, edge_attr_8, node_vec1)
    x, src, dst, edge_attr_4, edge_attr_8, node_vec1 = _rec_inputs()

    def _L0_gnn_setup():
        import jax, jax.numpy as jnp
        import numpy as np
        N = 3125
        E = 50000
        D = 256
        BN_EPS = 1e-05
        key = jax.random.key(seed)
        ks = jax.random.split(key, 6)
        node_feats = jax.random.normal(ks[0], (N, D), dtype=jnp.float32)
        src = jax.random.randint(ks[1], (E,), 0, N, dtype=jnp.int64)
        dst = jax.random.randint(ks[2], (E,), 0, N, dtype=jnp.int64)
        eps = jnp.zeros((1,), dtype=jnp.float32)
        W1 = jax.random.normal(ks[3], (D, 2 * D), dtype=jnp.float32) * (1.0 / np.sqrt(D))
        b1 = jnp.zeros((2 * D,), dtype=jnp.float32)
        W2 = jax.random.normal(ks[4], (2 * D, D), dtype=jnp.float32) * (1.0 / np.sqrt(2 * D))
        b2 = jnp.zeros((D,), dtype=jnp.float32)
        gamma = jnp.ones((D,), dtype=jnp.float32)
        beta = jnp.zeros((D,), dtype=jnp.float32)
        return {'node_feats': node_feats, 'src': src, 'dst': dst, 'eps': eps, 'W1': W1, 'b1': b1, 'W2': W2, 'b2': b2, 'gamma': gamma, 'beta': beta}
    _L0_gnn_all = _L0_gnn_setup()
    _L0_gnn_in = {k: v for k, v in _L0_gnn_all.items() if k in ('eps', 'W1', 'b1', 'W2', 'b2', 'gamma', 'beta')}
    del _L0_gnn_all

    def _L0_ffn_setup():
        import jax, jax.numpy as jnp
        import numpy as np
        B, S, H, F, E, K = (8, 128, 256, 512, 16, 2)
        EPS = 1e-05
        key = jax.random.key(seed)
        ks = jax.random.split(key, 9)
        sc = 0.02
        return {'x': jax.random.normal(ks[0], (B, S, H), dtype=jnp.float32), 'gate_w': jax.random.normal(ks[1], (H, E), dtype=jnp.float32) * sc, 'gate_b': jnp.zeros((E,), dtype=jnp.float32), 'w1': jax.random.normal(ks[2], (E, H, F), dtype=jnp.float32) * sc, 'b1': jnp.zeros((E, F), dtype=jnp.float32), 'w2': jax.random.normal(ks[3], (E, F, H), dtype=jnp.float32) * sc, 'b2': jnp.zeros((E, H), dtype=jnp.float32), 'gamma': jnp.ones((H,), dtype=jnp.float32), 'beta': jnp.zeros((H,), dtype=jnp.float32)}
    _L0_ffn_all = _L0_ffn_setup()
    _L0_ffn_in = {k: v for k, v in _L0_ffn_all.items() if k in ('gate_w', 'gate_b', 'w1', 'b1', 'w2', 'b2', 'gamma', 'beta')}
    del _L0_ffn_all

    def _L1_gnn_setup():
        import jax, jax.numpy as jnp
        import numpy as np
        import math
        N = 30000
        E = 18750
        MUL = 64
        NES = 8
        FCN = 64
        NUM_NEIGHBORS = 20.0
        SILU_NORM = 1.679
        INV_SQRT3 = 1.0 / math.sqrt(3.0)

        def _split(x):
            return (x[:, :MUL], x[:, MUL:].reshape(-1, MUL, 3))
        key = jax.random.key(seed)
        ks = jax.random.split(key, 16)
        inp = {'node_input': jax.random.normal(ks[0], (N, 4 * MUL), jnp.float32), 'node_attr': jnp.ones((N, 1), jnp.float32), 'edge_src': jax.random.randint(ks[1], (E,), 0, N), 'edge_dst': jax.random.randint(ks[2], (E,), 0, N), 'edge_attr': jax.random.normal(ks[3], (E, 4), jnp.float32), 'edge_scalars': jax.random.normal(ks[4], (E, NES), jnp.float32), 'sc_w0': jax.random.normal(ks[5], (MUL, MUL), jnp.float32), 'sc_w1': jax.random.normal(ks[6], (MUL, MUL), jnp.float32), 'lin1_w0': jax.random.normal(ks[7], (MUL, MUL), jnp.float32), 'lin1_w1': jax.random.normal(ks[8], (MUL, MUL), jnp.float32), 'fc_w1': jax.random.normal(ks[9], (NES, FCN), jnp.float32), 'fc_w2': jax.random.normal(ks[10], (FCN, 4 * MUL), jnp.float32), 'lin2_w00': jax.random.normal(ks[11], (MUL, MUL), jnp.float32), 'lin2_w01': jax.random.normal(ks[12], (MUL, MUL), jnp.float32), 'lin2_w10': jax.random.normal(ks[13], (MUL, MUL), jnp.float32), 'lin2_w11': jax.random.normal(ks[14], (MUL, MUL), jnp.float32)}
        return inp
    _L1_gnn_all = _L1_gnn_setup()
    _L1_gnn_in = {k: v for k, v in _L1_gnn_all.items() if k in ('sc_w0', 'sc_w1', 'lin1_w0', 'lin1_w1', 'fc_w1', 'fc_w2', 'lin2_w00', 'lin2_w01', 'lin2_w10', 'lin2_w11')}
    del _L1_gnn_all

    def _L1_ffn_setup():
        import jax, jax.numpy as jnp
        import numpy as np
        C = 256
        HID = 1024
        E = 8
        TEMP = 1.0
        key = jax.random.key(seed)
        ks = jax.random.split(key, 7)
        x = jax.random.normal(ks[0], (8, 512, C), dtype=jnp.float32)
        W1 = jax.random.normal(ks[1], (C, HID), dtype=jnp.float32) * 0.02
        b1 = jnp.zeros((HID,), dtype=jnp.float32)
        Wg = jax.random.normal(ks[2], (HID, E), dtype=jnp.float32) * 0.02
        bg = jnp.zeros((E,), dtype=jnp.float32)
        Wd = jax.random.normal(ks[3], (E, HID, C), dtype=jnp.float32) * 0.02
        bd = jnp.zeros((E, C), dtype=jnp.float32)
        return {'x': x, 'W1': W1, 'b1': b1, 'Wg': Wg, 'bg': bg, 'Wd': Wd, 'bd': bd}
    _L1_ffn_all = _L1_ffn_setup()
    _L1_ffn_in = {k: v for k, v in _L1_ffn_all.items() if k in ('W1', 'b1', 'Wg', 'bg', 'Wd', 'bd')}
    del _L1_ffn_all
    return {'x': x, 'src': src, 'dst': dst, 'edge_attr_4': edge_attr_4, 'edge_attr_8': edge_attr_8, 'node_vec1': node_vec1, 'L0_gnn_eps': _L0_gnn_in['eps'], 'L0_gnn_W1': _L0_gnn_in['W1'], 'L0_gnn_b1': _L0_gnn_in['b1'], 'L0_gnn_W2': _L0_gnn_in['W2'], 'L0_gnn_b2': _L0_gnn_in['b2'], 'L0_gnn_gamma': _L0_gnn_in['gamma'], 'L0_gnn_beta': _L0_gnn_in['beta'], 'L0_ffn_gate_w': _L0_ffn_in['gate_w'], 'L0_ffn_gate_b': _L0_ffn_in['gate_b'], 'L0_ffn_w1': _L0_ffn_in['w1'], 'L0_ffn_b1': _L0_ffn_in['b1'], 'L0_ffn_w2': _L0_ffn_in['w2'], 'L0_ffn_b2': _L0_ffn_in['b2'], 'L0_ffn_gamma': _L0_ffn_in['gamma'], 'L0_ffn_beta': _L0_ffn_in['beta'], 'L1_gnn_sc_w0': _L1_gnn_in['sc_w0'], 'L1_gnn_sc_w1': _L1_gnn_in['sc_w1'], 'L1_gnn_lin1_w0': _L1_gnn_in['lin1_w0'], 'L1_gnn_lin1_w1': _L1_gnn_in['lin1_w1'], 'L1_gnn_fc_w1': _L1_gnn_in['fc_w1'], 'L1_gnn_fc_w2': _L1_gnn_in['fc_w2'], 'L1_gnn_lin2_w00': _L1_gnn_in['lin2_w00'], 'L1_gnn_lin2_w01': _L1_gnn_in['lin2_w01'], 'L1_gnn_lin2_w10': _L1_gnn_in['lin2_w10'], 'L1_gnn_lin2_w11': _L1_gnn_in['lin2_w11'], 'L1_ffn_W1': _L1_ffn_in['W1'], 'L1_ffn_b1': _L1_ffn_in['b1'], 'L1_ffn_Wg': _L1_ffn_in['Wg'], 'L1_ffn_bg': _L1_ffn_in['bg'], 'L1_ffn_Wd': _L1_ffn_in['Wd'], 'L1_ffn_bd': _L1_ffn_in['bd']}

def reference(x, src, dst, edge_attr_4, edge_attr_8, node_vec1, L0_gnn_eps, L0_gnn_W1, L0_gnn_b1, L0_gnn_W2, L0_gnn_b2, L0_gnn_gamma, L0_gnn_beta, L0_ffn_gate_w, L0_ffn_gate_b, L0_ffn_w1, L0_ffn_b1, L0_ffn_w2, L0_ffn_b2, L0_ffn_gamma, L0_ffn_beta, L1_gnn_sc_w0, L1_gnn_sc_w1, L1_gnn_lin1_w0, L1_gnn_lin1_w1, L1_gnn_fc_w1, L1_gnn_fc_w2, L1_gnn_lin2_w00, L1_gnn_lin2_w01, L1_gnn_lin2_w10, L1_gnn_lin2_w11, L1_ffn_W1, L1_ffn_b1, L1_ffn_Wg, L1_ffn_bg, L1_ffn_Wd, L1_ffn_bd):
    import jax
    import jax.numpy as jnp

    def _L0_gnn_ref(node_feats, src, dst, eps, W1, b1, W2, b2, gamma, beta):
        import jax, jax.numpy as jnp
        import numpy as np
        N = 3125
        E = 50000
        D = 256
        BN_EPS = 1e-05
        n = node_feats.shape[0]
        neigh = jax.ops.segment_sum(node_feats[src], dst, num_segments=n)
        h = (1.0 + eps) * node_feats + neigh
        h = jax.nn.relu(h @ W1 + b1) @ W2 + b2
        mean = jnp.mean(h, axis=0)
        var = jnp.mean(jnp.square(h - mean), axis=0)
        h = (h - mean) * jax.lax.rsqrt(var + BN_EPS) * gamma + beta
        return h

    def _L0_ffn_ref(x, gate_w, gate_b, w1, b1, w2, b2, gamma, beta):
        import jax, jax.numpy as jnp
        import numpy as np
        B, S, H, F, E, K = (8, 128, 256, 512, 16, 2)
        EPS = 1e-05
        gate_logits = x @ gate_w + gate_b
        topk_vals, topk_idx = jax.lax.top_k(gate_logits, K)
        topk_w = jax.nn.softmax(topk_vals, axis=-1)
        h = jax.nn.relu(jnp.einsum('bsh,ehf->bsef', x, w1) + b1)
        expert_out = jnp.einsum('bsef,efh->bseh', h, w2) + b2
        sel = jnp.take_along_axis(expert_out, topk_idx[:, :, :, None], axis=2)
        moe = jnp.sum(topk_w[..., None] * sel, axis=2)
        y = x + moe
        mu = jnp.mean(y, axis=-1, keepdims=True)
        var = jnp.var(y, axis=-1, keepdims=True)
        return (y - mu) / jnp.sqrt(var + EPS) * gamma + beta

    def _L1_gnn_ref(node_input, node_attr, edge_src, edge_dst, edge_attr, edge_scalars, sc_w0, sc_w1, lin1_w0, lin1_w1, fc_w1, fc_w2, lin2_w00, lin2_w01, lin2_w10, lin2_w11):
        import jax, jax.numpy as jnp
        import numpy as np
        import math
        N = 30000
        E = 18750
        MUL = 64
        NES = 8
        FCN = 64
        NUM_NEIGHBORS = 20.0
        SILU_NORM = 1.679
        INV_SQRT3 = 1.0 / math.sqrt(3.0)

        def _split(x):
            return (x[:, :MUL], x[:, MUL:].reshape(-1, MUL, 3))
        n = node_input.shape[0]
        inv_mul = 1.0 / math.sqrt(MUL)
        x0, x1 = _split(node_input)
        a = node_attr
        s0 = x0 @ sc_w0 * a * inv_mul
        s1 = jnp.einsum('nuc,uv->nvc', x1, sc_w1) * a[:, :, None] * inv_mul
        y0 = x0 @ lin1_w0 * a * inv_mul
        y1 = jnp.einsum('nuc,uv->nvc', x1, lin1_w1) * a[:, :, None] * inv_mul
        h = jax.nn.silu(edge_scalars @ fc_w1 * (1.0 / math.sqrt(NES))) * SILU_NORM
        w = h @ fc_w2 * (1.0 / math.sqrt(FCN))
        w_a, w_b, w_c, w_d = (w[:, :MUL], w[:, MUL:2 * MUL], w[:, 2 * MUL:3 * MUL], w[:, 3 * MUL:])
        xg0 = y0[edge_src]
        xg1 = y1[edge_src]
        ea0 = edge_attr[:, :1]
        ea1 = edge_attr[:, 1:4]
        mid0 = w_a * xg0 * ea0
        mid1 = w_b * jnp.einsum('euc,ec->eu', xg1, ea1) * INV_SQRT3
        mid2 = (w_c * xg0)[:, :, None] * ea1[:, None, :]
        mid3 = (w_d * ea0)[:, :, None] * xg1
        mids = jnp.concatenate([mid0, mid1, mid2.reshape(-1, 3 * MUL), mid3.reshape(-1, 3 * MUL)], axis=1)
        agg = jax.ops.segment_sum(mids, edge_dst, num_segments=n)
        agg = agg * (1.0 / math.sqrt(NUM_NEIGHBORS))
        z0a = agg[:, :MUL]
        z0b = agg[:, MUL:2 * MUL]
        z1a = agg[:, 2 * MUL:5 * MUL].reshape(n, MUL, 3)
        z1b = agg[:, 5 * MUL:].reshape(n, MUL, 3)
        inv2 = 1.0 / math.sqrt(2 * MUL)
        o0 = (z0a @ lin2_w00 + z0b @ lin2_w01) * a * inv2
        o1 = (jnp.einsum('nuc,uv->nvc', z1a, lin2_w10) + jnp.einsum('nuc,uv->nvc', z1b, lin2_w11)) * a[:, :, None] * inv2
        c_s = math.sin(math.pi / 8.0)
        c_x = math.cos(math.pi / 8.0)
        out0 = c_s * s0 + c_x * o0
        out1 = c_s * s1 + c_x * o1
        return jnp.concatenate([out0, out1.reshape(n, 3 * MUL)], axis=1)

    def _L1_ffn_ref(x, W1, b1, Wg, bg, Wd, bd):
        import jax, jax.numpy as jnp
        import numpy as np
        C = 256
        HID = 1024
        E = 8
        TEMP = 1.0
        orig_shape = x.shape
        xf = x.reshape(-1, orig_shape[-1])
        H = jax.nn.gelu(xf @ W1 + b1, approximate=False)
        probs = jax.nn.softmax((H @ Wg + bg) / TEMP, axis=-1)
        assign = jnp.argmax(probs, axis=-1)
        out = jnp.zeros_like(xf)
        for e in range(Wd.shape[0]):
            y = H @ Wd[e] + bd[e]
            sel = (assign == e)[:, None]
            out = out + jnp.where(sel, probs[:, e:e + 1] * y, 0.0)
        return out.reshape(orig_shape)
    x = x + _L0_gnn_ref(_layernorm(x, axis=-1), src, dst, L0_gnn_eps, L0_gnn_W1, L0_gnn_b1, L0_gnn_W2, L0_gnn_b2, L0_gnn_gamma, L0_gnn_beta)
    x = x + _L0_ffn_ref(_layernorm(x, axis=-1)[None], L0_ffn_gate_w, L0_ffn_gate_b, L0_ffn_w1, L0_ffn_b1, L0_ffn_w2, L0_ffn_b2, L0_ffn_gamma, L0_ffn_beta)[0]
    x = x + _L1_gnn_ref(_layernorm(x, axis=-1), node_vec1, src, dst, edge_attr_4, edge_attr_8, L1_gnn_sc_w0, L1_gnn_sc_w1, L1_gnn_lin1_w0, L1_gnn_lin1_w1, L1_gnn_fc_w1, L1_gnn_fc_w2, L1_gnn_lin2_w00, L1_gnn_lin2_w01, L1_gnn_lin2_w10, L1_gnn_lin2_w11)
    x = x + _L1_ffn_ref(_layernorm(x, axis=-1)[None], L1_ffn_W1, L1_ffn_b1, L1_ffn_Wg, L1_ffn_bg, L1_ffn_Wd, L1_ffn_bd)[0]
    return x

_drawn_inputs = setup_inputs


def setup_inputs(seed=0):
    import zlib

    import numpy as np

    out = dict(_drawn_inputs(seed))
    spreads = {'L0_gnn_b1': (0.0, 0.526),
     'L0_gnn_b2': (0.0, 0.8),
     'L0_gnn_gamma': (1.0, 0.2),
     'L0_gnn_beta': (0.0, 0.1),
     'L0_ffn_gate_b': (0.0, 0.275),
     'L0_ffn_b1': (0.0, 0.8),
     'L0_ffn_b2': (0.0, 0.1),
     'L0_ffn_gamma': (1.0, 0.2),
     'L0_ffn_beta': (0.0, 0.1),
     'L1_ffn_b1': (0.0, 0.8),
     'L1_ffn_bg': (0.0, 0.8),
     'L1_ffn_bd': (0.0, 0.8)}
    factors = {'L1_ffn_W1': 6.468, 'L1_ffn_Wg': 6.558, 'L1_ffn_Wd': 7.798}
    for name, (base, spread) in spreads.items():
        noise = np.random.default_rng([zlib.crc32(name.encode()), seed]).standard_normal(out[name].shape)
        drawn = base * np.exp(spread * noise) if base else spread * noise
        out[name] = jnp.asarray(drawn.astype(out[name].dtype))
    for name, factor in factors.items():
        out[name] = (out[name] * factor).astype(out[name].dtype)
    return out
```

```python
from contextlib import ExitStack
import math

import concourse.bass as bass
from concourse import mybir

N, D = 3125, 256
E = 53125
P = 125
T = N // P
G = 5
NG = T // G
W = G * P
CUTS = [(0, 313), (313, W)]

EC = E // P
ER = 25
EG = EC // ER
REC = 16
DST, SRC = 12, 13
EB = 256
NEB = (E + T * (EB - 1)) // EB
SLOTS = 8
NEB = -(-NEB // SLOTS) * SLOTS

TOK = 128
EPS = 1e-5
MAGIC = 12582912.0
VALS = 128 * 6 + 800
OFF = 128 * 6

MUL = 64
INV_MUL = 1.0 / math.sqrt(MUL)
SILU_NORM = 1.679
C_S, C_X = math.sin(math.pi / 8.0), math.cos(math.pi / 8.0)

F32, BF16, I32, U32 = mybir.dt.float32, mybir.dt.bfloat16, mybir.dt.int32, mybir.dt.uint32
ALU, ACT, AX = mybir.AluOpType, mybir.ActivationFunctionType, mybir.AxisListType
ds = bass.ds

GNN_B1, GNN_B2, GNN_GAMMA, GNN_BETA, FFN0_B1, FFN1_B1 = 0, 4, 6, 8, 10, 74
VEC_ROWS = 82


class Kept:
    pass


class Phase:

    spent = []

    def __init__(self, nc, name):
        self.nc, self.name, self.ctx, self.taken = nc, name, ExitStack(), []

    def __enter__(self):
        self.ctx.__enter__()
        return self

    def __exit__(self, *what):
        self.ctx.__exit__(*what)
        self.spent += self.taken
        if what[0] is None and len(self.spent) > 70:
            self.nc.clear_and_free_semaphores(list(self.spent))
            self.nc.all_engine_barrier()
            self.spent.clear()

    def sb(self, name, shape, dt=F32):
        return self.ctx.enter_context(self.nc.sbuf_tensor(f"{self.name}_{name}", shape, dt))

    def ps(self, name, shape, dt=F32):
        return self.ctx.enter_context(self.nc.psum_tensor(f"{self.name}_ps_{name}", shape, dt))

    def sem(self, name):
        self.taken.append(self.nc.alloc_semaphore(f"{self.name}_{name}"))
        return self.taken[-1]

    def sems(self, name, n):
        return [self.sem(f"{name}{j}") for j in range(n)]


def load_inputs(nc, k):
    with Phase(nc, "load") as ph:
        rows = ph.sb("rows", [VEC_ROWS, 128])
        one_row = ph.sb("one_row", [1, 128])
        ps_cols = ph.ps("cols", [128, 128])
        loaded, zeroed, made = ph.sem("loaded"), ph.sem("zeroed"), ph.sem("made")
        cols_ready, copied = ph.sem("cols_ready"), ph.sem("copied")
        block = ph.ctx.enter_context(nc.Block())
        count = 0

        @block.sync
        def _(sp):
            nonlocal count

            def load(dst, src):
                nonlocal count
                sp.dma_start(dst, src).then_inc(loaded, 16)
                count += 16

            def vec(row, a):
                n = a.shape[-1] // 128 if len(a.shape) == 1 else a.shape[0] * a.shape[1] // 128
                src = a.rearrange("(r c) -> r c", c=128) if len(a.shape) == 1 else a.rearrange("e (r c) -> (e r) c", c=128)
                load(rows[row:row + n, :], src)

            vec(GNN_B1, k.L0_gnn_b1)
            vec(GNN_B2, k.L0_gnn_b2)
            vec(GNN_GAMMA, k.L0_gnn_gamma)
            vec(GNN_BETA, k.L0_gnn_beta)
            vec(FFN0_B1, k.L0_ffn_b1)
            vec(FFN1_B1, k.L1_ffn_b1)
            load(k.x_sb[0:P, :, :], k.x.rearrange("(t p) d -> p t d", p=P))
            load(k.gate_b[:, :], k.L0_ffn_gate_b.partition_broadcast(128))
            load(k.bg[:, :], k.L1_ffn_bg.partition_broadcast(128))
            load(k.gamma[:, :], k.L0_ffn_gamma.partition_broadcast(128))
            load(k.beta[:, :], k.L0_ffn_beta.partition_broadcast(128))
            load(k.eps[:, :], k.L0_gnn_eps.partition_broadcast(128))
            with nc.allow_non_contiguous_dma(reason="3125 single words, once"):
                load(k.node_a[0:P, :], k.node_vec1.rearrange("(t p) o -> p (t o)", p=P))
            sp.wait_ge(loaded, count)

        @block.gpsimd
        def _(pool):
            pool.memset(k.ident[:, :], 0.0).then_inc(zeroed, 1)
            pool.memset(k.below[:, :], 1.0).then_inc(zeroed, 1)
            pool.memset(k.tri[:, :], 1.0).then_inc(zeroed, 1)
            pool.memset(k.ones[:, :], 1.0).then_inc(made, 1)
            pool.memset(k.onesf[:, :], 1.0).then_inc(made, 1)
            pool.iota(k.iota_i[:, :], pattern=[[1, 256]], base=0, channel_multiplier=0).then_inc(made, 1)
            pool.wait_ge(zeroed, 3)
            pool.affine_select(out=k.ident[:, :], in_=k.ident[:, :], compare_op=ALU.not_equal, fill=1.0, base=0,
                               pattern=[[-1, 128]], channel_multiplier=1).then_inc(made, 1)
            pool.affine_select(out=k.below[:, :], in_=k.below[:, :], compare_op=ALU.is_gt, fill=0.0, base=-OFF,
                               pattern=[[1, VALS]], channel_multiplier=-1).then_inc(made, 1)
            pool.affine_select(out=k.tri[:, :], in_=k.tri[:, :], compare_op=ALU.is_gt, fill=0.0, base=0,
                               pattern=[[1, 128]], channel_multiplier=-1).then_inc(made, 1)

        @block.tensor
        def _(pe):
            pe.wait_ge(loaded, count)
            pe.wait_ge(made, 6)
            pe.transpose(ps_cols[:, 0:VEC_ROWS], rows[:, :], k.ident[0:VEC_ROWS, 0:VEC_ROWS]).then_inc(cols_ready, 1)

        @block.vector
        def _(dve):
            dve.wait_ge(cols_ready, 1)
            dve.tensor_copy(k.cols[:, :], ps_cols[:, 0:VEC_ROWS]).then_inc(copied, 1)
            dve.wait_ge(made, 6)
            dve.tensor_copy(k.iota[:, :], k.iota_i[:, :]).then_inc(copied, 1)
            dve.wait_ge(loaded, count)
            dve.tensor_scalar(k.eps[:, :], k.eps[:, :], 1.0, None, ALU.add).then_inc(copied, 1)


def pass_on(eng, gate):
    eng.sem_inc(gate, 1)


class LayerNorm:

    def __init__(self, ph):
        self.stats, self.mv = ph.sb("ln_stats", [128, G, 6]), ph.sb("ln_mv", [128, G, 2])
        self.std, self.rstd = ph.sb("ln_std", [128, G]), ph.sb("ln_rstd", [128, G])
        self.stats_done, self.mv_done = ph.sem("ln_stats_done"), ph.sem("ln_mv_done")
        self.std_done, self.rstd_done = ph.sem("ln_std_done"), ph.sem("ln_rstd_done")
        self.out_done, self.gate = ph.sem("ln_out_done"), ph.sem("ln_gate")


def ln_vector(dve, ln, i, source, target):
    for j in range(G):
        dve.bn_stats(ln.stats[0:P, j, :], source(j)).then_inc(ln.stats_done, 1)
    dve.wait_ge(ln.stats_done, i * G + G)
    pass_on(dve, ln.gate)
    for j in range(G):
        dve.bn_aggr(ln.mv[0:P, j, :], ln.stats[0:P, j, :]).then_inc(ln.mv_done, 1)
    dve.wait_ge(ln.std_done, i + 1)
    dve.wait_ge(ln.mv_done, i * G + G)
    dve.reciprocal(ln.rstd[0:P, :], ln.std[0:P, :]).then_inc(ln.rstd_done, 1)
    dve.wait_ge(ln.rstd_done, i + 1)
    for j in range(G):
        dve.tensor_scalar(target(j), source(j), ln.mv[0:P, j, 0:1], ln.rstd[0:P, j:j + 1],
                          ALU.subtract, ALU.mult).then_inc(ln.out_done, 1)


def ln_scalar(act, k, ln, i):
    act.wait_ge(ln.mv_done, i * G + G)
    act.activation(ln.std[0:P, :], ln.mv[0:P, :, 1], ACT.Sqrt, bias=k.eps5[0:P, 0:1]).then_inc(ln.std_done, 1)


def first_norm(nc, k):
    with Phase(nc, "norm0") as ph:
        ln = LayerNorm(ph)
        stored, eps_made = ph.sem("stored"), ph.sem("eps_made")
        block = ph.ctx.enter_context(nc.Block())

        @block.vector
        def _(dve):
            dve.memset(k.eps5[:, :], EPS).then_inc(eps_made, 1)
            with dve.Fori(0, NG) as i:
                ln_vector(dve, ln, i, lambda j: k.x_sb[0:P, ds(i * G + j, 1), :].rearrange("p o d -> p (o d)"),
                          lambda j: k.xn_sb[0:P, ds(i * G + j, 1), :].rearrange("p o d -> p (o d)"))

        @block.scalar
        def _(act):
            act.wait_ge(eps_made, 1)
            with act.Fori(0, NG) as i:
                ln_scalar(act, k, ln, i)

        @block.sync
        def _(sp):
            sp.wait_ge(ln.out_done, T)
            sp.dma_start(k.xn_dram.rearrange("(t p) d -> p t d", p=P), k.xn_sb[0:P, :, :]).then_inc(stored, 16)
            sp.wait_ge(stored, 16)


def sort_edges(nc, k):
    with ExitStack() as held:
        def sb(name, shape, dt=F32):
            return held.enter_context(nc.sbuf_tensor(f"edges_{name}", shape, dt))

        e = Kept()
        e.rec = sb("rec", [128, EC, REC])
        e.onehot = sb("onehot", [128, ER, T, EG], BF16)
        e.cum = sb("cum", [128, ER + 1, T * EG], BF16)
        e.base = sb("base", [128, T * EG])
        e.unsorted = sb("unsorted", [128, 1], I32)
        count_edges(nc, k, e)
        place_edges(nc, k, e)


def count_edges(nc, k, e):
    BG = T * EG
    chunks = [(c, min(128, BG - c)) for c in range(0, BG, 128)]
    with Phase(nc, "count") as ph:
        dst_i, next_i, src_i = ph.sb("dst_i", [128, EC], I32), ph.sb("next_i", [128, EC], I32), ph.sb("src_i", [128, EC], I32)
        ea4, ea8 = ph.sb("ea4", [128, EC, 4]), ph.sb("ea8", [128, EC, 8])
        dst_f, next_f = ph.sb("dst_f", [128, EC]), ph.sb("next_f", [128, EC])
        tile_y, tile_f = ph.sb("tile_y", [128, EC]), ph.sb("tile_f", [128, EC])
        falls = ph.sb("falls", [128, 1])
        totals = ph.sb("totals", [128, len(chunks)])
        totals_b = ph.sb("totals_b", [128, len(chunks), 128])
        ps_tot = ph.ps("tot", [128, len(chunks)])
        ps_base = ph.ps("base", [128, BG])
        ps_falls = ph.ps("falls", [128, 1])

        dst_in, next_in, other_in = ph.sem("dst_in"), ph.sem("next_in"), ph.sem("other_in")
        step = ph.sem("step")
        next_set, falls_made, falls_sum = ph.sem("next_set"), ph.sem("falls_made"), ph.sem("falls_sum")
        cum_ready, tot_ready, totb_ready, base_ready = (ph.sem(f"{x}_ready") for x in ("cum", "tot", "totb", "base"))
        fields = ph.sem("fields")
        block = ph.ctx.enter_context(nc.Block())

        @block.sync
        def _(sp):
            sp.dma_start(dst_i[0:P, :], k.dst.rearrange("(p c) -> p c", p=P)).then_inc(dst_in, 16)
            sp.wait_ge(next_set, 1)
            last = (P - 1) * EC
            sp.dma_start(next_i[0:P - 1, :], k.dst[1:last + 1].rearrange("(p c) -> p c", c=EC)).then_inc(next_in, 16)
            sp.dma_start(next_i[P - 1:P, 0:EC - 1], k.dst[last + 1:E].rearrange("(p c) -> p c", p=1)).then_inc(next_in, 16)

        @block.scalar
        def _(act):
            act.dma_start(src_i[0:P, :], k.src.rearrange("(p c) -> p c", p=P)).then_inc(other_in, 16)
            act.dma_start(ea4[0:P, :, :], k.edge_attr_4.rearrange("(p c) w -> p c w", p=P)).then_inc(other_in, 16)
            act.dma_start(ea8[0:P, :, :], k.edge_attr_8.rearrange("(p c) w -> p c w", p=P)).then_inc(other_in, 16)
            act.wait_ge(other_in, 48)
            act.activation(e.rec[0:P, :, 0:8], ea8[0:P, :, :], ACT.Copy).then_inc(fields, 1)
            act.activation(e.rec[0:P, :, 8:12], ea4[0:P, :, :], ACT.Copy).then_inc(fields, 1)

        @block.gpsimd
        def _(pool):
            pool.memset(next_i[:, :], N).then_inc(next_set, 1)
            pool.memset(e.rec[0:P, :, SRC + 1:REC], 0.0).then_inc(fields, 1)

        @block.tensor
        def _(pe):
            pe.wait_ge(falls_made, 1)
            pe.matmul(ps_falls[:, :], k.onesf[0:P, :], falls[0:P, :], start=True, stop=True).then_inc(falls_sum, 1)
            pe.wait_ge(cum_ready, 1)
            for c, (at, n) in enumerate(chunks):
                last = pe.matmul(ps_tot[0:n, c:c + 1], e.cum[0:P, ER, at:at + n], k.ones[0:P, 0:1], start=True, stop=True)
            last.then_inc(tot_ready, 1)
            pe.wait_ge(totb_ready, len(chunks))
            for c, (at, n) in enumerate(chunks):
                last = pe.matmul(ps_base[:, :], totals_b[0:n, c, :], k.below[0:n, OFF - at:OFF - at + BG],
                                 start=(c == 0), stop=(c == len(chunks) - 1))
            last.then_inc(base_ready, 1)

        @block.vector
        def _(dve):
            done = [0]

            def chain(ins):
                done[0] += 1
                ins.then_inc(step, 1)
                dve.wait_ge(step, done[0])

            dve.wait_ge(dst_in, 16)
            chain(dve.tensor_copy(dst_f[0:P, :], dst_i[0:P, :]))
            chain(dve.tensor_scalar(tile_y[0:P, :], dst_f[0:P, :], 1.0 / P, 0.5 / P - 0.5, ALU.mult, ALU.add))
            chain(dve.tensor_scalar(tile_f[0:P, :], tile_y[0:P, :], MAGIC, None, ALU.add))
            chain(dve.tensor_scalar(tile_f[0:P, :], tile_f[0:P, :], MAGIC, None, ALU.subtract))
            view = tile_f[0:P, :].rearrange("p (g r) -> p r g", r=ER)
            chain(dve.memset(e.cum[0:P, 0, :], 0.0))
            for r in range(ER):
                dve.tensor_tensor(e.onehot[0:P, r, :, :], view[:, r, :].unsqueeze(1).to_broadcast([P, T, EG]),
                                  k.iota[0:P, 0:T].unsqueeze(2).to_broadcast([P, T, EG]), ALU.is_equal).then_inc(step, 1)
            done[0] += ER
            dve.wait_ge(next_in, 32)
            chain(dve.tensor_copy(next_f[0:P, :], next_i[0:P, :]))
            chain(dve.tensor_tensor(next_f[0:P, :], dst_f[0:P, :], next_f[0:P, :], ALU.is_gt))
            dve.tensor_reduce(falls[0:P, :], next_f[0:P, :], AX.X, ALU.add).then_inc(falls_made, 1)
            for r in range(ER):
                chain(dve.tensor_tensor(e.cum[0:P, r + 1, :], e.cum[0:P, r, :],
                                        e.onehot[0:P, r, :, :].rearrange("p t g -> p (t g)"), ALU.add))
            dve.sem_inc(cum_ready, 1)
            dve.wait_ge(falls_sum, 1)
            dve.tensor_copy(e.unsorted[:, :], ps_falls[:, :])
            dve.wait_ge(tot_ready, 1)
            for c, (at, n) in enumerate(chunks):
                chain(dve.tensor_copy(totals[0:n, c:c + 1], ps_tot[0:n, c:c + 1]))
                dve.tensor_copy(totals_b[0:n, c, :], totals[0:n, c:c + 1].to_broadcast([n, 128])).then_inc(totb_ready, 1)
            dve.tensor_copy(e.rec[0:P, :, DST], dst_f[0:P, :]).then_inc(fields, 1)
            dve.wait_ge(other_in, 48)
            dve.tensor_copy(e.rec[0:P, :, SRC].bitcast(I32), src_i[0:P, :]).then_inc(fields, 1)
            dve.wait_ge(base_ready, 1)
            dve.tensor_copy(e.base[:, :], ps_base[:, :])


def place_edges(nc, k, e):
    BG = T * EG
    with Phase(nc, "place") as ph:
        tail = ph.sb("tail", [128, 2 * REC])
        sel = ph.sb("sel", [128, 2, BG])
        pos_f, pos_i = ph.sb("pos_f", [128, EG, ER]), ph.sb("pos_i", [128, EC], I32)
        row_st, idx_st = ph.sb("row_st", [128, G, REC]), ph.sb("idx_st", [128, G], I32)
        start_b, count_b = ph.sb("start_b", [128, T + 1]), ph.sb("count_b", [128, T])
        blk_y, blk_n = ph.sb("blk_y", [128, T]), ph.sb("blk_n", [128, T])
        blk_end = ph.sb("blk_end", [128, 2, T])
        shift, dshift = ph.sb("shift", [128, T]), ph.sb("dshift", [128, T])
        cmp = ph.sb("cmp", [128, NEB, T])
        blk_f, blk_s, blk_t = ph.sb("blk_f", [128, NEB]), ph.sb("blk_s", [128, NEB]), ph.sb("blk_t", [128, NEB])
        blk_c = ph.sb("blk_c", [128, NEB])
        ps_rank = [ph.ps(f"rank{s}", [128, BG]) for s in range(2)]
        step, rank_step = ph.sem("step"), ph.sem("rank_step")
        rank_ready, rank_read, staged = ph.sem("rank_ready"), ph.sem("rank_read"), ph.sem("staged")
        scattered = ph.sems("scattered", G)
        tail_made, stored, tail_stored, gate = ph.sem("tail_made"), ph.sem("stored"), ph.sem("tail_stored"), ph.sem("gate")
        block = ph.ctx.enter_context(nc.Block())

        @block.sync
        def _(sp):
            unsorted = sp.value_load(e.unsorted[0:1, 0:1], min_val=0, max_val=E)
            with sp.If(unsorted == 0):
                sp.dma_start(k.recs[0:E, :].rearrange("(p c) w -> p c w", p=P), e.rec[0:P, :, :]).then_inc(stored, 16)
                sp.wait_ge(stored, 16)
            sp.wait_ge(tail_made, 2)
            sp.dma_start(k.recs[E:E + EB, :].rearrange("(p u) w -> p (u w)", u=2), tail[:, :]).then_inc(tail_stored, 16)
            sp.wait_ge(tail_stored, 16)

        @block.tensor
        def _(pe):
            unsorted = pe.value_load(e.unsorted[0:1, 0:1], min_val=0, max_val=E)
            with pe.If(unsorted != 0):
                for r in range(ER):
                    if r >= 2:
                        pe.wait_ge(rank_read, r - 1)
                    pe.matmul(ps_rank[r % 2][0:P, :], k.onesf[0:1, 0:P], e.base[0:1, :], start=True, stop=False)
                    pe.matmul(ps_rank[r % 2][0:P, :], k.tri[0:P, 0:P], e.onehot[0:P, r, :, :].rearrange("p t g -> p (t g)"),
                              start=False, stop=False)
                    pe.matmul(ps_rank[r % 2][0:P, :], k.ones[0:P, 0:P], e.cum[0:P, r, :], start=False,
                              stop=True).then_inc(rank_ready, 1)

        @block.gpsimd
        def _(pool):
            pool.memset(tail[:, :], 0.0).then_inc(tail_made, 1)
            pool.wait_ge(tail_made, 1)
            pool.memset(tail[:, :].rearrange("p (u w) -> p u w", w=REC)[:, :, DST], -1.0).then_inc(tail_made, 1)
            unsorted = pool.value_load(e.unsorted[0:1, 0:1], min_val=0, max_val=E)
            with pool.If(unsorted != 0):
                with pool.Fori(0, EC // G) as i:
                    for j in range(G):
                        pool.wait_ge(staged, i * 2 * G + 2 * j + 2)
                        pass_on(pool, gate)
                        pool.indirect_dma_start(k.recs, bass.IndirectOffsetOnAxis(ap=idx_st[0:P, j:j + 1].bitcast(U32), axis=0),
                                                row_st[0:P, j, :], None).then_inc(scattered[j], 16)
                for j in range(G):
                    pool.wait_ge(scattered[j], (EC // G) * 16)

        @block.vector
        def _(dve):
            unsorted = dve.value_load(e.unsorted[0:1, 0:1], min_val=0, max_val=E)
            with dve.If(unsorted != 0):
                for r in range(ER):
                    dve.wait_ge(rank_ready, r + 1)
                    s = sel[0:P, r % 2, :]
                    dve.tensor_tensor(s, ps_rank[r % 2][0:P, :], e.onehot[0:P, r, :, :].rearrange("p t g -> p (t g)"), ALU.mult)\
                       .then_inc(rank_read, 1)
                    dve.wait_ge(rank_read, r + 1)
                    dve.tensor_reduce(pos_f[0:P, :, r], s.rearrange("p (t g) -> p g t", g=EG), AX.X, ALU.add).then_inc(rank_step, 1)
                dve.wait_ge(rank_step, ER)
                dve.tensor_copy(pos_i[0:P, :], pos_f[0:P, :, :].rearrange("p g r -> p (g r)")).then_inc(rank_step, 1)
                dve.wait_ge(rank_step, ER + 1)

                def stage(i, first=False):
                    for j in range(G):
                        if not first:
                            dve.wait_ge(scattered[j], i * 16)
                            pass_on(dve, gate)
                        dve.tensor_copy(row_st[0:P, j, :], row(e.rec, i * G + j)).then_inc(staged, 1)
                        dve.tensor_copy(idx_st[0:P, j:j + 1], pos_i[0:P, ds(i * G + j, 1)]).then_inc(staged, 1)

                stage(0, first=True)
                with dve.Fori(1, EC // G) as i:
                    stage(i)

            done = [0]

            def chain(ins):
                done[0] += 1
                ins.then_inc(step, 1)
                dve.wait_ge(step, done[0])

            first = e.base[:, :].rearrange("p (t g) -> p t g", g=EG)[:, :, 0]
            chain(dve.tensor_copy(start_b[:, 0:T], first))
            chain(dve.memset(start_b[:, T:T + 1], float(E)))
            chain(dve.tensor_tensor(count_b[:, :], start_b[:, 1:T + 1], start_b[:, 0:T], ALU.subtract))
            chain(dve.tensor_scalar(blk_y[:, :], count_b[:, :], 1.0 / EB, (EB - 1) / EB - 0.5 + 0.5 / EB, ALU.mult, ALU.add))
            chain(dve.tensor_scalar(blk_y[:, :], blk_y[:, :], MAGIC, None, ALU.add))
            chain(dve.tensor_scalar(blk_n[:, :], blk_y[:, :], MAGIC, None, ALU.subtract))
            chain(dve.tensor_copy(blk_end[:, 0, :], blk_n[:, :]))
            side, gap = 0, 1
            while gap < T:
                chain(dve.tensor_copy(blk_end[:, 1 - side, 0:gap], blk_end[:, side, 0:gap]))
                chain(dve.tensor_tensor(blk_end[:, 1 - side, gap:T], blk_end[:, side, gap:T], blk_end[:, side, 0:T - gap], ALU.add))
                side, gap = 1 - side, 2 * gap
            end = blk_end[:, side, :]
            chain(dve.tensor_tensor(shift[:, :], end, blk_n[:, :], ALU.subtract))
            chain(dve.scalar_tensor_tensor(shift[:, :], shift[:, :], float(-EB), start_b[:, 0:T], ALU.mult, ALU.add))
            chain(dve.memset(dshift[:, :], 0.0))
            chain(dve.tensor_tensor(dshift[:, 0:T - 1], shift[:, 1:T], shift[:, 0:T - 1], ALU.subtract))
            chain(dve.tensor_tensor(cmp[:, :, :], k.iota[:, 0:NEB].unsqueeze(2).to_broadcast([128, NEB, T]),
                                    end.unsqueeze(1).to_broadcast([128, NEB, T]), ALU.is_ge))
            chain(dve.tensor_reduce(blk_f[:, :], cmp[:, :, :], AX.X, ALU.add))
            chain(dve.tensor_tensor(cmp[:, :, :], cmp[:, :, :], dshift[:, :].unsqueeze(1).to_broadcast([128, NEB, T]), ALU.mult))
            chain(dve.tensor_reduce(blk_s[:, :], cmp[:, :, :], AX.X, ALU.add))
            chain(dve.scalar_tensor_tensor(blk_t[:, :], k.iota[:, 0:NEB], float(EB), blk_s[:, :], ALU.mult, ALU.add))
            chain(dve.tensor_scalar(blk_t[:, :], blk_t[:, :], float(E), None, ALU.min))
            chain(dve.tensor_copy(k.block_start[:, :], blk_t[:, :]))
            chain(dve.tensor_scalar(blk_c[:, :], blk_f[:, :], float(T - 1), None, ALU.min))
            chain(dve.tensor_copy(k.block_tile[:, :], blk_c[:, :]))
            chain(dve.tensor_scalar(k.block_node[:, :], blk_c[:, :], float(P), None, ALU.mult))


def row(buf, at, lo=0, hi=None, parts=P):
    return buf[0:parts, ds(at, 1), lo:hi].rearrange("p o d -> p (o d)")


def sum_neighbours(nc, k):
    with Phase(nc, "sum") as ph:
        rec = [ph.sb(f"rec{s}", [128, 2, REC]) for s in range(SLOTS)]
        got = [[ph.sb(f"got{s}{u}", [128, D]) for u in range(2)] for s in range(SLOTS)]
        onehot = [ph.sb(f"onehot{s}", [128, 2, P]) for s in range(SLOTS)]
        ps_sum = [ph.ps(f"sum{s}", [128, D]) for s in range(SLOTS)]
        rec_in, got_in = ph.sems("rec_in", SLOTS), ph.sems("got_in", SLOTS)
        summed, added = ph.sem("summed"), ph.sem("added")
        masked, gate = ph.sem("masked"), ph.sem("gate")
        block = ph.ctx.enter_context(nc.Block())

        @block.sync
        def _(sp):
            sp.sem_inc(summed, SLOTS)
            with sp.Fori(0, NEB // SLOTS) as i:
                for s in range(SLOTS):
                    n = i * SLOTS + s
                    start = sp.value_load(k.block_start[0:1, ds(n, 1)], min_val=0, max_val=E)
                    sp.wait_ge(summed, n + 1)
                    pass_on(sp, gate)
                    sp.dma_start(rec[s][:, :, :], k.recs[ds(start, EB), :].rearrange("(p u) w -> p u w", u=2))\
                      .then_inc(rec_in[s], 16)

        @block.gpsimd
        def _(pool):
            with pool.Fori(0, NEB // SLOTS) as i:
                for s in range(SLOTS):
                    pool.wait_ge(rec_in[s], i * 16 + 16)
                    pass_on(pool, gate)
                    for u in range(2):
                        pool.indirect_dma_start(
                            got[s][u][:, :], None, k.xn_dram,
                            bass.IndirectOffsetOnAxis(ap=rec[s][:, u, SRC:SRC + 1].bitcast(U32), axis=0)).then_inc(got_in[s], 16)

        @block.tensor
        def _(pe):
            with pe.Fori(0, NEB // SLOTS) as i:
                for s in range(SLOTS):
                    n = i * SLOTS + s
                    pe.wait_ge(added, n + 1)
                    pe.wait_ge(masked, n * 2 + 2)
                    pe.wait_ge(got_in[s], i * 32 + 32)
                    for u in range(2):
                        last = pe.matmul(ps_sum[s][0:P, :], onehot[s][:, u, :], got[s][u][:, :], start=(u == 0), stop=(u == 1))
                    last.then_inc(summed, 1)

        @block.vector
        def _(dve):
            dve.memset(k.agg[:, :, 0:D], 0.0).then_inc(added, SLOTS)

            def add_sum(n, s):
                tile = dve.value_load(k.block_tile[0:1, ds(n, 1)], min_val=0, max_val=T - 1)
                dve.wait_ge(summed, n + 1 + SLOTS)
                dve.wait_ge(added, n + SLOTS)
                dve.tensor_tensor(row(k.agg, tile, 0, D), ps_sum[s][0:P, :], row(k.agg, tile, 0, D), ALU.add)\
                   .then_inc(added, 1)

            def turn(i, first=False):
                for s in range(SLOTS):
                    n = i * SLOTS + s
                    dve.wait_ge(rec_in[s], i * 16 + 16)
                    for u in range(2):
                        dve.tensor_scalar(onehot[s][:, u, :], k.iota[:, 0:P], k.block_node[:, ds(n, 1)],
                                          rec[s][:, u, DST:DST + 1], ALU.add, ALU.is_equal).then_inc(masked, 1)
                    if not first or s >= 1:
                        add_sum(n - 1, (s - 1) % SLOTS)

            turn(0, first=True)
            with dve.Fori(1, NEB // SLOTS) as i:
                turn(i)
            add_sum(NEB - 1, SLOTS - 1)


def gin_mlp(nc, k):
    HID = 512
    HC = HID // 128
    with Phase(nc, "gin") as ph:
        w1, w2 = ph.sb("w1", [128, 2, HID]), ph.sb("w2", [128, HC, D])
        h = ph.sb("h", [128, G, D])
        h_t = ph.sb("h_t", [128, 2, W])
        hid = ph.sb("hid", [128, HC, W])
        h2 = ph.sb("h2", [128, 2, NG, W])
        stats = ph.sb("stats", [128, 2, 2 * NG, 6])
        mv, std, rstd = ph.sb("mv", [128, 2, 2]), ph.sb("std", [128, 2]), ph.sb("rstd", [128, 2])
        scale, shift = ph.sb("scale", [128, 2]), ph.sb("shift", [128, 2])
        bn = ph.sb("bn", [128, 2, W])
        ps_t = [ph.ps(f"t{s}", [128, 2, 128]) for s in range(2)]
        ps_h = [ph.ps(f"h{s}", [128, 512]) for s in range(4)]
        w_in = ph.sem("w_in")
        h_made, turned, kept = ph.sem("h_made"), ph.sem("turned"), ph.sem("kept")
        hid_sum, hid_made, out_sum, out_made = ph.sem("hid_sum"), ph.sem("hid_made"), ph.sem("out_sum"), ph.sem("out_made")
        step, bn_std = ph.sem("step"), ph.sem("bn_std")
        bn_made, bn_turned, x_made, gate = ph.sem("bn_made"), ph.sem("bn_turned"), ph.sem("x_made"), ph.sem("gate")
        block = ph.ctx.enter_context(nc.Block())

        @block.sync
        def _(sp):
            sp.dma_start(w1[:, :, :], k.L0_gnn_W1.rearrange("(c p) h -> p c h", p=128)).then_inc(w_in, 16)
            sp.dma_start(w2[:, :, :], k.L0_gnn_W2.rearrange("(c p) h -> p c h", p=128)).then_inc(w_in, 16)

        @block.vector
        def _(dve):
            dve.sem_inc(turned, G)
            with dve.Fori(0, NG) as i:
                for j in range(G):
                    dve.wait_ge(turned, i * G + j + 1)
                    pass_on(dve, gate)
                    dve.scalar_tensor_tensor(h[0:P, j, :], row(k.xn_sb, i * G + j), k.eps[0:P, 0:1], row(k.agg, i * G + j, 0, D),
                                             ALU.mult, ALU.add).then_inc(h_made, 1)
                for c, (a, b) in enumerate(CUTS):
                    for m in range(2):
                        dve.wait_ge(out_made, i * 4 + 2 * c + m + 1)
                        pass_on(dve, gate)
                        dve.bn_stats(stats[:, m, ds(i * 2 + c, 1), :].rearrange("p o w -> p (o w)"),
                                     h2[:, m, ds(i, 1), a:b].rearrange("p o w -> p (o w)")).then_inc(step, 1)
            done = [4 * NG]

            def chain(ins):
                done[0] += 1
                ins.then_inc(step, 1)
                dve.wait_ge(step, done[0])

            dve.wait_ge(step, done[0])
            for m in range(2):
                chain(dve.bn_aggr(mv[:, m, :], stats[:, m, :, :].rearrange("p n w -> p (n w)")))
            dve.wait_ge(bn_std, 1)
            chain(dve.reciprocal(rstd[:, :], std[:, :]))
            chain(dve.tensor_tensor(scale[:, :], rstd[:, :], k.cols[:, GNN_GAMMA:GNN_GAMMA + 2], ALU.mult))
            chain(dve.tensor_tensor(shift[:, :], mv[:, :, 0], scale[:, :], ALU.mult))
            chain(dve.tensor_tensor(shift[:, :], k.cols[:, GNN_BETA:GNN_BETA + 2], shift[:, :], ALU.subtract))
            with dve.Fori(0, NG) as i:
                for m in range(2):
                    dve.wait_ge(bn_turned, i * G + 1)
                    pass_on(dve, gate)
                    dve.tensor_scalar(bn[:, m, :], h2[:, m, ds(i, 1), :].rearrange("p o w -> p (o w)"), scale[:, m:m + 1],
                                      shift[:, m:m + 1], ALU.mult, ALU.add).then_inc(bn_made, 1)
                for j in range(G):
                    dve.wait_ge(bn_turned, i * G + j + 2)
                    pass_on(dve, gate)
                    dve.tensor_tensor(row(k.x_sb, i * G + j), ps_t[j % 2][0:P, :, :].rearrange("p m w -> p (m w)"),
                                      row(k.x_sb, i * G + j), ALU.add).then_inc(x_made, 1)

        @block.scalar
        def _(act):
            with act.Fori(0, NG) as i:
                for j in range(G):
                    act.wait_ge(turned, i * G + j + 1 + G)
                    act.wait_ge(hid_sum, i * 2 * HC + 1)
                    pass_on(act, gate)
                    act.activation(h_t[:, :, j * P:(j + 1) * P], ps_t[j % 2][:, :, 0:P], ACT.Copy).then_inc(kept, 1)
                for c, (a, b) in enumerate(CUTS):
                    for m in range(HC):
                        act.wait_ge(hid_sum, i * 2 * HC + c * HC + m + 2)
                        act.wait_ge(out_sum, i * 4 + 1)
                        pass_on(act, gate)
                        act.activation(hid[:, m, a:b], ps_h[(c * HC + m) % 4][:, 0:b - a], ACT.Relu,
                                       bias=k.cols[:, GNN_B1 + m:GNN_B1 + m + 1]).then_inc(hid_made, 1)
                for c, (a, b) in enumerate(CUTS):
                    for m in range(2):
                        act.wait_ge(out_sum, i * 4 + 2 * c + m + 2)
                        pass_on(act, gate)
                        act.activation(h2[:, m, ds(i, 1), a:b].rearrange("p o w -> p (o w)"), ps_h[2 * c + m][:, 0:b - a],
                                       ACT.Identity, bias=k.cols[:, GNN_B2 + m:GNN_B2 + m + 1]).then_inc(out_made, 1)
            act.wait_ge(step, 4 * NG + 2)
            act.activation(std[:, :], mv[:, :, 1], ACT.Sqrt, bias=k.eps5[:, 0:1]).then_inc(bn_std, 1)

        @block.tensor
        def _(pe):
            pe.wait_ge(w_in, 32)
            pe.sem_inc(hid_sum, 1)
            pe.sem_inc(out_sum, 1)
            pe.sem_inc(bn_turned, 1)
            pe.sem_inc(kept, 2)
            pe.sem_inc(x_made, 2)
            with pe.Fori(0, NG) as i:
                for j in range(G):
                    pe.wait_ge(h_made, i * G + j + 1)
                    pe.wait_ge(kept, i * G + j + 1)
                    for m in range(2):
                        last = pe.transpose(ps_t[j % 2][:, m, 0:P], h[0:P, j, m * 128:(m + 1) * 128], k.ident[0:P, 0:P])
                    last.then_inc(turned, 1)
                pe.wait_ge(kept, i * G + G + 2)
                for c, (a, b) in enumerate(CUTS):
                    for m in range(HC):
                        n = c * HC + m
                        if c:
                            pe.wait_ge(hid_made, i * 2 * HC + n - 3)
                        for q in range(2):
                            last = pe.matmul(ps_h[n % 4][:, 0:b - a], w1[:, q, m * 128:(m + 1) * 128], h_t[:, q, a:b],
                                             start=(q == 0), stop=(q == 1))
                        last.then_inc(hid_sum, 1)
                for c, (a, b) in enumerate(CUTS):
                    for m in range(2):
                        pe.wait_ge(hid_made, i * 2 * HC + 2 * HC)
                        for q in range(HC):
                            last = pe.matmul(ps_h[2 * c + m][:, 0:b - a], w2[:, q, m * 128:(m + 1) * 128], hid[:, q, a:b],
                                             start=(q == 0), stop=(q == HC - 1))
                        last.then_inc(out_sum, 1)
                pe.wait_ge(out_made, i * 4 + 4)
            with pe.Fori(0, NG) as i:
                pe.wait_ge(bn_made, i * 2 + 2)
                for j in range(G):
                    pe.wait_ge(x_made, i * G + j + 1)
                    for m in range(2):
                        last = pe.transpose(ps_t[j % 2][0:P, m, :], bn[:, m, j * P:(j + 1) * P], k.ident[:, :])
                    last.then_inc(bn_turned, 1)


class Experts:

    def __init__(self, nc, ctx, name, n, picks, hid, own_w1):
        self.name, self.n, self.picks, self.hid, self.own_w1 = name, n, picks, hid, own_w1
        self.cols = T * picks
        self.blocks = (N * picks + n * (TOK - 1)) // TOK
        self.blocks += self.blocks % 2

        def sb(what, shape, dt=F32):
            return ctx.enter_context(nc.sbuf_tensor(f"{name}_{what}", shape, dt))

        self.onehot = sb("onehot", [128, n, self.cols], BF16)
        self.prob = sb("prob", [128, self.cols])
        self.slot_i = sb("slot_i", [128, self.cols], I32)
        self.block_expert = sb("block_expert", [128, self.blocks], I32)
        self.rows = nc.dram_tensor(f"{name}_rows", [self.blocks * TOK, D], F32, kind="Internal").ap()
        self.results = nc.dram_tensor(f"{name}_results", [self.blocks * TOK, D], F32, kind="Internal").ap()


def pick_slots(nc, k, m):
    n, cols = m.n, m.cols
    width = n * cols
    cuts = [(a, min(a + 400, width)) for a in range(0, width, 400)]
    chunks = [(c, min(128, width - c)) for c in range(0, width, 128)]
    with Phase(nc, f"{m.name}_slots") as ph:
        totals = ph.sb("totals", [128, len(chunks)])
        totals_b = ph.sb("totals_b", [128, len(chunks), 128])
        base, rank = ph.sb("base", [128, n, cols]), ph.sb("rank", [128, n, cols])
        start_e, count_e = ph.sb("start_e", [128, n + 1]), ph.sb("count_e", [128, n])
        blk_n, blk_end = ph.sb("blk_n", [128, n]), ph.sb("blk_end", [128, 2, n])
        pad = ph.sb("pad", [128, n])
        cmp, blk_f = ph.sb("cmp", [128, m.blocks, n]), ph.sb("blk_f", [128, m.blocks])
        slot_f = ph.sb("slot_f", [128, cols])
        zeros = ph.sb("zeros", [128, 4, D])
        ps_tot = ph.ps("tot", [128, len(chunks)])
        ps_base = [ph.ps(f"base{c}", [128, 400]) for c in range(len(cuts))]
        ps_rank = [ph.ps(f"rank{c}", [128, 400]) for c in range(len(cuts))]
        tot_ready, totb_ready, base_ready, rank_ready = (ph.sem(f"{x}_ready") for x in ("tot", "totb", "base", "rank"))
        step, zero_made, zero_stored = ph.sem("step"), ph.sem("zero_made"), ph.sem("zero_stored")
        block = ph.ctx.enter_context(nc.Block())
        flat = m.onehot[:, :, :].rearrange("p e c -> p (e c)")

        @block.gpsimd
        def _(pool):
            pool.memset(zeros[:, :, :], 0.0).then_inc(zero_made, 1)

        @block.sync
        def _(sp):
            sp.wait_ge(zero_made, 1)
            for at in range(0, m.blocks, 4):
                c = min(4, m.blocks - at)
                sp.dma_start(m.rows[at * TOK:(at + c) * TOK, :].rearrange("(p c) d -> p c d", c=c),
                             zeros[:, 0:c, :]).then_inc(zero_stored, 16)
            sp.wait_ge(zero_stored, 16 * -(-m.blocks // 4))

        @block.tensor
        def _(pe):
            for c, (at, w) in enumerate(chunks):
                last = pe.matmul(ps_tot[0:w, c:c + 1], flat[0:P, at:at + w], k.ones[0:P, 0:1], start=True, stop=True)
            last.then_inc(tot_ready, 1)
            for c, (a, b) in enumerate(cuts):
                last = pe.matmul(ps_rank[c][0:P, 0:b - a], k.tri[0:P, 0:P], flat[0:P, a:b], start=True, stop=True)
            last.then_inc(rank_ready, 1)
            pe.wait_ge(totb_ready, len(chunks))
            for c, (a, b) in enumerate(cuts):
                for q, (at, w) in enumerate(chunks):
                    last = pe.matmul(ps_base[c][:, 0:b - a], totals_b[0:w, q, :], k.below[0:w, OFF - at + a:OFF - at + b],
                                     start=(q == 0), stop=(q == len(chunks) - 1))
            last.then_inc(base_ready, 1)

        @block.vector
        def _(dve):
            done = [0]

            def chain(ins):
                done[0] += 1
                ins.then_inc(step, 1)
                dve.wait_ge(step, done[0])

            dve.wait_ge(tot_ready, 1)
            for c, (at, w) in enumerate(chunks):
                chain(dve.tensor_copy(totals[0:w, c:c + 1], ps_tot[0:w, c:c + 1]))
                dve.tensor_copy(totals_b[0:w, c, :], totals[0:w, c:c + 1].to_broadcast([w, 128])).then_inc(totb_ready, 1)
            dve.wait_ge(base_ready, 1)
            flat_base, flat_rank = (x[:, :, :].rearrange("p e c -> p (e c)") for x in (base, rank))
            for c, (a, b) in enumerate(cuts):
                chain(dve.tensor_copy(flat_base[:, a:b], ps_base[c][:, 0:b - a]))
            chain(dve.tensor_copy(start_e[:, 0:n], base[:, :, 0]))
            chain(dve.memset(start_e[:, n:n + 1], float(N * m.picks)))
            chain(dve.tensor_tensor(count_e[:, :], start_e[:, 1:n + 1], start_e[:, 0:n], ALU.subtract))
            chain(dve.tensor_scalar(blk_n[:, :], count_e[:, :], 1.0 / TOK, (TOK - 1) / TOK - 0.5 + 0.5 / TOK, ALU.mult, ALU.add))
            chain(dve.tensor_scalar(blk_n[:, :], blk_n[:, :], MAGIC, None, ALU.add))
            chain(dve.tensor_scalar(blk_n[:, :], blk_n[:, :], MAGIC, None, ALU.subtract))
            chain(dve.tensor_copy(blk_end[:, 0, :], blk_n[:, :]))
            side, gap = 0, 1
            while gap < n:
                chain(dve.tensor_copy(blk_end[:, 1 - side, 0:gap], blk_end[:, side, 0:gap]))
                chain(dve.tensor_tensor(blk_end[:, 1 - side, gap:n], blk_end[:, side, gap:n], blk_end[:, side, 0:n - gap], ALU.add))
                side, gap = 1 - side, 2 * gap
            end = blk_end[:, side, :]
            chain(dve.tensor_tensor(pad[:, :], end, blk_n[:, :], ALU.subtract))
            chain(dve.scalar_tensor_tensor(pad[:, :], pad[:, :], float(TOK), start_e[:, 0:n], ALU.mult, ALU.subtract))
            chain(dve.tensor_tensor(base[:, :, :], base[:, :, :], pad[:, :].unsqueeze(2).to_broadcast([128, n, cols]), ALU.add))
            dve.wait_ge(rank_ready, 1)
            for c, (a, b) in enumerate(cuts):
                chain(dve.tensor_tensor(flat_rank[0:P, a:b], ps_rank[c][0:P, 0:b - a], flat_base[0:P, a:b], ALU.add))
            chain(dve.tensor_tensor(flat_rank[0:P, :], flat_rank[0:P, :], flat[0:P, :], ALU.mult))
            chain(dve.tensor_reduce(slot_f[0:P, :], rank[0:P, :, :].rearrange("p e c -> p c e"), AX.X, ALU.add))
            chain(dve.tensor_copy(m.slot_i[0:P, :], slot_f[0:P, :]))
            chain(dve.tensor_tensor(cmp[:, :, :], k.iota[:, 0:m.blocks].unsqueeze(2).to_broadcast([128, m.blocks, n]),
                                    end.unsqueeze(1).to_broadcast([128, m.blocks, n]), ALU.is_ge))
            chain(dve.tensor_reduce(blk_f[:, :], cmp[:, :, :], AX.X, ALU.add))
            chain(dve.tensor_scalar(blk_f[:, :], blk_f[:, :], float(n - 1), None, ALU.min))
            chain(dve.tensor_copy(m.block_expert[:, :], blk_f[:, :]))


def send_rows(nc, k, m):
    with Phase(nc, f"{m.name}_send") as ph:
        row_st, idx_st = ph.sb("row_st", [128, G, D]), ph.sb("idx_st", [128, G, m.picks], I32)
        staged, gate = ph.sem("staged"), ph.sem("gate")
        sent = ph.sems("sent", G)
        block = ph.ctx.enter_context(nc.Block())

        @block.vector
        def _(dve):
            def stage(i, first=False):
                for j in range(G):
                    if not first:
                        dve.wait_ge(sent[j], i * 16 * m.picks)
                        pass_on(dve, gate)
                    dve.tensor_copy(row_st[0:P, j, :], row(k.xn_sb, i * G + j)).then_inc(staged, 1)
                    dve.tensor_copy(idx_st[0:P, j, :], m.slot_i[0:P, ds((i * G + j) * m.picks, m.picks)]).then_inc(staged, 1)

            stage(0, first=True)
            with dve.Fori(1, NG) as i:
                stage(i)

        @block.gpsimd
        def _(pool):
            with pool.Fori(0, NG) as i:
                for j in range(G):
                    pool.wait_ge(staged, i * 2 * G + 2 * j + 2)
                    pass_on(pool, gate)
                    for q in range(m.picks):
                        pool.indirect_dma_start(m.rows, bass.IndirectOffsetOnAxis(ap=idx_st[0:P, j, q:q + 1].bitcast(U32), axis=0),
                                                row_st[0:P, j, :], None).then_inc(sent[j], 16)
            for j in range(G):
                pool.wait_ge(sent[j], NG * 16 * m.picks)


def run_experts(nc, k, m, w1_dram, w2_dram, bias_row, function):
    HC = m.hid // 128
    with Phase(nc, f"{m.name}_run") as ph:
        n_w1 = 2 if m.own_w1 else 1
        w1 = [ph.sb(f"w1_{s}", [128, 2, m.hid]) for s in range(n_w1)]
        w2 = [ph.sb(f"w2_{s}", [128, HC, D]) for s in range(2)]
        rows = [ph.sb(f"rows{s}", [128, D]) for s in range(2)]
        rows_t = [ph.sb(f"rows_t{s}", [128, 2, TOK]) for s in range(2)]
        hid = [ph.sb(f"hid{s}", [128, HC, TOK]) for s in range(2)]
        res = [ph.sb(f"res{s}", [128, D]) for s in range(2)]
        ps_t = [ph.ps(f"t{s}", [128, 2, TOK]) for s in range(2)]
        ps_h = [ph.ps(f"h{s}", [128, 4, TOK]) for s in range(4)]
        ps_r = [ph.ps(f"r{s}", [128, D]) for s in range(2)]
        HB = HC // 4
        w1_in, w2_in, rows_in, stored = (ph.sems(x, 2) for x in ("w1_in", "w2_in", "rows_in", "stored"))
        turned, kept, hid_sum, hid_made, res_sum, res_made = (
            ph.sem(x) for x in ("turned", "kept", "hid_sum", "hid_made", "res_sum", "res_made"))
        gate = ph.sem("gate")
        block = ph.ctx.enter_context(nc.Block())
        turns = m.blocks // 2

        @block.sync
        def _(sp):
            if not m.own_w1:
                sp.dma_start(w1[0][:, :, :], w1_dram.rearrange("(c p) h -> p c h", p=128)).then_inc(w1_in[0], 16)
            with sp.Fori(0, turns) as i:
                for s in range(2):
                    n = i * 2 + s
                    e = sp.value_load(m.block_expert[0:1, ds(n, 1)], min_val=0, max_val=m.n - 1)
                    sp.wait_ge(turned, n + 1)
                    pass_on(sp, gate)
                    sp.dma_start(rows[s][:, :], m.rows[ds(n * TOK, TOK), :]).then_inc(rows_in[s], 16)
                    sp.wait_ge(res_sum, n + 1)
                    pass_on(sp, gate)
                    if m.own_w1:
                        sp.dma_start(w1[s][:, :, :], w1_dram[ds(e, 1), :, :].rearrange("o (c p) h -> p (o c) h", p=128))\
                          .then_inc(w1_in[s], 16)
                    sp.dma_start(w2[s][:, :, :], w2_dram[ds(e, 1), :, :].rearrange("o (c p) h -> p (o c) h", p=128))\
                      .then_inc(w2_in[s], 16)

        @block.tensor
        def _(pe):
            pe.sem_inc(turned, 2)
            pe.sem_inc(hid_sum, 2 * HB)
            pe.sem_inc(res_sum, 2)
            if not m.own_w1:
                pe.wait_ge(w1_in[0], 16)
            with pe.Fori(0, turns) as i:
                for s in range(2):
                    n = i * 2 + s
                    pe.wait_ge(rows_in[s], i * 16 + 16)
                    pe.wait_ge(kept, n + 1)
                    for q in range(2):
                        last = pe.transpose(ps_t[s][:, q, :], rows[s][:, q * 128:(q + 1) * 128], k.ident[:, :])
                    last.then_inc(turned, 1)
                    pe.wait_ge(kept, n + 3)
                    if m.own_w1:
                        pe.wait_ge(w1_in[s], i * 16 + 16)
                    pe.wait_ge(hid_made, n + 1)
                    for c in range(HC):
                        for q in range(2):
                            last = pe.matmul(ps_h[s * HB + c // 4 if HB > 1 else s][:, c % 4, :],
                                             w1[s % n_w1][:, q, c * 128:(c + 1) * 128], rows_t[s][:, q, :],
                                             start=(q == 0), stop=(q == 1))
                        if c % 4 == 3:
                            last.then_inc(hid_sum, 1)
                    pe.wait_ge(w2_in[s], i * 16 + 16)
                    pe.wait_ge(hid_made, n + 3)
                    pe.wait_ge(res_made, n + 1)
                    for c in range(HC):
                        last = pe.matmul(ps_r[s][:, :], hid[s][:, c, :], w2[s][:, c, :], start=(c == 0), stop=(c == HC - 1))
                    last.then_inc(res_sum, 1)

        @block.scalar
        def _(act):
            act.sem_inc(hid_made, 2)
            with act.Fori(0, turns) as i:
                for s in range(2):
                    n = i * 2 + s
                    e = act.value_load(m.block_expert[0:1, ds(n, 1)], min_val=0, max_val=m.n - 1) if m.own_w1 else 0
                    act.wait_ge(res_sum, n + 1)
                    for c in range(HC):
                        if c % 4 == 0:
                            act.wait_ge(hid_sum, n * HB + c // 4 + 1 + 2 * HB)
                        pass_on(act, gate)
                        last = act.activation(hid[s][:, c, :], ps_h[s * HB + c // 4 if HB > 1 else s][:, c % 4, :], function,
                                              bias=k.cols[:, ds(bias_row + c + e * HC, 1)] if m.own_w1 else
                                              k.cols[:, bias_row + c:bias_row + c + 1])
                    last.then_inc(hid_made, 1)

        @block.vector
        def _(dve):
            dve.sem_inc(kept, 2)
            dve.sem_inc(res_made, 2)

            def keep_turned(n, s):
                dve.wait_ge(turned, n + 3)
                dve.wait_ge(res_sum, n + 1)
                dve.tensor_copy(rows_t[s][:, :, :], ps_t[s][:, :, :]).then_inc(kept, 1)

            def finish(i, s, first):
                dve.wait_ge(res_sum, i * 2 + s + 3)
                if not first:
                    dve.wait_ge(stored[s], i * 16)
                dve.tensor_copy(res[s][:, :], ps_r[s][:, :]).then_inc(res_made, 1)

            def turn(i, first=False):
                for s in range(2):
                    keep_turned(i * 2 + s, s)
                    finish(i, s, first)

            turn(0, first=True)
            with dve.Fori(1, turns) as i:
                turn(i)

        @block.gpsimd
        def _(pool):
            with pool.Fori(0, turns) as i:
                for s in range(2):
                    n = i * 2 + s
                    pool.wait_ge(res_made, n + 3)
                    pass_on(pool, gate)
                    pool.dma_start(m.results[ds(n * TOK, TOK), :], res[s][:, :]).then_inc(stored[s], 16)
            for s in range(2):
                pool.wait_ge(stored[s], 16 * turns)


def route_first(nc, k, m):
    with Phase(nc, "route0") as ph:
        ln = LayerNorm(ph)
        gw = ph.sb("gw", [128, 2, m.n])
        xs, x_t = ph.sb("xs", [128, G, D]), ph.sb("x_t", [128, 2, W])
        logit = ph.sb("logit", [128, G, m.n])
        top, top_i, top_f = ph.sb("top", [128, G, 8]), ph.sb("top_i", [128, G, 8], U32), ph.sb("top_f", [128, G, 2])
        diff, ratio, den = ph.sb("diff", [128, G]), ph.sb("ratio", [128, G]), ph.sb("den", [128, G])
        ps_t = [ph.ps(f"t{s}", [128, 2, 128]) for s in range(2)]
        ps_l = ph.ps("l", [128, G, m.n])
        w_in, turned, kept, logit_sum = ph.sem("w_in"), ph.sem("turned"), ph.sem("kept"), ph.sem("logit_sum")
        spread, step, diff_made, ratio_made = ph.sem("spread"), ph.sem("step"), ph.sem("diff_made"), ph.sem("ratio_made")
        gate = ph.sem("gate")
        block = ph.ctx.enter_context(nc.Block())
        STEPS = 2 + 2 * G + 5

        @block.sync
        def _(sp):
            sp.dma_start(gw[:, :, :], k.L0_ffn_gate_w.rearrange("(c p) e -> p c e", p=128)).then_inc(w_in, 16)

        @block.vector
        def _(dve):
            with dve.Fori(0, NG) as i:
                at = [i * STEPS]

                def chain(ins):
                    at[0] = at[0] + 1
                    ins.then_inc(step, 1)
                    dve.wait_ge(step, at[0])
                    pass_on(dve, gate)

                ln_vector(dve, ln, i, lambda j: row(k.x_sb, i * G + j), lambda j: xs[0:P, j, :])
                dve.wait_ge(logit_sum, i * G + G)
                chain(dve.tensor_tensor(logit[0:P, :, :], ps_l[0:P, :, :], k.gate_b[0:P, :].unsqueeze(1).to_broadcast([P, G, m.n]),
                                        ALU.add))
                for j in range(G):
                    chain(dve.max(top[0:P, j, :], logit[0:P, j, :]))
                    chain(dve.max_index(top_i[0:P, j, :], top[0:P, j, :], logit[0:P, j, :]))
                chain(dve.tensor_copy(top_f[0:P, :, :], top_i[0:P, :, 0:2]))
                dve.tensor_tensor(diff[0:P, :], top[0:P, :, 1], top[0:P, :, 0], ALU.subtract).then_inc(diff_made, 1)
                dve.wait_ge(ratio_made, i + 1)
                chain(dve.tensor_scalar(den[0:P, :], ratio[0:P, :], 1.0, None, ALU.add))
                chain(dve.reciprocal(den[0:P, :], den[0:P, :]))
                prob = m.prob[0:P, ds(i * 2 * G, 2 * G)].rearrange("p (j q) -> p j q", q=2)
                chain(dve.tensor_copy(prob[:, :, 0], den[0:P, :]))
                chain(dve.tensor_tensor(prob[:, :, 1], den[0:P, :], ratio[0:P, :], ALU.mult))
                chain(dve.tensor_tensor(m.onehot[0:P, :, ds(i * 2 * G, 2 * G)],
                                        top_f[0:P, :, :].rearrange("p j q -> p (j q)").unsqueeze(1).to_broadcast([P, m.n, 2 * G]),
                                        k.iota[0:P, 0:m.n].unsqueeze(2).to_broadcast([P, m.n, 2 * G]), ALU.is_equal))

        @block.scalar
        def _(act):
            with act.Fori(0, NG) as i:
                ln_scalar(act, k, ln, i)
                for j in range(G):
                    act.wait_ge(ln.out_done, i * G + j + 1)
                    pass_on(act, gate)
                    act.activation(row(k.xn_sb, i * G + j), xs[0:P, j, :], ACT.Copy).then_inc(spread, 1)
                    act.wait_ge(turned, i * G + j + 1)
                    pass_on(act, gate)
                    act.activation(x_t[:, :, j * P:(j + 1) * P], ps_t[j % 2][:, :, 0:P], ACT.Copy).then_inc(kept, 1)
                act.wait_ge(diff_made, i + 1)
                act.activation(ratio[0:P, :], diff[0:P, :], ACT.Exp).then_inc(ratio_made, 1)

        @block.tensor
        def _(pe):
            pe.wait_ge(w_in, 16)
            pe.sem_inc(kept, 2)
            with pe.Fori(0, NG) as i:
                for j in range(G):
                    pe.wait_ge(ln.out_done, i * G + j + 1)
                    pe.wait_ge(kept, i * G + j + 1)
                    for q in range(2):
                        last = pe.transpose(ps_t[j % 2][:, q, 0:P], xs[0:P, j, q * 128:(q + 1) * 128], k.ident[0:P, 0:P])
                    last.then_inc(turned, 1)
                for j in range(G):
                    pe.wait_ge(kept, i * G + j + 3)
                    for q in range(2):
                        last = pe.matmul(ps_l[0:P, j, :], x_t[:, q, j * P:(j + 1) * P], gw[:, q, :], start=(q == 0), stop=(q == 1))
                    last.then_inc(logit_sum, 1)


def combine(nc, k, m, bias_dram, norm):
    K = m.picks
    with Phase(nc, f"{m.name}_combine") as ph:
        ln = LayerNorm(ph)
        bias = ph.sb("bias", [m.n, D])
        idx_st = ph.sb("idx_st", [128, G, K], I32)
        got = ph.sb("got", [128, G, K, D])
        mix, mix_w = ph.sb("mix", [128, G, m.n, K]), ph.sb("mix_w", [128, G, m.n])
        mix_t = ph.sb("mix_t", [m.n, G, P])
        z, zn = ph.sb("z", [128, G, D]), ph.sb("zn", [128, G, D])
        ps_m = [ph.ps(f"m{s}", [128, 128]) for s in range(2)]
        ps_b = [ph.ps(f"b{s}", [128, D]) for s in range(2)]
        bias_in = ph.sem("bias_in")
        got_in = ph.sems("got_in", G)
        idx_made, mix_made, mixed, mix_turned, mix_kept = (
            ph.sem(x) for x in ("idx_made", "mix_made", "mixed", "mix_turned", "mix_kept"))
        bias_sum, z_made, zn_made, stored, gate = (ph.sem(x) for x in ("bias_sum", "z_made", "zn_made", "stored", "gate"))
        block = ph.ctx.enter_context(nc.Block())
        ZS = K + 1

        @block.sync
        def _(sp):
            sp.dma_start(bias[:, :], bias_dram).then_inc(bias_in, 16)
            if not norm:
                sp.wait_ge(zn_made, T)
                sp.dma_start(k.out.rearrange("(t p) d -> p t d", p=P), k.x_sb[0:P, :, :]).then_inc(stored, 16)
                sp.wait_ge(stored, 16)

        @block.gpsimd
        def _(pool):
            with pool.Fori(0, NG) as i:
                for j in range(G):
                    pool.wait_ge(idx_made, i * G + j + 1)
                    pass_on(pool, gate)
                    for q in range(K):
                        pool.indirect_dma_start(got[0:P, j, q, :], None, m.results,
                                                bass.IndirectOffsetOnAxis(ap=idx_st[0:P, j, q:q + 1].bitcast(U32), axis=0))\
                            .then_inc(got_in[j], 16)

        @block.vector
        def _(dve):
            with dve.Fori(0, NG) as i:
                for j in range(G):
                    dve.tensor_copy(idx_st[0:P, j, :], m.slot_i[0:P, ds((i * G + j) * K, K)]).then_inc(idx_made, 1)
                for j in range(G):
                    cols = ds((i * G + j) * K, K)
                    dve.tensor_tensor(mix[0:P, j, :, :], m.onehot[0:P, :, cols],
                                      m.prob[0:P, cols].unsqueeze(1).to_broadcast([P, m.n, K]), ALU.mult).then_inc(mix_made, 1)
                dve.wait_ge(mix_made, i * G + G)
                pass_on(dve, gate)
                for j in range(G):
                    dve.tensor_reduce(mix_w[0:P, j, :], mix[0:P, j, :, :], AX.X, ALU.add).then_inc(mixed, 1)
                for j in range(G):
                    base = row(k.xn_sb if norm else k.x_sb, i * G + j)
                    dve.wait_ge(bias_sum, i * G + j + 1)
                    pass_on(dve, gate)
                    dve.tensor_tensor(z[0:P, j, :], ps_b[j % 2][0:P, :], base, ALU.add).then_inc(z_made, 1)
                    dve.wait_ge(got_in[j], (i + 1) * 16 * K)
                    for q in range(K):
                        dve.wait_ge(z_made, (i * G + j) * ZS + q + 1)
                        ins = dve.scalar_tensor_tensor(z[0:P, j, :] if norm or q < K - 1 else base, got[0:P, j, q, :],
                                                       m.prob[0:P, ds((i * G + j) * K + q, 1)], z[0:P, j, :], ALU.mult, ALU.add)
                        ins.then_inc(z_made, 1)
                if norm:
                    dve.wait_ge(z_made, (i + 1) * G * ZS)
                    pass_on(dve, gate)
                    ln_vector(dve, ln, i, lambda j: z[0:P, j, :], lambda j: zn[0:P, j, :])
                    dve.wait_ge(ln.out_done, i * G + G)
                    dve.tensor_tensor(zn[0:P, :, :], zn[0:P, :, :], k.gamma[0:P, :].unsqueeze(1).to_broadcast([P, G, D]), ALU.mult)\
                       .then_inc(zn_made, 1)
                    dve.wait_ge(zn_made, i * 3 + 1)
                    dve.tensor_tensor(zn[0:P, :, :], zn[0:P, :, :], k.beta[0:P, :].unsqueeze(1).to_broadcast([P, G, D]), ALU.add)\
                       .then_inc(zn_made, 1)
                    dve.wait_ge(zn_made, i * 3 + 2)
                    group = k.x_sb[0:P, ds(i * G, G), :]
                    dve.tensor_tensor(group, zn[0:P, :, :], group, ALU.add).then_inc(zn_made, 1)
            if not norm:
                dve.wait_ge(z_made, T * ZS)
                dve.sem_inc(zn_made, T)

        @block.scalar
        def _(act):
            with act.Fori(0, NG) as i:
                for j in range(G):
                    act.wait_ge(mix_turned, i * G + j + 1)
                    pass_on(act, gate)
                    act.activation(mix_t[:, j, :], ps_m[j % 2][0:m.n, 0:P], ACT.Copy).then_inc(mix_kept, 1)
                if norm:
                    ln_scalar(act, k, ln, i)

        @block.tensor
        def _(pe):
            pe.wait_ge(bias_in, 16)
            pe.sem_inc(mix_kept, 2)

            def tiles(i, first=False):
                for j in range(G):
                    pe.wait_ge(mixed, i * G + j + 1)
                    pe.wait_ge(mix_kept, i * G + j + 1)
                    pe.transpose(ps_m[j % 2][0:m.n, 0:P], mix_w[0:P, j, :], k.ident[0:P, 0:P]).then_inc(mix_turned, 1)
                for j in range(G):
                    pe.wait_ge(mix_kept, i * G + j + 3)
                    if not first or j >= 2:
                        pe.wait_ge(z_made, (i * G + j - 2) * ZS + 1)
                    pe.matmul(ps_b[j % 2][0:P, :], mix_t[:, j, :], bias[:, :], start=True, stop=True).then_inc(bias_sum, 1)

            tiles(0, first=True)
            with pe.Fori(1, NG) as i:
                tiles(i)


def vectors_apart(ap):
    return ap[:, MUL:D].rearrange("p (u c) -> p c u", c=3)


def edge_table(nc, k):
    with Phase(nc, "table") as ph:
        ln = LayerNorm(ph)
        raw = ph.sb("raw", [128, 2, 2, 128])
        w = ph.sb("w", [128, 2, 2, 128])
        xs, xq, x_t = ph.sb("xs", [128, G, D]), ph.sb("xq", [128, G, D]), ph.sb("x_t", [128, G, 2, P])
        y = ph.sb("y", [128, G, D])
        ps_t = [ph.ps(f"t{s}", [128, 2, 128]) for s in range(2)]
        ps_y = [ph.ps(f"y{s}", [128, D]) for s in range(2)]
        ps_s = [ph.ps(f"s{s}", [128, D]) for s in range(2)]
        raw_zero, raw_in, w_made = ph.sem("raw_zero"), ph.sem("raw_in"), ph.sem("w_made")
        apart, turned, kept, made, y_made, added = (ph.sem(x) for x in ("apart", "turned", "kept", "made", "y_made", "added"))
        stored, gate = ph.sem("stored"), ph.sem("gate")
        block = ph.ctx.enter_context(nc.Block())

        @block.gpsimd
        def _(pool):
            pool.memset(raw[:, :, :, :], 0.0).then_inc(raw_zero, 1)

        @block.sync
        def _(sp):
            sp.wait_ge(raw_zero, 1)
            for which, (w0, w1) in enumerate([(k.L1_gnn_lin1_w0, k.L1_gnn_lin1_w1), (k.L1_gnn_sc_w0, k.L1_gnn_sc_w1)]):
                sp.dma_start(raw[0:MUL, which, 0, 0:MUL], w0).then_inc(raw_in, 16)
                sp.dma_start(raw[MUL:128, which, 0, MUL:128], w1).then_inc(raw_in, 16)
                sp.dma_start(raw[0:MUL, which, 1, 0:MUL], w1).then_inc(raw_in, 16)
                sp.dma_start(raw[MUL:128, which, 1, MUL:128], w1).then_inc(raw_in, 16)
            with sp.Fori(0, NG) as i:
                sp.wait_ge(y_made, i * G + G)
                pass_on(sp, gate)
                sp.dma_start(k.y_dram[ds(i * W, W), :].rearrange("(j p) d -> p j d", p=P), y[0:P, :, :]).then_inc(stored, 16)
                sp.wait_ge(stored, i * 16 + 16)
                pass_on(sp, gate)

        @block.vector
        def _(dve):
            dve.wait_ge(raw_in, 128)
            dve.tensor_scalar(w[:, 0, :, :], raw[:, 0, :, :], INV_MUL, None, ALU.mult).then_inc(w_made, 1)
            dve.tensor_scalar(w[:, 1, :, :], raw[:, 1, :, :], INV_MUL * C_S, None, ALU.mult).then_inc(w_made, 1)
            with dve.Fori(0, NG) as i:
                ln_vector(dve, ln, i, lambda j: row(k.x_sb, i * G + j), lambda j: xs[0:P, j, :])
                for j in range(G):
                    dve.wait_ge(made, i * G + j + 1)
                    pass_on(dve, gate)
                    x, a = row(k.x_sb, i * G + j), k.node_a[0:P, ds(i * G + j, 1)]
                    dve.scalar_tensor_tensor(x[:, 0:MUL], ps_s[j % 2][0:P, 0:MUL], a, x[:, 0:MUL], ALU.mult, ALU.add).then_inc(added, 1)
                    dve.scalar_tensor_tensor(vectors_apart(x), ps_s[j % 2][0:P, MUL:D].rearrange("p (c u) -> p c u", c=3), a,
                                             vectors_apart(x), ALU.mult, ALU.add).then_inc(added, 1)

        @block.scalar
        def _(act):
            def tiles(i, first=False):
                ln_scalar(act, k, ln, i)
                for j in range(G):
                    act.wait_ge(ln.out_done, i * G + j + 1)
                    act.activation(xq[0:P, j, 0:MUL], xs[0:P, j, 0:MUL], ACT.Copy).then_inc(apart, 1)
                    act.activation(xq[0:P, j, MUL:D].rearrange("p (c u) -> p c u", c=3), vectors_apart(xs[0:P, j, :]), ACT.Copy)\
                       .then_inc(apart, 1)
                for j in range(G):
                    act.wait_ge(turned, i * G + j + 1)
                    act.activation(x_t[:, j, :, :], ps_t[j % 2][:, :, 0:P], ACT.Copy).then_inc(kept, 1)
                for j in range(G):
                    act.wait_ge(made, i * G + j + 1)
                    if not first:
                        act.wait_ge(stored, i * 16)
                    pass_on(act, gate)
                    act.activation(y[0:P, j, :], ps_y[j % 2][0:P, :], ACT.Copy, scale=k.node_a[0:P, ds(i * G + j, 1)])\
                       .then_inc(y_made, 1)

            tiles(0, first=True)
            with act.Fori(1, NG) as i:
                tiles(i)

        @block.tensor
        def _(pe):
            pe.wait_ge(w_made, 2)
            pe.sem_inc(kept, 2)

            def tiles(i, first=False):
                for j in range(G):
                    pe.wait_ge(apart, (i * G + j) * 2 + 2)
                    pe.wait_ge(kept, i * G + j + 1)
                    for q in range(2):
                        last = pe.transpose(ps_t[j % 2][:, q, 0:P], xq[0:P, j, q * 128:(q + 1) * 128], k.ident[0:P, 0:P])
                    last.then_inc(turned, 1)
                for j in range(G):
                    pe.wait_ge(kept, i * G + j + 3)
                    if not first or j >= 2:
                        pe.wait_ge(y_made, i * G + j - 1)
                        pe.wait_ge(added, (i * G + j - 1) * 2)
                    for which, ps in enumerate((ps_y, ps_s)):
                        for q in range(2):
                            last = pe.matmul(ps[j % 2][0:P, q * 128:(q + 1) * 128], x_t[:, j, q, :], w[:, which, q, :],
                                             start=True, stop=True)
                    last.then_inc(made, 1)

            tiles(0, first=True)
            with pe.Fori(1, NG) as i:
                tiles(i)


def sum_messages(nc, k):
    with Phase(nc, "msg") as ph:
        fc1, fc2_raw, fc2 = ph.sb("fc1", [8, 64]), ph.sb("fc2_raw", [64, D]), ph.sb("fc2", [64, D])
        rec = [ph.sb(f"rec{s}", [128, 2, REC]) for s in range(SLOTS)]
        got = [ph.sb(f"got{s}", [128, 2, 4, MUL]) for s in range(SLOTS)]
        onehot = [ph.sb(f"onehot{s}", [128, 2, P]) for s in range(2)]
        attr_t = [ph.sb(f"attr_t{s}", [8, 2 * 128]) for s in range(2)]
        hid = [ph.sb(f"hid{s}", [64, 2 * 128]) for s in range(2)]
        scaled = [ph.sb(f"scaled{s}", [128, 2, 4, MUL]) for s in range(2)]
        part = [ph.sb(f"part{s}", [128, 2, 3, MUL]) for s in range(2)]
        cross = [ph.sb(f"cross{s}", [128, 2, MUL]) for s in range(2)]
        dot = [ph.sb(f"dot{s}", [128, 2, MUL]) for s in range(2)]
        msg = [ph.sb(f"msg{s}", [128, 2, 4, 2, MUL]) for s in range(2)]
        ps_e = [ph.ps(f"e{s}", [128, 512]) for s in range(2)]
        ps_w = [ph.ps(f"w{s}", [128, 2, 4, MUL]) for s in range(2)]
        ps_z = [ph.ps(f"z{s}", [128, 2 * D]) for s in range(2)]
        w_in, w_made = ph.sem("w_in"), ph.sem("w_made")
        rec_in, got_in = ph.sems("rec_in", SLOTS), ph.sems("got_in", SLOTS)
        attr_turned, attr_kept, hid_sum, hid_made, w_sum = (
            ph.sem(x) for x in ("attr_turned", "attr_kept", "hid_sum", "hid_made", "w_sum"))
        scaled_made, masked, msg_step, msg_made, summed, added = (
            ph.sem(x) for x in ("scaled_made", "masked", "msg_step", "msg_made", "summed", "added"))
        cleared, gate = ph.sem("cleared"), ph.sem("gate")
        block = ph.ctx.enter_context(nc.Block())
        turns = NEB // SLOTS

        @block.sync
        def _(sp):
            sp.dma_start(fc1[:, :], k.L1_gnn_fc_w1).then_inc(w_in, 16)
            sp.dma_start(fc2_raw[:, :], k.L1_gnn_fc_w2).then_inc(w_in, 16)

            def turn(i, first=False):
                for s in range(SLOTS):
                    n = i * SLOTS + s
                    start = sp.value_load(k.block_start[0:1, ds(n, 1)], min_val=0, max_val=E)
                    if not first:
                        sp.wait_ge(summed, n - SLOTS + 1)
                        pass_on(sp, gate)
                    sp.dma_start(rec[s][:, :, :], k.recs[ds(start, EB), :].rearrange("(p u) w -> p u w", u=2))\
                      .then_inc(rec_in[s], 16)

            turn(0, first=True)
            with sp.Fori(1, turns) as i:
                turn(i)

        @block.gpsimd
        def _(pool):
            with pool.Fori(0, turns) as i:
                for s in range(SLOTS):
                    pool.wait_ge(rec_in[s], i * 16 + 16)
                    pass_on(pool, gate)
                    for u in range(2):
                        pool.indirect_dma_start(
                            got[s][:, u, :, :].rearrange("p k v -> p (k v)"), None, k.y_dram,
                            bass.IndirectOffsetOnAxis(ap=rec[s][:, u, SRC:SRC + 1].bitcast(U32), axis=0)).then_inc(got_in[s], 16)

        @block.tensor
        def _(pe):
            pe.wait_ge(w_made, 1)

            def weigh(n, b):
                pe.wait_ge(hid_made, n + 1)
                for u in range(2):
                    last = pe.matmul(ps_w[b][:, u, :, :].rearrange("p k v -> p (k v)"), hid[b][:, u * 128:(u + 1) * 128],
                                     fc2[:, :], start=True, stop=True)
                last.then_inc(w_sum, 1)

            def add_up(n, b):
                pe.wait_ge(msg_made, n + 1)
                for u in range(2):
                    last = pe.matmul(ps_z[b][0:P, :], onehot[b][:, u, :], msg[b][:, u, :, :, :].rearrange("p k h v -> p (k h v)"),
                                     start=(u == 0), stop=(u == 1))
                last.then_inc(summed, 1)

            def turn(i, first=False):
                for s in range(SLOTS):
                    n, b = i * SLOTS + s, s % 2
                    pe.wait_ge(rec_in[s], i * 16 + 16)
                    if not first or s >= 2:
                        pe.wait_ge(hid_made, n - 1)
                    for u in range(2):
                        last = pe.transpose(ps_e[b][0:8, u * 128:(u + 1) * 128], rec[s][:, u, 0:8], k.ident[:, :])
                    last.then_inc(attr_turned, 1)
                    if not first or s >= 1:
                        if not first or s >= 3:
                            pe.wait_ge(msg_made, n - 2)
                        weigh(n - 1, 1 - b)
                    pe.wait_ge(attr_kept, n + 1)
                    pe.matmul(ps_e[b][0:64, 256:512], fc1[:, :], attr_t[b][:, :], start=True, stop=True).then_inc(hid_sum, 1)
                    if not first or s >= 2:
                        if not first or s >= 4:
                            pe.wait_ge(added, n - 3)
                        add_up(n - 2, b)

            turn(0, first=True)
            with pe.Fori(1, turns) as i:
                turn(i)
            pe.wait_ge(msg_made, NEB - 2)
            weigh(NEB - 1, 1)
            pe.wait_ge(added, NEB - 3)
            add_up(NEB - 2, 0)
            pe.wait_ge(added, NEB - 2)
            add_up(NEB - 1, 1)

        @block.scalar
        def _(act):
            def turn(i, first=False):
                for s in range(SLOTS):
                    n, b = i * SLOTS + s, s % 2
                    act.wait_ge(attr_turned, n + 1)
                    if not first or s >= 2:
                        act.wait_ge(w_sum, n - 1)
                    act.activation(attr_t[b][:, :], ps_e[b][0:8, 0:256], ACT.Copy).then_inc(attr_kept, 1)
                    act.wait_ge(hid_sum, n + 1)
                    act.activation(hid[b][:, :], ps_e[b][0:64, 256:512], ACT.Silu, scale=1.0 / math.sqrt(8)).then_inc(hid_made, 1)
                    act.wait_ge(got_in[s], i * 32 + 32)
                    if not first or s >= 2:
                        act.wait_ge(msg_made, n - 1)
                    pass_on(act, gate)
                    for u in range(2):
                        act.activation(scaled[b][:, u, :, :], got[s][:, u, :, :], ACT.Copy, scale=rec[s][:, u, 8:9])\
                           .then_inc(scaled_made, 1)

            turn(0, first=True)
            with act.Fori(1, turns) as i:
                turn(i)

        @block.vector
        def _(dve):
            dve.memset(k.agg[:, :, :], 0.0).then_inc(cleared, 1)
            dve.wait_ge(w_in, 32)
            dve.tensor_scalar(fc2[:, :], fc2_raw[:, :], SILU_NORM / 8.0, None, ALU.mult).then_inc(cleared, 1)
            dve.wait_ge(cleared, 2)
            dve.tensor_scalar(fc2[:, MUL:2 * MUL], fc2[:, MUL:2 * MUL], 1.0 / math.sqrt(3.0), None, ALU.mult).then_inc(w_made, 1)

            def add_sum(n, b, any_before=True):
                tile = dve.value_load(k.block_tile[0:1, ds(n, 1)], min_val=0, max_val=T - 1)
                dve.wait_ge(summed, n + 1)
                if any_before:
                    dve.wait_ge(added, n)
                dve.tensor_tensor(row(k.agg, tile), ps_z[b][0:P, :], row(k.agg, tile), ALU.add).then_inc(added, 1)

            def turn(i, first=False):
                for s in range(SLOTS):
                    n, b = i * SLOTS + s, s % 2
                    dve.wait_ge(rec_in[s], i * 16 + 16)
                    if not first or s >= 2:
                        dve.wait_ge(summed, n - 1)
                    for u in range(2):
                        dve.tensor_scalar(onehot[b][:, u, :], k.iota[:, 0:P], k.block_node[:, ds(n, 1)],
                                          rec[s][:, u, DST:DST + 1], ALU.add, ALU.is_equal).then_inc(masked, 1)
                    w, y, m = ps_w[b], got[s], msg[b]
                    ea1 = rec[s][:, :, 9:12].unsqueeze(3).to_broadcast([128, 2, 3, MUL])
                    dve.wait_ge(got_in[s], i * 32 + 32)
                    dve.tensor_tensor(part[b][:, :, :, :], y[:, :, 1:4, :], ea1, ALU.mult).then_inc(msg_step, 1)
                    dve.wait_ge(w_sum, n + 1)
                    dve.tensor_tensor(cross[b][:, :, :], w[:, :, 2, :], y[:, :, 0, :], ALU.mult).then_inc(msg_step, 1)
                    dve.wait_ge(msg_step, n * 3 + 1)
                    pass_on(dve, gate)
                    dve.tensor_reduce(dot[b][:, :, :], part[b][:, :, :, :].rearrange("p u c v -> p u v c"), AX.X, ALU.add)\
                       .then_inc(msg_step, 1)
                    dve.wait_ge(scaled_made, 2 * n + 2)
                    dve.tensor_tensor(m[:, :, 0, 0, :], w[:, :, 0, :], scaled[b][:, :, 0, :], ALU.mult)
                    dve.tensor_tensor(m[:, :, 1:4, 1, :], w[:, :, 3, :].unsqueeze(2).to_broadcast([128, 2, 3, MUL]),
                                      scaled[b][:, :, 1:4, :], ALU.mult)
                    dve.wait_ge(msg_step, n * 3 + 3)
                    dve.tensor_tensor(m[:, :, 1:4, 0, :], cross[b][:, :, :].unsqueeze(2).to_broadcast([128, 2, 3, MUL]), ea1, ALU.mult)
                    dve.tensor_tensor(m[:, :, 0, 1, :], w[:, :, 1, :], dot[b][:, :, :], ALU.mult).then_inc(msg_made, 1)
                    if not first or s >= 1:
                        add_sum(n - 1, 1 - b, any_before=not first or s >= 2)

            turn(0, first=True)
            with dve.Fori(1, turns) as i:
                turn(i)
            add_sum(NEB - 1, 1)


def update_nodes(nc, k):
    FACTOR = C_X / math.sqrt(20.0) / math.sqrt(2 * MUL)
    with Phase(nc, "update") as ph:
        raw, w = ph.sb("raw", [128, 2, MUL]), ph.sb("w", [128, 2, MUL])
        tile = ph.sb("tile", [128, G, 4, 128])
        tile_t = ph.sb("tile_t", [128, G, 4, P])
        ps_t = [ph.ps(f"t{s}", [128, 4, 128]) for s in range(2)]
        ps_o = [ph.ps(f"o{s}", [128, D]) for s in range(2)]
        raw_in, w_made, staged, turned, kept, made, added, gate = (
            ph.sem(x) for x in ("raw_in", "w_made", "staged", "turned", "kept", "made", "added", "gate"))
        block = ph.ctx.enter_context(nc.Block())

        @block.sync
        def _(sp):
            for q, (wa, wb) in enumerate([(k.L1_gnn_lin2_w00, k.L1_gnn_lin2_w01), (k.L1_gnn_lin2_w10, k.L1_gnn_lin2_w11)]):
                sp.dma_start(raw[0:MUL, q, :], wa).then_inc(raw_in, 16)
                sp.dma_start(raw[MUL:128, q, :], wb).then_inc(raw_in, 16)

        @block.vector
        def _(dve):
            dve.wait_ge(raw_in, 64)
            dve.tensor_scalar(w[:, :, :], raw[:, :, :], FACTOR, None, ALU.mult).then_inc(w_made, 1)
            dve.sem_inc(turned, G)
            with dve.Fori(0, NG) as i:
                for j in range(G):
                    dve.wait_ge(turned, i * G + j + 1)
                    pass_on(dve, gate)
                    dve.tensor_copy(tile[0:P, j, :, :].rearrange("p k v -> p (k v)"), row(k.agg, i * G + j)).then_inc(staged, 1)
                for j in range(G):
                    dve.wait_ge(made, i * G + j + 1)
                    pass_on(dve, gate)
                    x, a = row(k.x_sb, i * G + j), k.node_a[0:P, ds(i * G + j, 1)]
                    dve.scalar_tensor_tensor(x[:, 0:MUL], ps_o[j % 2][0:P, 0:MUL], a, x[:, 0:MUL], ALU.mult, ALU.add).then_inc(added, 1)
                    dve.scalar_tensor_tensor(vectors_apart(x), ps_o[j % 2][0:P, MUL:D].rearrange("p (c u) -> p c u", c=3), a,
                                             vectors_apart(x), ALU.mult, ALU.add).then_inc(added, 1)

        @block.scalar
        def _(act):
            with act.Fori(0, NG) as i:
                for j in range(G):
                    act.wait_ge(turned, i * G + j + 1 + G)
                    act.activation(tile_t[:, j, :, :], ps_t[j % 2][:, :, 0:P], ACT.Copy).then_inc(kept, 1)

        @block.tensor
        def _(pe):
            pe.wait_ge(w_made, 1)
            pe.sem_inc(kept, 2)

            def tiles(i, first=False):
                for j in range(G):
                    pe.wait_ge(staged, i * G + j + 1)
                    pe.wait_ge(kept, i * G + j + 1)
                    for q in range(4):
                        last = pe.transpose(ps_t[j % 2][:, q, 0:P], tile[0:P, j, q, :], k.ident[0:P, 0:P])
                    last.then_inc(turned, 1)
                for j in range(G):
                    pe.wait_ge(kept, i * G + j + 3)
                    if not first or j >= 2:
                        pe.wait_ge(added, (i * G + j - 1) * 2)
                    for q in range(4):
                        last = pe.matmul(ps_o[j % 2][0:P, q * MUL:(q + 1) * MUL], tile_t[:, j, q, :], w[:, min(q, 1), :],
                                         start=True, stop=True)
                    last.then_inc(made, 1)

            tiles(0, first=True)
            with pe.Fori(1, NG) as i:
                tiles(i)


def route_second(nc, k, m):
    HC = m.hid // 128
    with Phase(nc, "route1") as ph:
        ln = LayerNorm(ph)
        w1, wg = ph.sb("w1", [128, 2, m.hid]), ph.sb("wg", [128, HC, m.n])
        xs, x_t, hid = ph.sb("xs", [128, G, D]), ph.sb("x_t", [128, 2, W]), ph.sb("hid", [128, HC, W])
        logit, top, top_i = ph.sb("logit", [128, G, m.n]), ph.sb("top", [128, G, 8]), ph.sb("top_i", [128, G, 8], U32)
        top_f, total = ph.sb("top_f", [128, G]), ph.sb("total", [128, G])
        shifted, expd = ph.sb("shifted", [128, G, m.n]), ph.sb("expd", [128, G, m.n])
        ps_t = [ph.ps(f"t{s}", [128, 2, 128]) for s in range(2)]
        ps_h = [ph.ps(f"h{s}", [128, 512]) for s in range(4)]
        ps_l = ph.ps("l", [128, G, m.n])
        w_in, turned, kept, hid_sum, hid_made, logit_sum = (
            ph.sem(x) for x in ("w_in", "turned", "kept", "hid_sum", "hid_made", "logit_sum"))
        spread, step, shift_made, exp_made, gate = (ph.sem(x) for x in ("spread", "step", "shift_made", "exp_made", "gate"))
        block = ph.ctx.enter_context(nc.Block())
        STEPS = 1 + 2 * G + 4
        H2 = 2 * HC

        @block.sync
        def _(sp):
            sp.dma_start(w1[:, :, :], k.L1_ffn_W1.rearrange("(c p) h -> p c h", p=128)).then_inc(w_in, 16)
            sp.dma_start(wg[:, :, :], k.L1_ffn_Wg.rearrange("(c p) h -> p c h", p=128)).then_inc(w_in, 16)

        @block.vector
        def _(dve):
            with dve.Fori(0, NG) as i:
                at = [i * STEPS]

                def chain(ins):
                    at[0] = at[0] + 1
                    ins.then_inc(step, 1)
                    dve.wait_ge(step, at[0])
                    pass_on(dve, gate)

                ln_vector(dve, ln, i, lambda j: row(k.x_sb, i * G + j), lambda j: xs[0:P, j, :])
                dve.wait_ge(logit_sum, i * G + G)
                chain(dve.tensor_tensor(logit[0:P, :, :], ps_l[0:P, :, :], k.bg[0:P, :].unsqueeze(1).to_broadcast([P, G, m.n]), ALU.add))
                for j in range(G):
                    chain(dve.max(top[0:P, j, :], logit[0:P, j, :]))
                    chain(dve.max_index(top_i[0:P, j, :], top[0:P, j, :], logit[0:P, j, :]))
                chain(dve.tensor_copy(top_f[0:P, :], top_i[0:P, :, 0]))
                dve.tensor_tensor(shifted[0:P, :, :], logit[0:P, :, :], top[0:P, :, 0:1].to_broadcast([P, G, m.n]), ALU.subtract)\
                   .then_inc(shift_made, 1)
                dve.wait_ge(exp_made, i + 1)
                chain(dve.tensor_reduce(total[0:P, :], expd[0:P, :, :], AX.X, ALU.add))
                chain(dve.reciprocal(m.prob[0:P, ds(i * G, G)], total[0:P, :]))
                chain(dve.tensor_tensor(m.onehot[0:P, :, ds(i * G, G)], top_f[0:P, :].unsqueeze(1).to_broadcast([P, m.n, G]),
                                        k.iota[0:P, 0:m.n].unsqueeze(2).to_broadcast([P, m.n, G]), ALU.is_equal))

        @block.scalar
        def _(act):
            with act.Fori(0, NG) as i:
                ln_scalar(act, k, ln, i)
                for j in range(G):
                    act.wait_ge(ln.out_done, i * G + j + 1)
                    pass_on(act, gate)
                    act.activation(row(k.xn_sb, i * G + j), xs[0:P, j, :], ACT.Copy).then_inc(spread, 1)
                    act.wait_ge(turned, i * G + j + 1)
                    pass_on(act, gate)
                    act.activation(x_t[:, :, j * P:(j + 1) * P], ps_t[j % 2][:, :, 0:P], ACT.Copy).then_inc(kept, 1)
                for c, (a, b) in enumerate(CUTS):
                    for h in range(HC):
                        act.wait_ge(hid_sum, i * H2 + c * HC + h + 1)
                        act.activation(hid[:, h, a:b], ps_h[h % 4][:, 0:b - a], ACT.Gelu,
                                       bias=k.cols[:, FFN1_B1 + h:FFN1_B1 + h + 1]).then_inc(hid_made, 1)
                act.wait_ge(shift_made, i + 1)
                act.activation(expd[0:P, :, :], shifted[0:P, :, :], ACT.Exp).then_inc(exp_made, 1)

        @block.tensor
        def _(pe):
            pe.wait_ge(w_in, 32)
            pe.sem_inc(kept, 2)
            pe.sem_inc(hid_made, 4)
            with pe.Fori(0, NG) as i:
                for j in range(G):
                    pe.wait_ge(ln.out_done, i * G + j + 1)
                    pe.wait_ge(kept, i * G + j + 1)
                    for q in range(2):
                        last = pe.transpose(ps_t[j % 2][:, q, 0:P], xs[0:P, j, q * 128:(q + 1) * 128], k.ident[0:P, 0:P])
                    last.then_inc(turned, 1)
                pe.wait_ge(kept, i * G + G + 2)
                for c, (a, b) in enumerate(CUTS):
                    for h in range(HC):
                        pe.wait_ge(hid_made, i * H2 + c * HC + h + 1)
                        for q in range(2):
                            last = pe.matmul(ps_h[h % 4][:, 0:b - a], w1[:, q, h * 128:(h + 1) * 128], x_t[:, q, a:b],
                                             start=(q == 0), stop=(q == 1))
                        last.then_inc(hid_sum, 1)
                pe.wait_ge(hid_made, i * H2 + H2 + 4)
                for j in range(G):
                    for h in range(HC):
                        last = pe.matmul(ps_l[0:P, j, :], hid[:, h, j * P:(j + 1) * P], wg[:, h, :], start=(h == 0), stop=(h == HC - 1))
                    last.then_inc(logit_sum, 1)


_NAMES = ['x', 'src', 'dst', 'edge_attr_4', 'edge_attr_8', 'node_vec1', 'L0_gnn_eps', 'L0_gnn_W1', 'L0_gnn_b1',
          'L0_gnn_W2', 'L0_gnn_b2', 'L0_gnn_gamma', 'L0_gnn_beta', 'L0_ffn_gate_w', 'L0_ffn_gate_b', 'L0_ffn_w1',
          'L0_ffn_b1', 'L0_ffn_w2', 'L0_ffn_b2', 'L0_ffn_gamma', 'L0_ffn_beta', 'L1_gnn_sc_w0', 'L1_gnn_sc_w1',
          'L1_gnn_lin1_w0', 'L1_gnn_lin1_w1', 'L1_gnn_fc_w1', 'L1_gnn_fc_w2', 'L1_gnn_lin2_w00', 'L1_gnn_lin2_w01',
          'L1_gnn_lin2_w10', 'L1_gnn_lin2_w11', 'L1_ffn_W1', 'L1_ffn_b1', 'L1_ffn_Wg', 'L1_ffn_bg', 'L1_ffn_Wd',
          'L1_ffn_bd']


def build(nc, inputs, out, stop=99):
    k = Kept()
    (k.x, k.src, k.dst, k.edge_attr_4, k.edge_attr_8, k.node_vec1, k.L0_gnn_eps, k.L0_gnn_W1, k.L0_gnn_b1,
     k.L0_gnn_W2, k.L0_gnn_b2, k.L0_gnn_gamma, k.L0_gnn_beta, k.L0_ffn_gate_w, k.L0_ffn_gate_b, k.L0_ffn_w1,
     k.L0_ffn_b1, k.L0_ffn_w2, k.L0_ffn_b2, k.L0_ffn_gamma, k.L0_ffn_beta, k.L1_gnn_sc_w0, k.L1_gnn_sc_w1,
     k.L1_gnn_lin1_w0, k.L1_gnn_lin1_w1, k.L1_gnn_fc_w1, k.L1_gnn_fc_w2, k.L1_gnn_lin2_w00, k.L1_gnn_lin2_w01,
     k.L1_gnn_lin2_w10, k.L1_gnn_lin2_w11, k.L1_ffn_W1, k.L1_ffn_b1, k.L1_ffn_Wg, k.L1_ffn_bg, k.L1_ffn_Wd,
     k.L1_ffn_bd) = inputs
    Phase.spent.clear()
    with ExitStack() as ctx:
        def sb(name, shape, dt=F32):
            return ctx.enter_context(nc.sbuf_tensor(name, shape, dt))

        k.x_sb = sb("x_sb", [128, T, D])
        k.xn_sb = sb("xn_sb", [128, T, D])
        k.ident = sb("ident", [128, 128])
        k.below = sb("below", [128, VALS])
        k.tri = sb("tri", [128, 128], BF16)
        k.ones = sb("ones", [128, 128], BF16)
        k.onesf = sb("onesf", [128, 128])
        k.iota_i = sb("iota_i", [128, 256], I32)
        k.iota = sb("iota", [128, 256])
        k.cols = sb("cols", [128, VEC_ROWS])
        k.gate_b = sb("gate_b", [128, 16])
        k.bg = sb("bg", [128, 8])
        k.gamma = sb("gamma", [128, D])
        k.beta = sb("beta", [128, D])
        k.eps = sb("eps", [128, 1])
        k.eps5 = sb("eps5", [128, 1])
        k.node_a = sb("node_a", [128, T])
        k.block_start = sb("block_start", [128, NEB], I32)
        k.block_tile = sb("block_tile", [128, NEB], I32)
        k.block_node = sb("block_node", [128, NEB])

        def dram(name, shape, dt=F32):
            return nc.dram_tensor(name, shape, dt, kind="Internal").ap()

        k.xn_dram = dram("xn_dram", [N, D])
        k.recs = dram("recs", [E + EB, REC])
        k.out = out
        k.y_dram = dram("y_dram", [N, D])

        load_inputs(nc, k)
        first_norm(nc, k)
        sort_edges(nc, k)
        with nc.sbuf_tensor("agg0", [128, T, D], F32) as k.agg:
            sum_neighbours(nc, k)
            gin_mlp(nc, k)
        if stop <= 1:
            return
        with ExitStack() as held:
            m = Experts(nc, held, "ffn0", 16, 2, 512, True)
            route_first(nc, k, m)
            pick_slots(nc, k, m)
            send_rows(nc, k, m)
            run_experts(nc, k, m, k.L0_ffn_w1, k.L0_ffn_w2, FFN0_B1, ACT.Relu)
            combine(nc, k, m, k.L0_ffn_b2, norm=True)
        if stop <= 2:
            return
        edge_table(nc, k)
        with nc.sbuf_tensor("agg1", [128, T, 2 * D], F32) as k.agg:
            sum_messages(nc, k)
            update_nodes(nc, k)
        if stop <= 3:
            return
        with ExitStack() as held:
            m = Experts(nc, held, "ffn1", 8, 1, 1024, False)
            route_second(nc, k, m)
            pick_slots(nc, k, m)
            send_rows(nc, k, m)
            run_experts(nc, k, m, k.L1_ffn_W1, k.L1_ffn_Wd, FFN1_B1, ACT.Gelu)
            combine(nc, k, m, k.L1_ffn_bd, norm=False)


def kernel(**inputs):
    import numpy as _np
    import concourse.bacc as _bacc
    from concourse import mybir as _mybir
    from concourse.bass_utils import run_bass_kernel_spmd as _run

    nc = _bacc.Bacc("TRN2", target_bir_lowering=False, num_devices=1)
    arrays, aps = {}, []
    for name in _NAMES:
        a = _np.ascontiguousarray(inputs[name])
        arrays[f"in_{name}"] = a
        aps.append(nc.dram_tensor(f"in_{name}", a.shape, _mybir.dt.from_np(a.dtype), kind="ExternalInput").ap())
    out = nc.dram_tensor("out_0", (N, D), F32, kind="ExternalOutput").ap()
    build(nc, aps, out)
    r = _run(nc, [arrays], core_ids=[0])
    return r.results[0]["out_0"]
```

```python
from contextlib import ExitStack
import math

import concourse.bass as bass
from concourse import mybir

N, D = 3125, 256
E = 53125
P = 125
T = N // P
G = 5
NG = T // G
W = G * P
CUTS = [(0, 313), (313, W)]

EC = E // P
ER = 25
EG = EC // ER
REC = 16
DST, SRC = 12, 13
EB = 256
NEB = (E + T * (EB - 1)) // EB
SLOTS = 8
NEB = -(-NEB // SLOTS) * SLOTS

TOK = 128
EPS = 1e-5
MAGIC = 12582912.0
VALS = 128 * 6 + 800
OFF = 128 * 6

MUL = 64
INV_MUL = 1.0 / math.sqrt(MUL)
SILU_NORM = 1.679
C_S, C_X = math.sin(math.pi / 8.0), math.cos(math.pi / 8.0)

F32, BF16, I32, U32 = mybir.dt.float32, mybir.dt.bfloat16, mybir.dt.int32, mybir.dt.uint32
ALU, ACT, AX = mybir.AluOpType, mybir.ActivationFunctionType, mybir.AxisListType
ds = bass.ds

GNN_B1, GNN_B2, GNN_GAMMA, GNN_BETA, FFN0_B1, FFN1_B1 = 0, 4, 6, 8, 10, 74
VEC_ROWS = 82


class Kept:
    pass


class Phase:

    spent = []

    def __init__(self, nc, name):
        self.nc, self.name, self.ctx, self.taken = nc, name, ExitStack(), []

    def __enter__(self):
        self.ctx.__enter__()
        return self

    def __exit__(self, *what):
        self.ctx.__exit__(*what)
        self.spent += self.taken
        if what[0] is None and len(self.spent) > 70:
            self.nc.clear_and_free_semaphores(list(self.spent))
            self.nc.all_engine_barrier()
            self.spent.clear()

    def sb(self, name, shape, dt=F32):
        return self.ctx.enter_context(self.nc.sbuf_tensor(f"{self.name}_{name}", shape, dt))

    def ps(self, name, shape, dt=F32):
        return self.ctx.enter_context(self.nc.psum_tensor(f"{self.name}_ps_{name}", shape, dt))

    def sem(self, name):
        self.taken.append(self.nc.alloc_semaphore(f"{self.name}_{name}"))
        return self.taken[-1]

    def sems(self, name, n):
        return [self.sem(f"{name}{j}") for j in range(n)]


def load_inputs(nc, k):
    with Phase(nc, "load") as ph:
        rows = ph.sb("rows", [VEC_ROWS, 128])
        iota_i = ph.sb("iota_i", [128, N], I32)
        ps_cols = ph.ps("cols", [128, 128])
        loaded, zeroed, made = ph.sem("loaded"), ph.sem("zeroed"), ph.sem("made")
        cols_ready, copied = ph.sem("cols_ready"), ph.sem("copied")
        block = ph.ctx.enter_context(nc.Block())
        count = 0

        @block.sync
        def _(sp):
            nonlocal count

            def load(dst, src):
                nonlocal count
                sp.dma_start(dst, src).then_inc(loaded, 16)
                count += 16

            def vec(row, a):
                n = a.shape[-1] // 128 if len(a.shape) == 1 else a.shape[0] * a.shape[1] // 128
                src = a.rearrange("(r c) -> r c", c=128) if len(a.shape) == 1 else a.rearrange("e (r c) -> (e r) c", c=128)
                load(rows[row:row + n, :], src)

            vec(GNN_B1, k.L0_gnn_b1)
            vec(GNN_B2, k.L0_gnn_b2)
            vec(GNN_GAMMA, k.L0_gnn_gamma)
            vec(GNN_BETA, k.L0_gnn_beta)
            vec(FFN0_B1, k.L0_ffn_b1)
            vec(FFN1_B1, k.L1_ffn_b1)
            load(k.x_sb[0:P, :, :], k.x.rearrange("(t p) d -> p t d", p=P))
            load(k.gate_b[:, :], k.L0_ffn_gate_b.partition_broadcast(128))
            load(k.bg[:, :], k.L1_ffn_bg.partition_broadcast(128))
            load(k.gamma[:, :], k.L0_ffn_gamma.partition_broadcast(128))
            load(k.beta[:, :], k.L0_ffn_beta.partition_broadcast(128))
            load(k.eps[:, :], k.L0_gnn_eps.partition_broadcast(128))
            with nc.allow_non_contiguous_dma(reason="3125 single words, once"):
                load(k.node_a[0:P, :], k.node_vec1.rearrange("(t p) o -> p (t o)", p=P))
            sp.wait_ge(loaded, count)

        @block.gpsimd
        def _(pool):
            pool.memset(k.ident[:, :], 0.0).then_inc(zeroed, 1)
            pool.memset(k.below[:, :], 1.0).then_inc(zeroed, 1)
            pool.memset(k.tri[:, :], 1.0).then_inc(zeroed, 1)
            pool.memset(k.ones[:, :], 1.0).then_inc(made, 1)
            pool.memset(k.onesf[:, :], 1.0).then_inc(made, 1)
            pool.iota(iota_i[:, :], pattern=[[1, N]], base=0, channel_multiplier=0).then_inc(made, 1)
            pool.wait_ge(zeroed, 3)
            pool.affine_select(out=k.ident[:, :], in_=k.ident[:, :], compare_op=ALU.not_equal, fill=1.0, base=0,
                               pattern=[[-1, 128]], channel_multiplier=1).then_inc(made, 1)
            pool.affine_select(out=k.below[:, :], in_=k.below[:, :], compare_op=ALU.is_gt, fill=0.0, base=-OFF,
                               pattern=[[1, VALS]], channel_multiplier=-1).then_inc(made, 1)
            pool.affine_select(out=k.tri[:, :], in_=k.tri[:, :], compare_op=ALU.is_gt, fill=0.0, base=0,
                               pattern=[[1, 128]], channel_multiplier=-1).then_inc(made, 1)

        @block.tensor
        def _(pe):
            pe.wait_ge(loaded, count)
            pe.wait_ge(made, 6)
            pe.transpose(ps_cols[:, 0:VEC_ROWS], rows[:, :], k.ident[0:VEC_ROWS, 0:VEC_ROWS]).then_inc(cols_ready, 1)

        @block.vector
        def _(dve):
            dve.wait_ge(cols_ready, 1)
            dve.tensor_copy(k.cols[:, :], ps_cols[:, 0:VEC_ROWS]).then_inc(copied, 1)
            dve.wait_ge(made, 6)
            dve.tensor_copy(k.iota[:, :], iota_i[:, :]).then_inc(copied, 1)
            dve.wait_ge(loaded, count)
            dve.tensor_scalar(k.eps[:, :], k.eps[:, :], 1.0, None, ALU.add).then_inc(copied, 1)


def pass_on(eng, gate):
    eng.sem_inc(gate, 1)


class LayerNorm:

    def __init__(self, ph):
        self.stats, self.mv = ph.sb("ln_stats", [128, G, 6]), ph.sb("ln_mv", [128, G, 2])
        self.std, self.rstd = ph.sb("ln_std", [128, G]), ph.sb("ln_rstd", [128, G])
        self.stats_done, self.mv_done = ph.sem("ln_stats_done"), ph.sem("ln_mv_done")
        self.std_done, self.rstd_done = ph.sem("ln_std_done"), ph.sem("ln_rstd_done")
        self.out_done, self.gate = ph.sem("ln_out_done"), ph.sem("ln_gate")


def ln_vector(dve, ln, i, source, target):
    for j in range(G):
        dve.bn_stats(ln.stats[0:P, j, :], source(j)).then_inc(ln.stats_done, 1)
    dve.wait_ge(ln.stats_done, i * G + G)
    pass_on(dve, ln.gate)
    for j in range(G):
        dve.bn_aggr(ln.mv[0:P, j, :], ln.stats[0:P, j, :]).then_inc(ln.mv_done, 1)
    dve.wait_ge(ln.std_done, i + 1)
    dve.wait_ge(ln.mv_done, i * G + G)
    dve.reciprocal(ln.rstd[0:P, :], ln.std[0:P, :]).then_inc(ln.rstd_done, 1)
    dve.wait_ge(ln.rstd_done, i + 1)
    for j in range(G):
        dve.tensor_scalar(target(j), source(j), ln.mv[0:P, j, 0:1], ln.rstd[0:P, j:j + 1],
                          ALU.subtract, ALU.mult).then_inc(ln.out_done, 1)


def ln_scalar(act, k, ln, i):
    act.wait_ge(ln.mv_done, i * G + G)
    act.activation(ln.std[0:P, :], ln.mv[0:P, :, 1], ACT.Sqrt, bias=k.eps5[0:P, 0:1]).then_inc(ln.std_done, 1)


def first_norm(nc, k):
    with Phase(nc, "norm0") as ph:
        ln = LayerNorm(ph)
        stored, eps_made = ph.sem("stored"), ph.sem("eps_made")
        block = ph.ctx.enter_context(nc.Block())

        @block.vector
        def _(dve):
            dve.memset(k.eps5[:, :], EPS).then_inc(eps_made, 1)
            with dve.Fori(0, NG) as i:
                ln_vector(dve, ln, i, lambda j: k.x_sb[0:P, ds(i * G + j, 1), :].rearrange("p o d -> p (o d)"),
                          lambda j: k.xn_sb[0:P, ds(i * G + j, 1), :].rearrange("p o d -> p (o d)"))

        @block.scalar
        def _(act):
            act.wait_ge(eps_made, 1)
            with act.Fori(0, NG) as i:
                ln_scalar(act, k, ln, i)

        @block.sync
        def _(sp):
            sp.wait_ge(ln.out_done, T)
            sp.dma_start(k.xn_dram.rearrange("(t p) d -> p t d", p=P), k.xn_sb[0:P, :, :]).then_inc(stored, 16)
            sp.wait_ge(stored, 16)


def sort_edges(nc, k):
    with ExitStack() as held:
        def sb(name, shape, dt=F32):
            return held.enter_context(nc.sbuf_tensor(f"edges_{name}", shape, dt))

        e = Kept()
        e.rec = sb("rec", [128, EC, REC])
        e.onehot = sb("onehot", [128, ER, T, EG], BF16)
        e.cum = sb("cum", [128, ER + 1, T * EG], BF16)
        e.base = sb("base", [128, T * EG])
        e.unsorted = sb("unsorted", [128, 1], I32)
        count_edges(nc, k, e)
        place_edges(nc, k, e)


def count_edges(nc, k, e):
    BG = T * EG
    chunks = [(c, min(128, BG - c)) for c in range(0, BG, 128)]
    with Phase(nc, "count") as ph:
        dst_i, next_i, src_i = ph.sb("dst_i", [128, EC], I32), ph.sb("next_i", [128, EC], I32), ph.sb("src_i", [128, EC], I32)
        ea4, ea8 = ph.sb("ea4", [128, EC, 4]), ph.sb("ea8", [128, EC, 8])
        dst_f, next_f = ph.sb("dst_f", [128, EC]), ph.sb("next_f", [128, EC])
        tile_y, tile_f = ph.sb("tile_y", [128, EC]), ph.sb("tile_f", [128, EC])
        falls = ph.sb("falls", [128, 1])
        totals = ph.sb("totals", [128, len(chunks)])
        totals_b = ph.sb("totals_b", [128, len(chunks), 128])
        ps_tot = ph.ps("tot", [128, len(chunks)])
        ps_base = ph.ps("base", [128, BG])
        ps_falls = ph.ps("falls", [128, 1])

        dst_in, next_in, other_in = ph.sem("dst_in"), ph.sem("next_in"), ph.sem("other_in")
        step = ph.sem("step")
        next_set, falls_made, falls_sum = ph.sem("next_set"), ph.sem("falls_made"), ph.sem("falls_sum")
        cum_ready, tot_ready, totb_ready, base_ready = (ph.sem(f"{x}_ready") for x in ("cum", "tot", "totb", "base"))
        fields = ph.sem("fields")
        block = ph.ctx.enter_context(nc.Block())

        @block.sync
        def _(sp):
            sp.dma_start(dst_i[0:P, :], k.dst.rearrange("(p c) -> p c", p=P)).then_inc(dst_in, 16)
            sp.wait_ge(next_set, 1)
            last = (P - 1) * EC
            sp.dma_start(next_i[0:P - 1, :], k.dst[1:last + 1].rearrange("(p c) -> p c", c=EC)).then_inc(next_in, 16)
            sp.dma_start(next_i[P - 1:P, 0:EC - 1], k.dst[last + 1:E].rearrange("(p c) -> p c", p=1)).then_inc(next_in, 16)

        @block.scalar
        def _(act):
            act.dma_start(src_i[0:P, :], k.src.rearrange("(p c) -> p c", p=P)).then_inc(other_in, 16)
            act.dma_start(ea4[0:P, :, :], k.edge_attr_4.rearrange("(p c) w -> p c w", p=P)).then_inc(other_in, 16)
            act.dma_start(ea8[0:P, :, :], k.edge_attr_8.rearrange("(p c) w -> p c w", p=P)).then_inc(other_in, 16)
            act.wait_ge(other_in, 48)
            act.activation(e.rec[0:P, :, 0:8], ea8[0:P, :, :], ACT.Copy).then_inc(fields, 1)
            act.activation(e.rec[0:P, :, 8:12], ea4[0:P, :, :], ACT.Copy).then_inc(fields, 1)

        @block.gpsimd
        def _(pool):
            pool.memset(next_i[:, :], N).then_inc(next_set, 1)
            pool.memset(e.rec[0:P, :, SRC + 1:REC], 0.0).then_inc(fields, 1)

        @block.tensor
        def _(pe):
            pe.wait_ge(falls_made, 1)
            pe.matmul(ps_falls[:, :], k.onesf[0:P, :], falls[0:P, :], start=True, stop=True).then_inc(falls_sum, 1)
            pe.wait_ge(cum_ready, 1)
            for c, (at, n) in enumerate(chunks):
                last = pe.matmul(ps_tot[0:n, c:c + 1], e.cum[0:P, ER, at:at + n], k.ones[0:P, 0:1], start=True, stop=True)
            last.then_inc(tot_ready, 1)
            pe.wait_ge(totb_ready, len(chunks))
            for c, (at, n) in enumerate(chunks):
                last = pe.matmul(ps_base[:, :], totals_b[0:n, c, :], k.below[0:n, OFF - at:OFF - at + BG],
                                 start=(c == 0), stop=(c == len(chunks) - 1))
            last.then_inc(base_ready, 1)

        @block.vector
        def _(dve):
            done = [0]

            def chain(ins):
                done[0] += 1
                ins.then_inc(step, 1)
                dve.wait_ge(step, done[0])

            dve.wait_ge(dst_in, 16)
            chain(dve.tensor_copy(dst_f[0:P, :], dst_i[0:P, :]))
            chain(dve.tensor_scalar(tile_y[0:P, :], dst_f[0:P, :], 1.0 / P, 0.5 / P - 0.5, ALU.mult, ALU.add))
            chain(dve.tensor_scalar(tile_f[0:P, :], tile_y[0:P, :], MAGIC, None, ALU.add))
            chain(dve.tensor_scalar(tile_f[0:P, :], tile_f[0:P, :], MAGIC, None, ALU.subtract))
            view = tile_f[0:P, :].rearrange("p (g r) -> p r g", r=ER)
            chain(dve.memset(e.cum[0:P, 0, :], 0.0))
            for r in range(ER):
                dve.tensor_tensor(e.onehot[0:P, r, :, :], view[:, r, :].unsqueeze(1).to_broadcast([P, T, EG]),
                                  k.iota[0:P, 0:T].unsqueeze(2).to_broadcast([P, T, EG]), ALU.is_equal).then_inc(step, 1)
            done[0] += ER
            dve.wait_ge(next_in, 32)
            chain(dve.tensor_copy(next_f[0:P, :], next_i[0:P, :]))
            chain(dve.tensor_tensor(next_f[0:P, :], dst_f[0:P, :], next_f[0:P, :], ALU.is_gt))
            dve.tensor_reduce(falls[0:P, :], next_f[0:P, :], AX.X, ALU.add).then_inc(falls_made, 1)
            for r in range(ER):
                chain(dve.tensor_tensor(e.cum[0:P, r + 1, :], e.cum[0:P, r, :],
                                        e.onehot[0:P, r, :, :].rearrange("p t g -> p (t g)"), ALU.add))
            dve.sem_inc(cum_ready, 1)
            dve.wait_ge(falls_sum, 1)
            dve.tensor_copy(e.unsorted[:, :], ps_falls[:, :])
            dve.wait_ge(tot_ready, 1)
            for c, (at, n) in enumerate(chunks):
                chain(dve.tensor_copy(totals[0:n, c:c + 1], ps_tot[0:n, c:c + 1]))
                dve.tensor_copy(totals_b[0:n, c, :], totals[0:n, c:c + 1].to_broadcast([n, 128])).then_inc(totb_ready, 1)
            dve.tensor_copy(e.rec[0:P, :, DST], dst_f[0:P, :]).then_inc(fields, 1)
            dve.wait_ge(other_in, 48)
            dve.tensor_copy(e.rec[0:P, :, SRC].bitcast(I32), src_i[0:P, :]).then_inc(fields, 1)
            dve.wait_ge(base_ready, 1)
            dve.tensor_copy(e.base[:, :], ps_base[:, :])


def place_edges(nc, k, e):
    BG = T * EG
    with Phase(nc, "place") as ph:
        tail = ph.sb("tail", [128, 2 * REC])
        sel = ph.sb("sel", [128, 2, BG])
        pos_f, pos_i = ph.sb("pos_f", [128, EG, ER]), ph.sb("pos_i", [128, EC], I32)
        row_st, idx_st = ph.sb("row_st", [128, G, REC]), ph.sb("idx_st", [128, G], I32)
        start_b, count_b = ph.sb("start_b", [128, T + 1]), ph.sb("count_b", [128, T])
        blk_y, blk_n = ph.sb("blk_y", [128, T]), ph.sb("blk_n", [128, T])
        blk_end = ph.sb("blk_end", [128, 2, T])
        shift, dshift = ph.sb("shift", [128, T]), ph.sb("dshift", [128, T])
        cmp = ph.sb("cmp", [128, NEB, T])
        blk_f, blk_s, blk_t = ph.sb("blk_f", [128, NEB]), ph.sb("blk_s", [128, NEB]), ph.sb("blk_t", [128, NEB])
        blk_c = ph.sb("blk_c", [128, NEB])
        ps_rank = [ph.ps(f"rank{s}", [128, BG]) for s in range(2)]
        step, rank_step = ph.sem("step"), ph.sem("rank_step")
        rank_ready, rank_read, staged = ph.sem("rank_ready"), ph.sem("rank_read"), ph.sem("staged")
        scattered = ph.sems("scattered", G)
        tail_made, stored, tail_stored, gate = ph.sem("tail_made"), ph.sem("stored"), ph.sem("tail_stored"), ph.sem("gate")
        block = ph.ctx.enter_context(nc.Block())

        @block.sync
        def _(sp):
            unsorted = sp.value_load(e.unsorted[0:1, 0:1], min_val=0, max_val=E)
            with sp.If(unsorted == 0):
                sp.dma_start(k.recs[0:E, :].rearrange("(p c) w -> p c w", p=P), e.rec[0:P, :, :]).then_inc(stored, 16)
                sp.wait_ge(stored, 16)
            sp.wait_ge(tail_made, 2)
            sp.dma_start(k.recs[E:E + EB, :].rearrange("(p u) w -> p (u w)", u=2), tail[:, :]).then_inc(tail_stored, 16)
            sp.wait_ge(tail_stored, 16)

        @block.tensor
        def _(pe):
            unsorted = pe.value_load(e.unsorted[0:1, 0:1], min_val=0, max_val=E)
            with pe.If(unsorted != 0):
                for r in range(ER):
                    if r >= 2:
                        pe.wait_ge(rank_read, r - 1)
                    pe.matmul(ps_rank[r % 2][0:P, :], k.onesf[0:1, 0:P], e.base[0:1, :], start=True, stop=False)
                    pe.matmul(ps_rank[r % 2][0:P, :], k.tri[0:P, 0:P], e.onehot[0:P, r, :, :].rearrange("p t g -> p (t g)"),
                              start=False, stop=False)
                    pe.matmul(ps_rank[r % 2][0:P, :], k.ones[0:P, 0:P], e.cum[0:P, r, :], start=False,
                              stop=True).then_inc(rank_ready, 1)

        @block.gpsimd
        def _(pool):
            pool.memset(tail[:, :], 0.0).then_inc(tail_made, 1)
            pool.wait_ge(tail_made, 1)
            pool.memset(tail[:, :].rearrange("p (u w) -> p u w", w=REC)[:, :, DST], -1.0).then_inc(tail_made, 1)
            unsorted = pool.value_load(e.unsorted[0:1, 0:1], min_val=0, max_val=E)
            with pool.If(unsorted != 0):
                with pool.Fori(0, EC // G) as i:
                    for j in range(G):
                        pool.wait_ge(staged, i * 2 * G + 2 * j + 2)
                        pass_on(pool, gate)
                        pool.indirect_dma_start(k.recs, bass.IndirectOffsetOnAxis(ap=idx_st[0:P, j:j + 1].bitcast(U32), axis=0),
                                                row_st[0:P, j, :], None).then_inc(scattered[j], 16)
                for j in range(G):
                    pool.wait_ge(scattered[j], (EC // G) * 16)

        @block.vector
        def _(dve):
            unsorted = dve.value_load(e.unsorted[0:1, 0:1], min_val=0, max_val=E)
            with dve.If(unsorted != 0):
                for r in range(ER):
                    dve.wait_ge(rank_ready, r + 1)
                    s = sel[0:P, r % 2, :]
                    dve.tensor_tensor(s, ps_rank[r % 2][0:P, :], e.onehot[0:P, r, :, :].rearrange("p t g -> p (t g)"), ALU.mult)\
                       .then_inc(rank_read, 1)
                    dve.wait_ge(rank_read, r + 1)
                    dve.tensor_reduce(pos_f[0:P, :, r], s.rearrange("p (t g) -> p g t", g=EG), AX.X, ALU.add).then_inc(rank_step, 1)
                dve.wait_ge(rank_step, ER)
                dve.tensor_copy(pos_i[0:P, :], pos_f[0:P, :, :].rearrange("p g r -> p (g r)")).then_inc(rank_step, 1)
                dve.wait_ge(rank_step, ER + 1)

                def stage(i, first=False):
                    for j in range(G):
                        if not first:
                            dve.wait_ge(scattered[j], i * 16)
                            pass_on(dve, gate)
                        dve.tensor_copy(row_st[0:P, j, :], row(e.rec, i * G + j)).then_inc(staged, 1)
                        dve.tensor_copy(idx_st[0:P, j:j + 1], pos_i[0:P, ds(i * G + j, 1)]).then_inc(staged, 1)

                stage(0, first=True)
                with dve.Fori(1, EC // G) as i:
                    stage(i)

            done = [0]

            def chain(ins):
                done[0] += 1
                ins.then_inc(step, 1)
                dve.wait_ge(step, done[0])

            first = e.base[:, :].rearrange("p (t g) -> p t g", g=EG)[:, :, 0]
            chain(dve.tensor_copy(start_b[:, 0:T], first))
            chain(dve.memset(start_b[:, T:T + 1], float(E)))
            chain(dve.tensor_tensor(count_b[:, :], start_b[:, 1:T + 1], start_b[:, 0:T], ALU.subtract))
            chain(dve.tensor_scalar(blk_y[:, :], count_b[:, :], 1.0 / EB, (EB - 1) / EB - 0.5 + 0.5 / EB, ALU.mult, ALU.add))
            chain(dve.tensor_scalar(blk_y[:, :], blk_y[:, :], MAGIC, None, ALU.add))
            chain(dve.tensor_scalar(blk_n[:, :], blk_y[:, :], MAGIC, None, ALU.subtract))
            chain(dve.tensor_copy(blk_end[:, 0, :], blk_n[:, :]))
            side, gap = 0, 1
            while gap < T:
                chain(dve.tensor_copy(blk_end[:, 1 - side, 0:gap], blk_end[:, side, 0:gap]))
                chain(dve.tensor_tensor(blk_end[:, 1 - side, gap:T], blk_end[:, side, gap:T], blk_end[:, side, 0:T - gap], ALU.add))
                side, gap = 1 - side, 2 * gap
            end = blk_end[:, side, :]
            chain(dve.tensor_tensor(shift[:, :], end, blk_n[:, :], ALU.subtract))
            chain(dve.scalar_tensor_tensor(shift[:, :], shift[:, :], float(-EB), start_b[:, 0:T], ALU.mult, ALU.add))
            chain(dve.memset(dshift[:, :], 0.0))
            chain(dve.tensor_tensor(dshift[:, 0:T - 1], shift[:, 1:T], shift[:, 0:T - 1], ALU.subtract))
            chain(dve.tensor_tensor(cmp[:, :, :], k.iota[:, 0:NEB].unsqueeze(2).to_broadcast([128, NEB, T]),
                                    end.unsqueeze(1).to_broadcast([128, NEB, T]), ALU.is_ge))
            chain(dve.tensor_reduce(blk_f[:, :], cmp[:, :, :], AX.X, ALU.add))
            chain(dve.tensor_tensor(cmp[:, :, :], cmp[:, :, :], dshift[:, :].unsqueeze(1).to_broadcast([128, NEB, T]), ALU.mult))
            chain(dve.tensor_reduce(blk_s[:, :], cmp[:, :, :], AX.X, ALU.add))
            chain(dve.scalar_tensor_tensor(blk_t[:, :], k.iota[:, 0:NEB], float(EB), blk_s[:, :], ALU.mult, ALU.add))
            chain(dve.tensor_scalar(blk_t[:, :], blk_t[:, :], float(E), None, ALU.min))
            chain(dve.tensor_copy(k.block_start[:, :], blk_t[:, :]))
            chain(dve.tensor_scalar(blk_c[:, :], blk_f[:, :], float(T - 1), None, ALU.min))
            chain(dve.tensor_copy(k.block_tile[:, :], blk_c[:, :]))


def row(buf, at, lo=0, hi=None, parts=P):
    return buf[0:parts, ds(at, 1), lo:hi].rearrange("p o d -> p (o d)")


def node_ids(k, tile):
    return k.iota[:, ds(tile * P, P)].unsqueeze(1).to_broadcast([128, 2, P])


def sum_neighbours(nc, k):
    with Phase(nc, "sum") as ph:
        rec = [ph.sb(f"rec{s}", [128, 2, REC]) for s in range(SLOTS)]
        got = [[ph.sb(f"got{s}{u}", [128, D]) for u in range(2)] for s in range(SLOTS)]
        onehot = [ph.sb(f"onehot{s}", [128, 2, P]) for s in range(SLOTS)]
        ps_sum = [ph.ps(f"sum{s}", [128, D]) for s in range(SLOTS)]
        rec_in, got_in = ph.sems("rec_in", SLOTS), ph.sems("got_in", SLOTS)
        summed, added = ph.sem("summed"), ph.sem("added")
        masked, gate = ph.sem("masked"), ph.sem("gate")
        block = ph.ctx.enter_context(nc.Block())

        @block.sync
        def _(sp):
            sp.sem_inc(summed, SLOTS)
            with sp.Fori(0, NEB // SLOTS) as i:
                for s in range(SLOTS):
                    n = i * SLOTS + s
                    start = sp.value_load(k.block_start[0:1, ds(n, 1)], min_val=0, max_val=E)
                    sp.wait_ge(summed, n + 1)
                    pass_on(sp, gate)
                    sp.dma_start(rec[s][:, :, :], k.recs[ds(start, EB), :].rearrange("(p u) w -> p u w", u=2))\
                      .then_inc(rec_in[s], 16)

        @block.gpsimd
        def _(pool):
            with pool.Fori(0, NEB // SLOTS) as i:
                for s in range(SLOTS):
                    pool.wait_ge(rec_in[s], i * 16 + 16)
                    pass_on(pool, gate)
                    for u in range(2):
                        pool.indirect_dma_start(
                            got[s][u][:, :], None, k.xn_dram,
                            bass.IndirectOffsetOnAxis(ap=rec[s][:, u, SRC:SRC + 1].bitcast(U32), axis=0)).then_inc(got_in[s], 16)

        @block.tensor
        def _(pe):
            with pe.Fori(0, NEB // SLOTS) as i:
                for s in range(SLOTS):
                    n = i * SLOTS + s
                    pe.wait_ge(added, n + 1)
                    pe.wait_ge(masked, n + 1)
                    pe.wait_ge(got_in[s], i * 32 + 32)
                    for u in range(2):
                        last = pe.matmul(ps_sum[s][0:P, :], onehot[s][:, u, :], got[s][u][:, :], start=(u == 0), stop=(u == 1))
                    last.then_inc(summed, 1)

        @block.vector
        def _(dve):
            dve.memset(k.agg[:, :, 0:D], 0.0).then_inc(added, SLOTS)

            def tile_of(n):
                return dve.value_load(k.block_tile[0:1, ds(n, 1)], min_val=0, max_val=T - 1)

            def add_sum(n, s, tile):
                dve.wait_ge(summed, n + 1 + SLOTS)
                dve.wait_ge(added, n + SLOTS)
                dve.tensor_tensor(row(k.agg, tile, 0, D), ps_sum[s][0:P, :], row(k.agg, tile, 0, D), ALU.add)\
                   .then_inc(added, 1)

            def turn(i, first=False):
                tile_before = None if first else tile_of(i * SLOTS - 1)
                for s in range(SLOTS):
                    n = i * SLOTS + s
                    tile = tile_of(n)
                    dve.wait_ge(rec_in[s], i * 16 + 16)
                    dve.tensor_tensor(onehot[s][:, :, :], node_ids(k, tile), rec[s][:, :, DST:DST + 1].to_broadcast([128, 2, P]),
                                      ALU.is_equal).then_inc(masked, 1)
                    if not first or s >= 1:
                        add_sum(n - 1, (s - 1) % SLOTS, tile_before)
                    tile_before = tile

            turn(0, first=True)
            with dve.Fori(1, NEB // SLOTS) as i:
                turn(i)
            add_sum(NEB - 1, SLOTS - 1, tile_of(NEB - 1))


def gin_mlp(nc, k):
    HID = 512
    HC = HID // 128
    with Phase(nc, "gin") as ph:
        w1, w2 = ph.sb("w1", [128, 2, HID]), ph.sb("w2", [128, HC, D])
        h = ph.sb("h", [128, G, D])
        h_t = ph.sb("h_t", [128, 2, W])
        hid = ph.sb("hid", [128, HC, W])
        h2 = ph.sb("h2", [128, 2, NG, W])
        stats = ph.sb("stats", [128, 2, 2 * NG, 6])
        mv, std, rstd = ph.sb("mv", [128, 2, 2]), ph.sb("std", [128, 2]), ph.sb("rstd", [128, 2])
        scale, shift = ph.sb("scale", [128, 2]), ph.sb("shift", [128, 2])
        bn = ph.sb("bn", [128, 2, W])
        ps_t = [ph.ps(f"t{s}", [128, 2, 128]) for s in range(2)]
        ps_h = [ph.ps(f"h{s}", [128, 512]) for s in range(4)]
        w_in = ph.sem("w_in")
        h_made, turned, kept = ph.sem("h_made"), ph.sem("turned"), ph.sem("kept")
        hid_sum, hid_made, out_sum, out_made = ph.sem("hid_sum"), ph.sem("hid_made"), ph.sem("out_sum"), ph.sem("out_made")
        step, bn_std = ph.sem("step"), ph.sem("bn_std")
        bn_made, bn_turned, x_made, gate = ph.sem("bn_made"), ph.sem("bn_turned"), ph.sem("x_made"), ph.sem("gate")
        block = ph.ctx.enter_context(nc.Block())

        @block.sync
        def _(sp):
            sp.dma_start(w1[:, :, :], k.L0_gnn_W1.rearrange("(c p) h -> p c h", p=128)).then_inc(w_in, 16)
            sp.dma_start(w2[:, :, :], k.L0_gnn_W2.rearrange("(c p) h -> p c h", p=128)).then_inc(w_in, 16)

        @block.vector
        def _(dve):
            dve.sem_inc(turned, G)
            with dve.Fori(0, NG) as i:
                for j in range(G):
                    dve.wait_ge(turned, i * G + j + 1)
                    pass_on(dve, gate)
                    dve.scalar_tensor_tensor(h[0:P, j, :], row(k.xn_sb, i * G + j), k.eps[0:P, 0:1], row(k.agg, i * G + j, 0, D),
                                             ALU.mult, ALU.add).then_inc(h_made, 1)
                for c, (a, b) in enumerate(CUTS):
                    for m in range(2):
                        dve.wait_ge(out_made, i * 4 + 2 * c + m + 1)
                        pass_on(dve, gate)
                        dve.bn_stats(stats[:, m, ds(i * 2 + c, 1), :].rearrange("p o w -> p (o w)"),
                                     h2[:, m, ds(i, 1), a:b].rearrange("p o w -> p (o w)")).then_inc(step, 1)
            done = [4 * NG]

            def chain(ins):
                done[0] += 1
                ins.then_inc(step, 1)
                dve.wait_ge(step, done[0])

            dve.wait_ge(step, done[0])
            for m in range(2):
                chain(dve.bn_aggr(mv[:, m, :], stats[:, m, :, :].rearrange("p n w -> p (n w)")))
            dve.wait_ge(bn_std, 1)
            chain(dve.reciprocal(rstd[:, :], std[:, :]))
            chain(dve.tensor_tensor(scale[:, :], rstd[:, :], k.cols[:, GNN_GAMMA:GNN_GAMMA + 2], ALU.mult))
            chain(dve.tensor_tensor(shift[:, :], mv[:, :, 0], scale[:, :], ALU.mult))
            chain(dve.tensor_tensor(shift[:, :], k.cols[:, GNN_BETA:GNN_BETA + 2], shift[:, :], ALU.subtract))
            with dve.Fori(0, NG) as i:
                for m in range(2):
                    dve.wait_ge(bn_turned, i * G + 1)
                    pass_on(dve, gate)
                    dve.tensor_scalar(bn[:, m, :], h2[:, m, ds(i, 1), :].rearrange("p o w -> p (o w)"), scale[:, m:m + 1],
                                      shift[:, m:m + 1], ALU.mult, ALU.add).then_inc(bn_made, 1)
                for j in range(G):
                    dve.wait_ge(bn_turned, i * G + j + 2)
                    pass_on(dve, gate)
                    dve.tensor_tensor(row(k.x_sb, i * G + j), ps_t[j % 2][0:P, :, :].rearrange("p m w -> p (m w)"),
                                      row(k.x_sb, i * G + j), ALU.add).then_inc(x_made, 1)

        @block.scalar
        def _(act):
            with act.Fori(0, NG) as i:
                for j in range(G):
                    act.wait_ge(turned, i * G + j + 1 + G)
                    act.wait_ge(hid_sum, i * 2 * HC + 1)
                    pass_on(act, gate)
                    act.activation(h_t[:, :, j * P:(j + 1) * P], ps_t[j % 2][:, :, 0:P], ACT.Copy).then_inc(kept, 1)
                for c, (a, b) in enumerate(CUTS):
                    for m in range(HC):
                        act.wait_ge(hid_sum, i * 2 * HC + c * HC + m + 2)
                        act.wait_ge(out_sum, i * 4 + 1)
                        pass_on(act, gate)
                        act.activation(hid[:, m, a:b], ps_h[(c * HC + m) % 4][:, 0:b - a], ACT.Relu,
                                       bias=k.cols[:, GNN_B1 + m:GNN_B1 + m + 1]).then_inc(hid_made, 1)
                for c, (a, b) in enumerate(CUTS):
                    for m in range(2):
                        act.wait_ge(out_sum, i * 4 + 2 * c + m + 2)
                        pass_on(act, gate)
                        act.activation(h2[:, m, ds(i, 1), a:b].rearrange("p o w -> p (o w)"), ps_h[2 * c + m][:, 0:b - a],
                                       ACT.Identity, bias=k.cols[:, GNN_B2 + m:GNN_B2 + m + 1]).then_inc(out_made, 1)
            act.wait_ge(step, 4 * NG + 2)
            act.activation(std[:, :], mv[:, :, 1], ACT.Sqrt, bias=k.eps5[:, 0:1]).then_inc(bn_std, 1)

        @block.tensor
        def _(pe):
            pe.wait_ge(w_in, 32)
            pe.sem_inc(hid_sum, 1)
            pe.sem_inc(out_sum, 1)
            pe.sem_inc(bn_turned, 1)
            pe.sem_inc(kept, 2)
            pe.sem_inc(x_made, 2)
            with pe.Fori(0, NG) as i:
                for j in range(G):
                    pe.wait_ge(h_made, i * G + j + 1)
                    pe.wait_ge(kept, i * G + j + 1)
                    for m in range(2):
                        last = pe.transpose(ps_t[j % 2][:, m, 0:P], h[0:P, j, m * 128:(m + 1) * 128], k.ident[0:P, 0:P])
                    last.then_inc(turned, 1)
                pe.wait_ge(kept, i * G + G + 2)
                for c, (a, b) in enumerate(CUTS):
                    for m in range(HC):
                        n = c * HC + m
                        if c:
                            pe.wait_ge(hid_made, i * 2 * HC + n - 3)
                        for q in range(2):
                            last = pe.matmul(ps_h[n % 4][:, 0:b - a], w1[:, q, m * 128:(m + 1) * 128], h_t[:, q, a:b],
                                             start=(q == 0), stop=(q == 1))
                        last.then_inc(hid_sum, 1)
                for c, (a, b) in enumerate(CUTS):
                    for m in range(2):
                        pe.wait_ge(hid_made, i * 2 * HC + 2 * HC)
                        for q in range(HC):
                            last = pe.matmul(ps_h[2 * c + m][:, 0:b - a], w2[:, q, m * 128:(m + 1) * 128], hid[:, q, a:b],
                                             start=(q == 0), stop=(q == HC - 1))
                        last.then_inc(out_sum, 1)
                pe.wait_ge(out_made, i * 4 + 4)
            with pe.Fori(0, NG) as i:
                pe.wait_ge(bn_made, i * 2 + 2)
                for j in range(G):
                    pe.wait_ge(x_made, i * G + j + 1)
                    for m in range(2):
                        last = pe.transpose(ps_t[j % 2][0:P, m, :], bn[:, m, j * P:(j + 1) * P], k.ident[:, :])
                    last.then_inc(bn_turned, 1)


class Experts:

    def __init__(self, nc, ctx, name, n, picks, hid, own_w1):
        self.name, self.n, self.picks, self.hid, self.own_w1 = name, n, picks, hid, own_w1
        self.cols = T * picks
        self.blocks = (N * picks + n * (TOK - 1)) // TOK
        self.blocks += -self.blocks % 4

        def sb(what, shape, dt=F32):
            return ctx.enter_context(nc.sbuf_tensor(f"{name}_{what}", shape, dt))

        self.onehot = sb("onehot", [128, n, self.cols], BF16)
        self.prob = sb("prob", [128, self.cols])
        self.slot_i = sb("slot_i", [128, self.cols], I32)
        self.block_expert = sb("block_expert", [128, self.blocks], I32)
        self.rows = nc.dram_tensor(f"{name}_rows", [self.blocks * TOK, D], F32, kind="Internal").ap()
        self.results = nc.dram_tensor(f"{name}_results", [self.blocks * TOK, D], F32, kind="Internal").ap()


def pick_slots(nc, k, m):
    n, cols = m.n, m.cols
    width = n * cols
    cuts = [(a, min(a + 400, width)) for a in range(0, width, 400)]
    chunks = [(c, min(128, width - c)) for c in range(0, width, 128)]
    with Phase(nc, f"{m.name}_slots") as ph:
        totals = ph.sb("totals", [128, len(chunks)])
        totals_b = ph.sb("totals_b", [128, len(chunks), 128])
        base, rank = ph.sb("base", [128, n, cols]), ph.sb("rank", [128, n, cols])
        start_e, count_e = ph.sb("start_e", [128, n + 1]), ph.sb("count_e", [128, n])
        blk_n, blk_end = ph.sb("blk_n", [128, n]), ph.sb("blk_end", [128, 2, n])
        pad = ph.sb("pad", [128, n])
        cmp, blk_f = ph.sb("cmp", [128, m.blocks, n]), ph.sb("blk_f", [128, m.blocks])
        slot_f = ph.sb("slot_f", [128, cols])
        zeros = ph.sb("zeros", [128, 4, D])
        ps_tot = ph.ps("tot", [128, len(chunks)])
        ps_base = [ph.ps(f"base{c}", [128, 400]) for c in range(len(cuts))]
        ps_rank = [ph.ps(f"rank{c}", [128, 400]) for c in range(len(cuts))]
        tot_ready, totb_ready, base_ready, rank_ready = (ph.sem(f"{x}_ready") for x in ("tot", "totb", "base", "rank"))
        step, zero_made, zero_stored = ph.sem("step"), ph.sem("zero_made"), ph.sem("zero_stored")
        block = ph.ctx.enter_context(nc.Block())
        flat = m.onehot[:, :, :].rearrange("p e c -> p (e c)")

        @block.gpsimd
        def _(pool):
            pool.memset(zeros[:, :, :], 0.0).then_inc(zero_made, 1)

        @block.sync
        def _(sp):
            sp.wait_ge(zero_made, 1)
            for at in range(0, m.blocks, 4):
                c = min(4, m.blocks - at)
                sp.dma_start(m.rows[at * TOK:(at + c) * TOK, :].rearrange("(p c) d -> p c d", c=c),
                             zeros[:, 0:c, :]).then_inc(zero_stored, 16)
            sp.wait_ge(zero_stored, 16 * -(-m.blocks // 4))

        @block.tensor
        def _(pe):
            for c, (at, w) in enumerate(chunks):
                last = pe.matmul(ps_tot[0:w, c:c + 1], flat[0:P, at:at + w], k.ones[0:P, 0:1], start=True, stop=True)
            last.then_inc(tot_ready, 1)
            for c, (a, b) in enumerate(cuts):
                last = pe.matmul(ps_rank[c][0:P, 0:b - a], k.tri[0:P, 0:P], flat[0:P, a:b], start=True, stop=True)
            last.then_inc(rank_ready, 1)
            pe.wait_ge(totb_ready, len(chunks))
            for c, (a, b) in enumerate(cuts):
                for q, (at, w) in enumerate(chunks):
                    last = pe.matmul(ps_base[c][:, 0:b - a], totals_b[0:w, q, :], k.below[0:w, OFF - at + a:OFF - at + b],
                                     start=(q == 0), stop=(q == len(chunks) - 1))
            last.then_inc(base_ready, 1)

        @block.vector
        def _(dve):
            done = [0]

            def chain(ins):
                done[0] += 1
                ins.then_inc(step, 1)
                dve.wait_ge(step, done[0])

            dve.wait_ge(tot_ready, 1)
            for c, (at, w) in enumerate(chunks):
                chain(dve.tensor_copy(totals[0:w, c:c + 1], ps_tot[0:w, c:c + 1]))
                dve.tensor_copy(totals_b[0:w, c, :], totals[0:w, c:c + 1].to_broadcast([w, 128])).then_inc(totb_ready, 1)
            dve.wait_ge(base_ready, 1)
            flat_base, flat_rank = (x[:, :, :].rearrange("p e c -> p (e c)") for x in (base, rank))
            for c, (a, b) in enumerate(cuts):
                chain(dve.tensor_copy(flat_base[:, a:b], ps_base[c][:, 0:b - a]))
            chain(dve.tensor_copy(start_e[:, 0:n], base[:, :, 0]))
            chain(dve.memset(start_e[:, n:n + 1], float(N * m.picks)))
            chain(dve.tensor_tensor(count_e[:, :], start_e[:, 1:n + 1], start_e[:, 0:n], ALU.subtract))
            chain(dve.tensor_scalar(blk_n[:, :], count_e[:, :], 1.0 / TOK, (TOK - 1) / TOK - 0.5 + 0.5 / TOK, ALU.mult, ALU.add))
            chain(dve.tensor_scalar(blk_n[:, :], blk_n[:, :], MAGIC, None, ALU.add))
            chain(dve.tensor_scalar(blk_n[:, :], blk_n[:, :], MAGIC, None, ALU.subtract))
            chain(dve.tensor_copy(blk_end[:, 0, :], blk_n[:, :]))
            side, gap = 0, 1
            while gap < n:
                chain(dve.tensor_copy(blk_end[:, 1 - side, 0:gap], blk_end[:, side, 0:gap]))
                chain(dve.tensor_tensor(blk_end[:, 1 - side, gap:n], blk_end[:, side, gap:n], blk_end[:, side, 0:n - gap], ALU.add))
                side, gap = 1 - side, 2 * gap
            end = blk_end[:, side, :]
            chain(dve.tensor_tensor(pad[:, :], end, blk_n[:, :], ALU.subtract))
            chain(dve.scalar_tensor_tensor(pad[:, :], pad[:, :], float(TOK), start_e[:, 0:n], ALU.mult, ALU.subtract))
            chain(dve.tensor_tensor(base[:, :, :], base[:, :, :], pad[:, :].unsqueeze(2).to_broadcast([128, n, cols]), ALU.add))
            dve.wait_ge(rank_ready, 1)
            for c, (a, b) in enumerate(cuts):
                chain(dve.tensor_tensor(flat_rank[0:P, a:b], ps_rank[c][0:P, 0:b - a], flat_base[0:P, a:b], ALU.add))
            chain(dve.tensor_tensor(flat_rank[0:P, :], flat_rank[0:P, :], flat[0:P, :], ALU.mult))
            chain(dve.tensor_reduce(slot_f[0:P, :], rank[0:P, :, :].rearrange("p e c -> p c e"), AX.X, ALU.add))
            chain(dve.tensor_copy(m.slot_i[0:P, :], slot_f[0:P, :]))
            chain(dve.tensor_tensor(cmp[:, :, :], k.iota[:, 0:m.blocks].unsqueeze(2).to_broadcast([128, m.blocks, n]),
                                    end.unsqueeze(1).to_broadcast([128, m.blocks, n]), ALU.is_ge))
            chain(dve.tensor_reduce(blk_f[:, :], cmp[:, :, :], AX.X, ALU.add))
            chain(dve.tensor_scalar(blk_f[:, :], blk_f[:, :], float(n - 1), None, ALU.min))
            chain(dve.tensor_copy(m.block_expert[:, :], blk_f[:, :]))


def send_rows(nc, k, m):
    with Phase(nc, f"{m.name}_send") as ph:
        row_st, idx_st = ph.sb("row_st", [128, G, D]), ph.sb("idx_st", [128, G, m.picks], I32)
        staged, gate = ph.sem("staged"), ph.sem("gate")
        sent = ph.sems("sent", G)
        block = ph.ctx.enter_context(nc.Block())

        @block.vector
        def _(dve):
            def stage(i, first=False):
                for j in range(G):
                    if not first:
                        dve.wait_ge(sent[j], i * 16 * m.picks)
                        pass_on(dve, gate)
                    dve.tensor_copy(row_st[0:P, j, :], row(k.xn_sb, i * G + j)).then_inc(staged, 1)
                    dve.tensor_copy(idx_st[0:P, j, :], m.slot_i[0:P, ds((i * G + j) * m.picks, m.picks)]).then_inc(staged, 1)

            stage(0, first=True)
            with dve.Fori(1, NG) as i:
                stage(i)

        @block.gpsimd
        def _(pool):
            with pool.Fori(0, NG) as i:
                for j in range(G):
                    pool.wait_ge(staged, i * 2 * G + 2 * j + 2)
                    pass_on(pool, gate)
                    for q in range(m.picks):
                        pool.indirect_dma_start(m.rows, bass.IndirectOffsetOnAxis(ap=idx_st[0:P, j, q:q + 1].bitcast(U32), axis=0),
                                                row_st[0:P, j, :], None).then_inc(sent[j], 16)
            for j in range(G):
                pool.wait_ge(sent[j], NG * 16 * m.picks)


def run_experts(nc, k, m, w1_dram, w2_dram, bias_row, function):
    HC = m.hid // 128
    S = 4
    with Phase(nc, f"{m.name}_run") as ph:
        n_w1 = S if m.own_w1 else 1
        w1 = [ph.sb(f"w1_{s}", [128, 2, m.hid]) for s in range(n_w1)]
        w2 = [ph.sb(f"w2_{s}", [128, HC, D]) for s in range(S)]
        rows = [ph.sb(f"rows{s}", [128, D]) for s in range(S)]
        rows_t = [ph.sb(f"rows_t{b}", [128, 2, TOK]) for b in range(2)]
        hid = [ph.sb(f"hid{b}", [128, HC, TOK]) for b in range(2)]
        res = [ph.sb(f"res{s}", [128, D]) for s in range(S)]
        HB = HC // 4
        ps_t = [ph.ps(f"t{b}", [128, 2, TOK]) for b in range(2)]
        ps_h = [[ph.ps(f"h{b}{c}", [128, 4, TOK]) for c in range(HB)] for b in range(2)]
        ps_r = [ph.ps(f"r{b}", [128, D]) for b in range(2)]
        w1_in, w2_in, rows_in, stored = (ph.sems(x, S) for x in ("w1_in", "w2_in", "rows_in", "stored"))
        turned, kept, hid_sum, hid_made, res_sum, res_made = (
            ph.sem(x) for x in ("turned", "kept", "hid_sum", "hid_made", "res_sum", "res_made"))
        gate = ph.sem("gate")
        block = ph.ctx.enter_context(nc.Block())
        turns = m.blocks // S

        @block.sync
        def _(sp):
            if not m.own_w1:
                sp.dma_start(w1[0][:, :, :], w1_dram.rearrange("(c p) h -> p c h", p=128)).then_inc(w1_in[0], 16)

            def turn(i, first=False):
                for s in range(S):
                    n = i * S + s
                    e = sp.value_load(m.block_expert[0:1, ds(n, 1)], min_val=0, max_val=m.n - 1)
                    if not first:
                        sp.wait_ge(res_sum, n - S + 1)
                        pass_on(sp, gate)
                    sp.dma_start(rows[s][:, :], m.rows[ds(n * TOK, TOK), :]).then_inc(rows_in[s], 16)
                    if m.own_w1:
                        sp.dma_start(w1[s][:, :, :], w1_dram[ds(e, 1), :, :].rearrange("o (c p) h -> p (o c) h", p=128))\
                          .then_inc(w1_in[s], 16)
                    sp.dma_start(w2[s][:, :, :], w2_dram[ds(e, 1), :, :].rearrange("o (c p) h -> p (o c) h", p=128))\
                      .then_inc(w2_in[s], 16)

            turn(0, first=True)
            with sp.Fori(1, turns) as i:
                turn(i)

        @block.tensor
        def _(pe):
            if not m.own_w1:
                pe.wait_ge(w1_in[0], 16)

            def landed(sems, i, s):
                pe.wait_ge(sems[s % S], i * 16 + (16 if s >= 0 else 0))

            def hidden(n, i, s, b, banks_used=True):
                pe.wait_ge(kept, n + 1)
                if m.own_w1:
                    landed(w1_in, i, s)
                if banks_used:
                    pe.wait_ge(hid_made, n - 1)
                for c in range(HC):
                    for q in range(2):
                        last = pe.matmul(ps_h[b][c // 4][:, c % 4, :], w1[s % n_w1][:, q, c * 128:(c + 1) * 128],
                                         rows_t[b][:, q, :], start=(q == 0), stop=(q == 1))
                    if c % 4 == 3:
                        last.then_inc(hid_sum, 1)

            def result(n, i, s, b, bank_used=True):
                landed(w2_in, i, s)
                pe.wait_ge(hid_made, n + 1)
                if bank_used:
                    pe.wait_ge(res_made, n - 1)
                for c in range(HC):
                    last = pe.matmul(ps_r[b][:, :], hid[b][:, c, :], w2[s % S][:, c, :], start=(c == 0), stop=(c == HC - 1))
                last.then_inc(res_sum, 1)

            def turn(i, first=False):
                for s in range(S):
                    n, b = i * S + s, s % 2
                    if not first or s >= 1:
                        hidden(n - 1, i, s - 1, 1 - b, banks_used=not first or s >= 3)
                    landed(rows_in, i, s)
                    if not first or s >= 2:
                        pe.wait_ge(kept, n - 1)
                    for q in range(2):
                        last = pe.transpose(ps_t[b][:, q, :], rows[s][:, q * 128:(q + 1) * 128], k.ident[:, :])
                    last.then_inc(turned, 1)
                    if not first or s >= 2:
                        result(n - 2, i, s - 2, b, bank_used=not first)

            turn(0, first=True)
            with pe.Fori(1, turns) as i:
                turn(i)
            hidden(m.blocks - 1, turns - 1, S - 1, 1)
            result(m.blocks - 2, turns - 1, S - 2, 0)
            result(m.blocks - 1, turns - 1, S - 1, 1)

        @block.scalar
        def _(act):
            def turn(i, first=False):
                for s in range(S):
                    n, b = i * S + s, s % 2
                    e = act.value_load(m.block_expert[0:1, ds(n, 1)], min_val=0, max_val=m.n - 1) if m.own_w1 else 0
                    if not first or s >= 2:
                        act.wait_ge(res_sum, n - 1)
                    for c in range(HC):
                        if c % 4 == 0:
                            act.wait_ge(hid_sum, n * HB + c // 4 + 1)
                            pass_on(act, gate)
                        last = act.activation(hid[b][:, c, :], ps_h[b][c // 4][:, c % 4, :], function,
                                              bias=k.cols[:, ds(bias_row + c + e * HC, 1)] if m.own_w1 else
                                              k.cols[:, bias_row + c:bias_row + c + 1])
                    last.then_inc(hid_made, 1)

            turn(0, first=True)
            with act.Fori(1, turns) as i:
                turn(i)

        @block.vector
        def _(dve):
            def finish(n, i, s, b, slot_used=True):
                dve.wait_ge(res_sum, n + 1)
                if slot_used:
                    dve.wait_ge(stored[s % S], i * 16 - (16 if s < 0 else 0))
                dve.tensor_copy(res[s % S][:, :], ps_r[b][:, :]).then_inc(res_made, 1)

            def turn(i, first=False, second=False):
                for s in range(S):
                    n, b = i * S + s, s % 2
                    dve.wait_ge(turned, n + 1)
                    dve.tensor_copy(rows_t[b][:, :, :], ps_t[b][:, :, :]).then_inc(kept, 1)
                    if not first or s >= 2:
                        finish(n - 2, i, s - 2, b, slot_used=not first and not (second and s < 2))

            turn(0, first=True)
            turn(1, second=True)
            with dve.Fori(2, turns) as i:
                turn(i)
            finish(m.blocks - 2, turns - 1, S - 2, 0)
            finish(m.blocks - 1, turns - 1, S - 1, 1)

        @block.gpsimd
        def _(pool):
            with pool.Fori(0, turns) as i:
                for s in range(S):
                    n = i * S + s
                    pool.wait_ge(res_made, n + 1)
                    pass_on(pool, gate)
                    pool.dma_start(m.results[ds(n * TOK, TOK), :], res[s][:, :]).then_inc(stored[s], 16)
            for s in range(S):
                pool.wait_ge(stored[s], 16 * turns)


def route_first(nc, k, m):
    with Phase(nc, "route0") as ph:
        ln = LayerNorm(ph)
        gw = ph.sb("gw", [128, 2, m.n])
        xs, x_t = ph.sb("xs", [128, G, D]), ph.sb("x_t", [128, 2, W])
        logit = ph.sb("logit", [128, G, m.n])
        top, top_i, top_f = ph.sb("top", [128, G, 8]), ph.sb("top_i", [128, G, 8], U32), ph.sb("top_f", [128, G, 2])
        diff, ratio, den = ph.sb("diff", [128, G]), ph.sb("ratio", [128, G]), ph.sb("den", [128, G])
        ps_t = [ph.ps(f"t{s}", [128, 2, 128]) for s in range(2)]
        ps_l = ph.ps("l", [128, G, m.n])
        w_in, turned, kept, logit_sum = ph.sem("w_in"), ph.sem("turned"), ph.sem("kept"), ph.sem("logit_sum")
        spread, step, diff_made, ratio_made = ph.sem("spread"), ph.sem("step"), ph.sem("diff_made"), ph.sem("ratio_made")
        gate = ph.sem("gate")
        block = ph.ctx.enter_context(nc.Block())
        STEPS = 2 + 2 * G + 5

        @block.sync
        def _(sp):
            sp.dma_start(gw[:, :, :], k.L0_ffn_gate_w.rearrange("(c p) e -> p c e", p=128)).then_inc(w_in, 16)

        @block.vector
        def _(dve):
            with dve.Fori(0, NG) as i:
                at = [i * STEPS]

                def chain(ins):
                    at[0] = at[0] + 1
                    ins.then_inc(step, 1)
                    dve.wait_ge(step, at[0])
                    pass_on(dve, gate)

                ln_vector(dve, ln, i, lambda j: row(k.x_sb, i * G + j), lambda j: xs[0:P, j, :])
                dve.wait_ge(logit_sum, i * G + G)
                chain(dve.tensor_tensor(logit[0:P, :, :], ps_l[0:P, :, :], k.gate_b[0:P, :].unsqueeze(1).to_broadcast([P, G, m.n]),
                                        ALU.add))
                for j in range(G):
                    chain(dve.max(top[0:P, j, :], logit[0:P, j, :]))
                    chain(dve.max_index(top_i[0:P, j, :], top[0:P, j, :], logit[0:P, j, :]))
                chain(dve.tensor_copy(top_f[0:P, :, :], top_i[0:P, :, 0:2]))
                dve.tensor_tensor(diff[0:P, :], top[0:P, :, 1], top[0:P, :, 0], ALU.subtract).then_inc(diff_made, 1)
                dve.wait_ge(ratio_made, i + 1)
                chain(dve.tensor_scalar(den[0:P, :], ratio[0:P, :], 1.0, None, ALU.add))
                chain(dve.reciprocal(den[0:P, :], den[0:P, :]))
                prob = m.prob[0:P, ds(i * 2 * G, 2 * G)].rearrange("p (j q) -> p j q", q=2)
                chain(dve.tensor_copy(prob[:, :, 0], den[0:P, :]))
                chain(dve.tensor_tensor(prob[:, :, 1], den[0:P, :], ratio[0:P, :], ALU.mult))
                chain(dve.tensor_tensor(m.onehot[0:P, :, ds(i * 2 * G, 2 * G)],
                                        top_f[0:P, :, :].rearrange("p j q -> p (j q)").unsqueeze(1).to_broadcast([P, m.n, 2 * G]),
                                        k.iota[0:P, 0:m.n].unsqueeze(2).to_broadcast([P, m.n, 2 * G]), ALU.is_equal))

        @block.scalar
        def _(act):
            with act.Fori(0, NG) as i:
                ln_scalar(act, k, ln, i)
                for j in range(G):
                    act.wait_ge(ln.out_done, i * G + j + 1)
                    pass_on(act, gate)
                    act.activation(row(k.xn_sb, i * G + j), xs[0:P, j, :], ACT.Copy).then_inc(spread, 1)
                    act.wait_ge(turned, i * G + j + 1)
                    pass_on(act, gate)
                    act.activation(x_t[:, :, j * P:(j + 1) * P], ps_t[j % 2][:, :, 0:P], ACT.Copy).then_inc(kept, 1)
                act.wait_ge(diff_made, i + 1)
                act.activation(ratio[0:P, :], diff[0:P, :], ACT.Exp).then_inc(ratio_made, 1)

        @block.tensor
        def _(pe):
            pe.wait_ge(w_in, 16)
            pe.sem_inc(kept, 2)
            with pe.Fori(0, NG) as i:
                for j in range(G):
                    pe.wait_ge(ln.out_done, i * G + j + 1)
                    pe.wait_ge(kept, i * G + j + 1)
                    for q in range(2):
                        last = pe.transpose(ps_t[j % 2][:, q, 0:P], xs[0:P, j, q * 128:(q + 1) * 128], k.ident[0:P, 0:P])
                    last.then_inc(turned, 1)
                for j in range(G):
                    pe.wait_ge(kept, i * G + j + 3)
                    for q in range(2):
                        last = pe.matmul(ps_l[0:P, j, :], x_t[:, q, j * P:(j + 1) * P], gw[:, q, :], start=(q == 0), stop=(q == 1))
                    last.then_inc(logit_sum, 1)


def combine(nc, k, m, bias_dram, norm):
    K = m.picks
    with Phase(nc, f"{m.name}_combine") as ph:
        ln = LayerNorm(ph)
        bias = ph.sb("bias", [m.n, D])
        idx_st = ph.sb("idx_st", [128, G, K], I32)
        got = ph.sb("got", [128, G, K, D])
        mix, mix_w = ph.sb("mix", [128, G, m.n, K]), ph.sb("mix_w", [128, G, m.n])
        mix_t = ph.sb("mix_t", [m.n, G, P])
        z, zn = ph.sb("z", [128, G, D]), ph.sb("zn", [128, G, D])
        ps_m = [ph.ps(f"m{s}", [128, 128]) for s in range(2)]
        ps_b = [ph.ps(f"b{s}", [128, D]) for s in range(2)]
        bias_in = ph.sem("bias_in")
        got_in = ph.sems("got_in", G)
        idx_made, mix_made, mixed, mix_turned, mix_kept = (
            ph.sem(x) for x in ("idx_made", "mix_made", "mixed", "mix_turned", "mix_kept"))
        bias_sum, z_made, zn_made, stored, gate = (ph.sem(x) for x in ("bias_sum", "z_made", "zn_made", "stored", "gate"))
        block = ph.ctx.enter_context(nc.Block())
        ZS = K + 1

        @block.sync
        def _(sp):
            sp.dma_start(bias[:, :], bias_dram).then_inc(bias_in, 16)
            if not norm:
                sp.wait_ge(zn_made, T)
                sp.dma_start(k.out.rearrange("(t p) d -> p t d", p=P), k.x_sb[0:P, :, :]).then_inc(stored, 16)
                sp.wait_ge(stored, 16)

        @block.gpsimd
        def _(pool):
            with pool.Fori(0, NG) as i:
                for j in range(G):
                    pool.wait_ge(idx_made, i * G + j + 1)
                    pass_on(pool, gate)
                    for q in range(K):
                        pool.indirect_dma_start(got[0:P, j, q, :], None, m.results,
                                                bass.IndirectOffsetOnAxis(ap=idx_st[0:P, j, q:q + 1].bitcast(U32), axis=0))\
                            .then_inc(got_in[j], 16)

        @block.vector
        def _(dve):
            with dve.Fori(0, NG) as i:
                for j in range(G):
                    dve.tensor_copy(idx_st[0:P, j, :], m.slot_i[0:P, ds((i * G + j) * K, K)]).then_inc(idx_made, 1)
                for j in range(G):
                    cols = ds((i * G + j) * K, K)
                    dve.tensor_tensor(mix[0:P, j, :, :], m.onehot[0:P, :, cols],
                                      m.prob[0:P, cols].unsqueeze(1).to_broadcast([P, m.n, K]), ALU.mult).then_inc(mix_made, 1)
                dve.wait_ge(mix_made, i * G + G)
                pass_on(dve, gate)
                for j in range(G):
                    dve.tensor_reduce(mix_w[0:P, j, :], mix[0:P, j, :, :], AX.X, ALU.add).then_inc(mixed, 1)
                for j in range(G):
                    base = row(k.xn_sb if norm else k.x_sb, i * G + j)
                    dve.wait_ge(bias_sum, i * G + j + 1)
                    pass_on(dve, gate)
                    dve.tensor_tensor(z[0:P, j, :], ps_b[j % 2][0:P, :], base, ALU.add).then_inc(z_made, 1)
                    dve.wait_ge(got_in[j], (i + 1) * 16 * K)
                    for q in range(K):
                        dve.wait_ge(z_made, (i * G + j) * ZS + q + 1)
                        ins = dve.scalar_tensor_tensor(z[0:P, j, :] if norm or q < K - 1 else base, got[0:P, j, q, :],
                                                       m.prob[0:P, ds((i * G + j) * K + q, 1)], z[0:P, j, :], ALU.mult, ALU.add)
                        ins.then_inc(z_made, 1)
                if norm:
                    dve.wait_ge(z_made, (i + 1) * G * ZS)
                    pass_on(dve, gate)
                    ln_vector(dve, ln, i, lambda j: z[0:P, j, :], lambda j: zn[0:P, j, :])
                    dve.wait_ge(ln.out_done, i * G + G)
                    dve.tensor_tensor(zn[0:P, :, :], zn[0:P, :, :], k.gamma[0:P, :].unsqueeze(1).to_broadcast([P, G, D]), ALU.mult)\
                       .then_inc(zn_made, 1)
                    dve.wait_ge(zn_made, i * 3 + 1)
                    dve.tensor_tensor(zn[0:P, :, :], zn[0:P, :, :], k.beta[0:P, :].unsqueeze(1).to_broadcast([P, G, D]), ALU.add)\
                       .then_inc(zn_made, 1)
                    dve.wait_ge(zn_made, i * 3 + 2)
                    group = k.x_sb[0:P, ds(i * G, G), :]
                    dve.tensor_tensor(group, zn[0:P, :, :], group, ALU.add).then_inc(zn_made, 1)
            if not norm:
                dve.wait_ge(z_made, T * ZS)
                dve.sem_inc(zn_made, T)

        @block.scalar
        def _(act):
            with act.Fori(0, NG) as i:
                for j in range(G):
                    act.wait_ge(mix_turned, i * G + j + 1)
                    pass_on(act, gate)
                    act.activation(mix_t[:, j, :], ps_m[j % 2][0:m.n, 0:P], ACT.Copy).then_inc(mix_kept, 1)
                if norm:
                    ln_scalar(act, k, ln, i)

        @block.tensor
        def _(pe):
            pe.wait_ge(bias_in, 16)
            pe.sem_inc(mix_kept, 2)

            def tiles(i, first=False):
                for j in range(G):
                    pe.wait_ge(mixed, i * G + j + 1)
                    pe.wait_ge(mix_kept, i * G + j + 1)
                    pe.transpose(ps_m[j % 2][0:m.n, 0:P], mix_w[0:P, j, :], k.ident[0:P, 0:P]).then_inc(mix_turned, 1)
                for j in range(G):
                    pe.wait_ge(mix_kept, i * G + j + 3)
                    if not first or j >= 2:
                        pe.wait_ge(z_made, (i * G + j - 2) * ZS + 1)
                    pe.matmul(ps_b[j % 2][0:P, :], mix_t[:, j, :], bias[:, :], start=True, stop=True).then_inc(bias_sum, 1)

            tiles(0, first=True)
            with pe.Fori(1, NG) as i:
                tiles(i)


def vectors_apart(ap):
    return ap[:, MUL:D].rearrange("p (u c) -> p c u", c=3)


def edge_table(nc, k):
    with Phase(nc, "table") as ph:
        ln = LayerNorm(ph)
        raw = ph.sb("raw", [128, 2, 2, 128])
        w = ph.sb("w", [128, 2, 2, 128])
        xs, xq, x_t = ph.sb("xs", [128, G, D]), ph.sb("xq", [128, G, D]), ph.sb("x_t", [128, G, 2, P])
        y = ph.sb("y", [128, G, D])
        ps_t = [ph.ps(f"t{s}", [128, 2, 128]) for s in range(2)]
        ps_y = [ph.ps(f"y{s}", [128, D]) for s in range(2)]
        ps_s = [ph.ps(f"s{s}", [128, D]) for s in range(2)]
        raw_zero, raw_in, w_made = ph.sem("raw_zero"), ph.sem("raw_in"), ph.sem("w_made")
        apart, turned, kept, made, y_made, added = (ph.sem(x) for x in ("apart", "turned", "kept", "made", "y_made", "added"))
        stored, gate = ph.sem("stored"), ph.sem("gate")
        block = ph.ctx.enter_context(nc.Block())

        @block.gpsimd
        def _(pool):
            pool.memset(raw[:, :, :, :], 0.0).then_inc(raw_zero, 1)

        @block.sync
        def _(sp):
            sp.wait_ge(raw_zero, 1)
            for which, (w0, w1) in enumerate([(k.L1_gnn_lin1_w0, k.L1_gnn_lin1_w1), (k.L1_gnn_sc_w0, k.L1_gnn_sc_w1)]):
                sp.dma_start(raw[0:MUL, which, 0, 0:MUL], w0).then_inc(raw_in, 16)
                sp.dma_start(raw[MUL:128, which, 0, MUL:128], w1).then_inc(raw_in, 16)
                sp.dma_start(raw[0:MUL, which, 1, 0:MUL], w1).then_inc(raw_in, 16)
                sp.dma_start(raw[MUL:128, which, 1, MUL:128], w1).then_inc(raw_in, 16)
            with sp.Fori(0, NG) as i:
                sp.wait_ge(y_made, i * G + G)
                pass_on(sp, gate)
                sp.dma_start(k.y_dram[ds(i * W, W), :].rearrange("(j p) d -> p j d", p=P), y[0:P, :, :]).then_inc(stored, 16)
                sp.wait_ge(stored, i * 16 + 16)
                pass_on(sp, gate)

        @block.vector
        def _(dve):
            dve.wait_ge(raw_in, 128)
            dve.tensor_scalar(w[:, 0, :, :], raw[:, 0, :, :], INV_MUL, None, ALU.mult).then_inc(w_made, 1)
            dve.tensor_scalar(w[:, 1, :, :], raw[:, 1, :, :], INV_MUL * C_S, None, ALU.mult).then_inc(w_made, 1)
            with dve.Fori(0, NG) as i:
                ln_vector(dve, ln, i, lambda j: row(k.x_sb, i * G + j), lambda j: xs[0:P, j, :])
                for j in range(G):
                    dve.wait_ge(made, i * G + j + 1)
                    pass_on(dve, gate)
                    x, a = row(k.x_sb, i * G + j), k.node_a[0:P, ds(i * G + j, 1)]
                    dve.scalar_tensor_tensor(x[:, 0:MUL], ps_s[j % 2][0:P, 0:MUL], a, x[:, 0:MUL], ALU.mult, ALU.add).then_inc(added, 1)
                    dve.scalar_tensor_tensor(vectors_apart(x), ps_s[j % 2][0:P, MUL:D].rearrange("p (c u) -> p c u", c=3), a,
                                             vectors_apart(x), ALU.mult, ALU.add).then_inc(added, 1)

        @block.scalar
        def _(act):
            def tiles(i, first=False):
                ln_scalar(act, k, ln, i)
                for j in range(G):
                    act.wait_ge(ln.out_done, i * G + j + 1)
                    act.activation(xq[0:P, j, 0:MUL], xs[0:P, j, 0:MUL], ACT.Copy).then_inc(apart, 1)
                    act.activation(xq[0:P, j, MUL:D].rearrange("p (c u) -> p c u", c=3), vectors_apart(xs[0:P, j, :]), ACT.Copy)\
                       .then_inc(apart, 1)
                for j in range(G):
                    act.wait_ge(turned, i * G + j + 1)
                    act.activation(x_t[:, j, :, :], ps_t[j % 2][:, :, 0:P], ACT.Copy).then_inc(kept, 1)
                for j in range(G):
                    act.wait_ge(made, i * G + j + 1)
                    if not first:
                        act.wait_ge(stored, i * 16)
                    pass_on(act, gate)
                    act.activation(y[0:P, j, :], ps_y[j % 2][0:P, :], ACT.Copy, scale=k.node_a[0:P, ds(i * G + j, 1)])\
                       .then_inc(y_made, 1)

            tiles(0, first=True)
            with act.Fori(1, NG) as i:
                tiles(i)

        @block.tensor
        def _(pe):
            pe.wait_ge(w_made, 2)
            pe.sem_inc(kept, 2)

            def tiles(i, first=False):
                for j in range(G):
                    pe.wait_ge(apart, (i * G + j) * 2 + 2)
                    pe.wait_ge(kept, i * G + j + 1)
                    for q in range(2):
                        last = pe.transpose(ps_t[j % 2][:, q, 0:P], xq[0:P, j, q * 128:(q + 1) * 128], k.ident[0:P, 0:P])
                    last.then_inc(turned, 1)
                for j in range(G):
                    pe.wait_ge(kept, i * G + j + 3)
                    if not first or j >= 2:
                        pe.wait_ge(y_made, i * G + j - 1)
                        pe.wait_ge(added, (i * G + j - 1) * 2)
                    for which, ps in enumerate((ps_y, ps_s)):
                        for q in range(2):
                            last = pe.matmul(ps[j % 2][0:P, q * 128:(q + 1) * 128], x_t[:, j, q, :], w[:, which, q, :],
                                             start=True, stop=True)
                    last.then_inc(made, 1)

            tiles(0, first=True)
            with pe.Fori(1, NG) as i:
                tiles(i)


def sum_messages(nc, k):
    with Phase(nc, "msg") as ph:
        fc1, fc2_raw, fc2 = ph.sb("fc1", [2 * REC, 128]), ph.sb("fc2_raw", [128, D]), ph.sb("fc2", [128, 4, MUL])
        rec = [ph.sb(f"rec{s}", [128, 2, REC]) for s in range(SLOTS)]
        got = [ph.sb(f"got{s}", [128, 2, 4, MUL]) for s in range(SLOTS)]
        onehot = [ph.sb(f"onehot{b}", [128, 2, P]) for b in range(2)]
        onehot_ea0 = [ph.sb(f"onehot_ea0{b}", [128, 2, P]) for b in range(2)]
        attr_t = [ph.sb(f"attr_t{b}", [2 * REC, 128]) for b in range(2)]
        hid = [ph.sb(f"hid{b}", [128, 128]) for b in range(2)]
        part = [ph.sb(f"part{b}", [128, 2, 3, MUL]) for b in range(2)]
        dot = [ph.sb(f"dot{b}", [128, 2, MUL]) for b in range(2)]
        msg = [ph.sb(f"msg{b}", [128, 2, 9, MUL]) for b in range(2)]
        ps_e = [ph.ps(f"e{b}", [128, 512]) for b in range(2)]
        ps_w = [ph.ps(f"w{b}", [128, 2, 8, MUL]) for b in range(2)]
        ps_z = [ph.ps(f"z{b}", [128, 2, D]) for b in range(2)]
        w_in, w_made = ph.sem("w_in"), ph.sem("w_made")
        rec_in, got_in = ph.sems("rec_in", SLOTS), ph.sems("got_in", SLOTS)
        attr_turned, attr_kept, hid_sum, hid_made, w_sum = (
            ph.sem(x) for x in ("attr_turned", "attr_kept", "hid_sum", "hid_made", "w_sum"))
        ea0_made, part_made, masked, msg_step, msg_made, summed, added = (
            ph.sem(x) for x in ("ea0_made", "part_made", "masked", "msg_step", "msg_made", "summed", "added"))
        fc1_zero, cleared, gate = ph.sem("fc1_zero"), ph.sem("cleared"), ph.sem("gate")
        block = ph.ctx.enter_context(nc.Block())
        turns = NEB // SLOTS

        @block.sync
        def _(sp):
            sp.wait_ge(fc1_zero, 1)
            for u in range(2):
                sp.dma_start(fc1[REC * u:REC * u + 8, 64 * u:64 * u + 64], k.L1_gnn_fc_w1).then_inc(w_in, 16)
                sp.dma_start(fc2_raw[64 * u:64 * u + 64, :], k.L1_gnn_fc_w2).then_inc(w_in, 16)

            def turn(i, first=False):
                for s in range(SLOTS):
                    n = i * SLOTS + s
                    start = sp.value_load(k.block_start[0:1, ds(n, 1)], min_val=0, max_val=E)
                    if not first:
                        sp.wait_ge(summed, n - SLOTS + 1)
                        pass_on(sp, gate)
                    sp.dma_start(rec[s][:, :, :], k.recs[ds(start, EB), :].rearrange("(p u) w -> p u w", u=2))\
                      .then_inc(rec_in[s], 16)

            turn(0, first=True)
            with sp.Fori(1, turns) as i:
                turn(i)

        @block.gpsimd
        def _(pool):
            with pool.Fori(0, turns) as i:
                for s in range(SLOTS):
                    pool.wait_ge(rec_in[s], i * 16 + 16)
                    pass_on(pool, gate)
                    for u in range(2):
                        pool.indirect_dma_start(
                            got[s][:, u, :, :].rearrange("p k v -> p (k v)"), None, k.y_dram,
                            bass.IndirectOffsetOnAxis(ap=rec[s][:, u, SRC:SRC + 1].bitcast(U32), axis=0)).then_inc(got_in[s], 16)

        @block.tensor
        def _(pe):
            pe.wait_ge(w_made, 4)

            def weigh(n, b):
                pe.wait_ge(hid_made, n + 1)
                for u in range(2):
                    last = pe.matmul(ps_w[b][:, u, 0:4, :].rearrange("p k v -> p (k v)"), hid[b][64 * u:64 * u + 64, :],
                                     fc2[64 * u:64 * u + 64, :, :].rearrange("p k v -> p (k v)"), start=True, stop=True)
                last.then_inc(w_sum, 1)

            def add_up(n, b):
                pe.wait_ge(ea0_made, 2 * n + 2)
                pe.wait_ge(msg_made, n + 1)
                for h, mask in enumerate((onehot_ea0[b], onehot[b])):
                    for u in range(2):
                        last = pe.matmul(ps_z[b][0:P, h, :], mask[:, u, :],
                                         msg[b][:, u, 4 * h:4 * h + 4, :].rearrange("p k v -> p (k v)"),
                                         start=(u == 0), stop=(u == 1))
                last.then_inc(summed, 1)

            def turn(i, first=False):
                for s in range(SLOTS):
                    n, b = i * SLOTS + s, s % 2
                    pe.wait_ge(rec_in[s], i * 16 + 16)
                    if not first or s >= 2:
                        pe.wait_ge(hid_made, n - 1)
                    pe.transpose(ps_e[b][0:2 * REC, 0:128], rec[s][:, :, :].rearrange("p u w -> p (u w)"), k.ident[:, :])\
                      .then_inc(attr_turned, 1)
                    if not first or s >= 1:
                        if not first or s >= 3:
                            pe.wait_ge(msg_made, n - 2)
                        weigh(n - 1, 1 - b)
                    pe.wait_ge(attr_kept, n + 1)
                    pe.matmul(ps_e[b][:, 128:256], fc1[:, :], attr_t[b][:, :], start=True, stop=True).then_inc(hid_sum, 1)
                    if not first or s >= 2:
                        if not first or s >= 4:
                            pe.wait_ge(added, n - 3)
                        add_up(n - 2, b)

            turn(0, first=True)
            with pe.Fori(1, turns) as i:
                turn(i)
            pe.wait_ge(msg_made, NEB - 2)
            weigh(NEB - 1, 1)
            pe.wait_ge(added, NEB - 3)
            add_up(NEB - 2, 0)
            pe.wait_ge(added, NEB - 2)
            add_up(NEB - 1, 1)

        @block.scalar
        def _(act):
            def scale_parts(n, i, s, b, slot_used=True):
                act.wait_ge(got_in[s % SLOTS], i * 32 + (32 if s >= 0 else 0))
                if slot_used:
                    act.wait_ge(msg_made, n - 1)
                pass_on(act, gate)
                for u in range(2):
                    for c in range(3):
                        last = act.activation(part[b][:, u, c, :], got[s % SLOTS][:, u, 1 + c, :], ACT.Copy,
                                              scale=rec[s % SLOTS][:, u, 9 + c:10 + c])
                last.then_inc(part_made, 1)

            def scale_onehots(n, s, b):
                act.wait_ge(masked, n + 1)
                pass_on(act, gate)
                for u in range(2):
                    act.activation(onehot_ea0[b][:, u, :], onehot[b][:, u, :], ACT.Copy, scale=rec[s % SLOTS][:, u, 8:9])\
                       .then_inc(ea0_made, 1)

            def turn(i, first=False):
                for s in range(SLOTS):
                    n, b = i * SLOTS + s, s % 2
                    act.wait_ge(attr_turned, n + 1)
                    act.activation(attr_t[b][:, :], ps_e[b][0:2 * REC, 0:128], ACT.Copy).then_inc(attr_kept, 1)
                    if not first or s >= 1:
                        scale_parts(n - 1, i, s - 1, 1 - b, slot_used=not first or s >= 3)
                    act.wait_ge(hid_sum, n + 1)
                    if not first or s >= 2:
                        act.wait_ge(w_sum, n - 1)
                    act.activation(hid[b][:, :], ps_e[b][:, 128:256], ACT.Silu, scale=1.0 / math.sqrt(8)).then_inc(hid_made, 1)
                    if not first or s >= 1:
                        scale_onehots(n - 1, s - 1, 1 - b)

            turn(0, first=True)
            with act.Fori(1, turns) as i:
                turn(i)
            scale_parts(NEB - 1, turns - 1, SLOTS - 1, 1)
            scale_onehots(NEB - 1, SLOTS - 1, 1)

        @block.vector
        def _(dve):
            dve.memset(k.agg[:, :, :], 0.0).then_inc(cleared, 1)
            dve.memset(fc1[:, :], 0.0).then_inc(fc1_zero, 1)
            dve.wait_ge(w_in, 64)
            for at, (which, factor) in enumerate([(0, 1.0), (2, 1.0), (1, 1.0 / math.sqrt(3.0)), (3, 1.0)]):
                dve.tensor_scalar(fc2[:, at, :], fc2_raw[:, which * MUL:(which + 1) * MUL], SILU_NORM / 8.0 * factor, None, ALU.mult)\
                   .then_inc(w_made, 1)

            def tile_of(n):
                return dve.value_load(k.block_tile[0:1, ds(n, 1)], min_val=0, max_val=T - 1)

            def add_sum(n, b, tile, any_before=True):
                dve.wait_ge(summed, n + 1)
                if any_before:
                    dve.wait_ge(added, n)
                dve.tensor_tensor(row(k.agg, tile), ps_z[b][0:P, :, :].rearrange("p h v -> p (h v)"), row(k.agg, tile), ALU.add)\
                   .then_inc(added, 1)

            def turn(i, first=False):
                tile_before = None if first else tile_of(i * SLOTS - 1)
                for s in range(SLOTS):
                    n, b = i * SLOTS + s, s % 2
                    tile = tile_of(n)
                    dve.wait_ge(rec_in[s], i * 16 + 16)
                    if not first or s >= 2:
                        dve.wait_ge(summed, n - 1)
                    dve.tensor_tensor(onehot[b][:, :, :], node_ids(k, tile), rec[s][:, :, DST:DST + 1].to_broadcast([128, 2, P]),
                                      ALU.is_equal).then_inc(masked, 1)
                    w, y, m = ps_w[b], got[s], msg[b]
                    ea1 = rec[s][:, :, 9:12].unsqueeze(3).to_broadcast([128, 2, 3, MUL])
                    dve.wait_ge(got_in[s], i * 32 + 32)
                    dve.wait_ge(w_sum, n + 1)
                    dve.tensor_tensor(m[:, :, 0:9:8, :], w[:, :, 0:2, :], y[:, :, 0:1, :].to_broadcast([128, 2, 2, MUL]), ALU.mult)\
                       .then_inc(msg_step, 1)
                    dve.wait_ge(part_made, n + 1)
                    pass_on(dve, gate)
                    dve.tensor_reduce(dot[b][:, :, :], part[b][:, :, :, :].rearrange("p u c v -> p u v c"), AX.X, ALU.add)\
                       .then_inc(msg_step, 1)
                    dve.tensor_tensor(m[:, :, 1:4, :], w[:, :, 3:4, :].to_broadcast([128, 2, 3, MUL]), y[:, :, 1:4, :], ALU.mult)
                    dve.wait_ge(msg_step, n * 2 + 2)
                    dve.tensor_tensor(m[:, :, 5:8, :], m[:, :, 8:9, :].to_broadcast([128, 2, 3, MUL]), ea1, ALU.mult)
                    dve.tensor_tensor(m[:, :, 4, :], w[:, :, 2, :], dot[b][:, :, :], ALU.mult).then_inc(msg_made, 1)
                    if not first or s >= 1:
                        add_sum(n - 1, 1 - b, tile_before, any_before=not first or s >= 2)
                    tile_before = tile

            turn(0, first=True)
            with dve.Fori(1, turns) as i:
                turn(i)
            add_sum(NEB - 1, 1, tile_of(NEB - 1))


def update_nodes(nc, k):
    FACTOR = C_X / math.sqrt(20.0) / math.sqrt(2 * MUL)
    with Phase(nc, "update") as ph:
        raw, w = ph.sb("raw", [128, 4, 128]), ph.sb("w", [128, 4, 128])
        tile = ph.sb("tile", [128, G, 4, 128])
        tile_t = ph.sb("tile_t", [128, G, 4, P])
        ps_t = [ph.ps(f"t{s}", [128, 4, 128]) for s in range(2)]
        ps_o = [ph.ps(f"o{s}", [128, D]) for s in range(2)]
        raw_zero, raw_in, w_made, staged, turned, kept, made, added, gate = (
            ph.sem(x) for x in ("raw_zero", "raw_in", "w_made", "staged", "turned", "kept", "made", "added", "gate"))
        block = ph.ctx.enter_context(nc.Block())

        @block.sync
        def _(sp):
            w00, w01, w10, w11 = k.L1_gnn_lin2_w00, k.L1_gnn_lin2_w01, k.L1_gnn_lin2_w10, k.L1_gnn_lin2_w11
            sp.wait_ge(raw_zero, 1)
            for q, (wa, wb) in enumerate([(w00, w11), (w11, w11), (w01, w10), (w10, w10)]):
                sp.dma_start(raw[0:MUL, q, 0:MUL], wa).then_inc(raw_in, 16)
                sp.dma_start(raw[MUL:128, q, MUL:128], wb).then_inc(raw_in, 16)

        @block.vector
        def _(dve):
            dve.memset(raw[:, :, :], 0.0).then_inc(raw_zero, 1)
            dve.wait_ge(raw_in, 128)
            dve.tensor_scalar(w[:, :, :], raw[:, :, :], FACTOR, None, ALU.mult).then_inc(w_made, 1)
            dve.sem_inc(turned, G)
            with dve.Fori(0, NG) as i:
                for j in range(G):
                    dve.wait_ge(turned, i * G + j + 1)
                    pass_on(dve, gate)
                    dve.tensor_copy(tile[0:P, j, :, :].rearrange("p k v -> p (k v)"), row(k.agg, i * G + j)).then_inc(staged, 1)
                for j in range(G):
                    dve.wait_ge(made, i * G + j + 1)
                    pass_on(dve, gate)
                    x, a = row(k.x_sb, i * G + j), k.node_a[0:P, ds(i * G + j, 1)]
                    dve.scalar_tensor_tensor(x[:, 0:MUL], ps_o[j % 2][0:P, 0:MUL], a, x[:, 0:MUL], ALU.mult, ALU.add).then_inc(added, 1)
                    dve.scalar_tensor_tensor(vectors_apart(x), ps_o[j % 2][0:P, MUL:D].rearrange("p (c u) -> p c u", c=3), a,
                                             vectors_apart(x), ALU.mult, ALU.add).then_inc(added, 1)

        @block.scalar
        def _(act):
            with act.Fori(0, NG) as i:
                for j in range(G):
                    act.wait_ge(turned, i * G + j + 1 + G)
                    act.activation(tile_t[:, j, :, :], ps_t[j % 2][:, :, 0:P], ACT.Copy).then_inc(kept, 1)

        @block.tensor
        def _(pe):
            pe.wait_ge(w_made, 1)
            pe.sem_inc(kept, 2)

            def tiles(i, first=False):
                for j in range(G):
                    pe.wait_ge(staged, i * G + j + 1)
                    pe.wait_ge(kept, i * G + j + 1)
                    for q in range(4):
                        last = pe.transpose(ps_t[j % 2][:, q, 0:P], tile[0:P, j, q, :], k.ident[0:P, 0:P])
                    last.then_inc(turned, 1)
                for j in range(G):
                    pe.wait_ge(kept, i * G + j + 3)
                    if not first or j >= 2:
                        pe.wait_ge(added, (i * G + j - 1) * 2)
                    for h in range(2):
                        for q in (h, h + 2):
                            last = pe.matmul(ps_o[j % 2][0:P, h * 128:(h + 1) * 128], tile_t[:, j, q, :], w[:, q, :],
                                             start=(q == h), stop=(q == h + 2))
                    last.then_inc(made, 1)

            tiles(0, first=True)
            with pe.Fori(1, NG) as i:
                tiles(i)


def route_second(nc, k, m):
    HC = m.hid // 128
    with Phase(nc, "route1") as ph:
        ln = LayerNorm(ph)
        w1, wg = ph.sb("w1", [128, 2, m.hid]), ph.sb("wg", [128, HC, m.n])
        xs, x_t, hid = ph.sb("xs", [128, G, D]), ph.sb("x_t", [128, 2, W]), ph.sb("hid", [128, HC, W])
        logit, top, top_i = ph.sb("logit", [128, G, m.n]), ph.sb("top", [128, G, 8]), ph.sb("top_i", [128, G, 8], U32)
        top_f, total = ph.sb("top_f", [128, G]), ph.sb("total", [128, G])
        shifted, expd = ph.sb("shifted", [128, G, m.n]), ph.sb("expd", [128, G, m.n])
        ps_t = [ph.ps(f"t{s}", [128, 2, 128]) for s in range(2)]
        ps_h = [ph.ps(f"h{s}", [128, 512]) for s in range(4)]
        ps_l = ph.ps("l", [128, G, m.n])
        w_in, turned, kept, hid_sum, hid_made, logit_sum = (
            ph.sem(x) for x in ("w_in", "turned", "kept", "hid_sum", "hid_made", "logit_sum"))
        spread, step, shift_made, exp_made, gate = (ph.sem(x) for x in ("spread", "step", "shift_made", "exp_made", "gate"))
        block = ph.ctx.enter_context(nc.Block())
        STEPS = 1 + 2 * G + 4
        H2 = 2 * HC

        @block.sync
        def _(sp):
            sp.dma_start(w1[:, :, :], k.L1_ffn_W1.rearrange("(c p) h -> p c h", p=128)).then_inc(w_in, 16)
            sp.dma_start(wg[:, :, :], k.L1_ffn_Wg.rearrange("(c p) h -> p c h", p=128)).then_inc(w_in, 16)

        @block.vector
        def _(dve):
            with dve.Fori(0, NG) as i:
                at = [i * STEPS]

                def chain(ins):
                    at[0] = at[0] + 1
                    ins.then_inc(step, 1)
                    dve.wait_ge(step, at[0])
                    pass_on(dve, gate)

                ln_vector(dve, ln, i, lambda j: row(k.x_sb, i * G + j), lambda j: xs[0:P, j, :])
                dve.wait_ge(logit_sum, i * G + G)
                chain(dve.tensor_tensor(logit[0:P, :, :], ps_l[0:P, :, :], k.bg[0:P, :].unsqueeze(1).to_broadcast([P, G, m.n]), ALU.add))
                for j in range(G):
                    chain(dve.max(top[0:P, j, :], logit[0:P, j, :]))
                    chain(dve.max_index(top_i[0:P, j, :], top[0:P, j, :], logit[0:P, j, :]))
                chain(dve.tensor_copy(top_f[0:P, :], top_i[0:P, :, 0]))
                dve.tensor_tensor(shifted[0:P, :, :], logit[0:P, :, :], top[0:P, :, 0:1].to_broadcast([P, G, m.n]), ALU.subtract)\
                   .then_inc(shift_made, 1)
                dve.wait_ge(exp_made, i + 1)
                chain(dve.tensor_reduce(total[0:P, :], expd[0:P, :, :], AX.X, ALU.add))
                chain(dve.reciprocal(m.prob[0:P, ds(i * G, G)], total[0:P, :]))
                chain(dve.tensor_tensor(m.onehot[0:P, :, ds(i * G, G)], top_f[0:P, :].unsqueeze(1).to_broadcast([P, m.n, G]),
                                        k.iota[0:P, 0:m.n].unsqueeze(2).to_broadcast([P, m.n, G]), ALU.is_equal))

        @block.scalar
        def _(act):
            with act.Fori(0, NG) as i:
                ln_scalar(act, k, ln, i)
                for j in range(G):
                    act.wait_ge(ln.out_done, i * G + j + 1)
                    pass_on(act, gate)
                    act.activation(row(k.xn_sb, i * G + j), xs[0:P, j, :], ACT.Copy).then_inc(spread, 1)
                    act.wait_ge(turned, i * G + j + 1)
                    pass_on(act, gate)
                    act.activation(x_t[:, :, j * P:(j + 1) * P], ps_t[j % 2][:, :, 0:P], ACT.Copy).then_inc(kept, 1)
                for c, (a, b) in enumerate(CUTS):
                    for h in range(HC):
                        act.wait_ge(hid_sum, i * H2 + c * HC + h + 1)
                        act.activation(hid[:, h, a:b], ps_h[h % 4][:, 0:b - a], ACT.Gelu,
                                       bias=k.cols[:, FFN1_B1 + h:FFN1_B1 + h + 1]).then_inc(hid_made, 1)
                act.wait_ge(shift_made, i + 1)
                act.activation(expd[0:P, :, :], shifted[0:P, :, :], ACT.Exp).then_inc(exp_made, 1)

        @block.tensor
        def _(pe):
            pe.wait_ge(w_in, 32)
            pe.sem_inc(kept, 2)
            pe.sem_inc(hid_made, 4)
            with pe.Fori(0, NG) as i:
                for j in range(G):
                    pe.wait_ge(ln.out_done, i * G + j + 1)
                    pe.wait_ge(kept, i * G + j + 1)
                    for q in range(2):
                        last = pe.transpose(ps_t[j % 2][:, q, 0:P], xs[0:P, j, q * 128:(q + 1) * 128], k.ident[0:P, 0:P])
                    last.then_inc(turned, 1)
                pe.wait_ge(kept, i * G + G + 2)
                for c, (a, b) in enumerate(CUTS):
                    for h in range(HC):
                        pe.wait_ge(hid_made, i * H2 + c * HC + h + 1)
                        for q in range(2):
                            last = pe.matmul(ps_h[h % 4][:, 0:b - a], w1[:, q, h * 128:(h + 1) * 128], x_t[:, q, a:b],
                                             start=(q == 0), stop=(q == 1))
                        last.then_inc(hid_sum, 1)
                pe.wait_ge(hid_made, i * H2 + H2 + 4)
                for j in range(G):
                    for h in range(HC):
                        last = pe.matmul(ps_l[0:P, j, :], hid[:, h, j * P:(j + 1) * P], wg[:, h, :], start=(h == 0), stop=(h == HC - 1))
                    last.then_inc(logit_sum, 1)


_NAMES = ['x', 'src', 'dst', 'edge_attr_4', 'edge_attr_8', 'node_vec1', 'L0_gnn_eps', 'L0_gnn_W1', 'L0_gnn_b1',
          'L0_gnn_W2', 'L0_gnn_b2', 'L0_gnn_gamma', 'L0_gnn_beta', 'L0_ffn_gate_w', 'L0_ffn_gate_b', 'L0_ffn_w1',
          'L0_ffn_b1', 'L0_ffn_w2', 'L0_ffn_b2', 'L0_ffn_gamma', 'L0_ffn_beta', 'L1_gnn_sc_w0', 'L1_gnn_sc_w1',
          'L1_gnn_lin1_w0', 'L1_gnn_lin1_w1', 'L1_gnn_fc_w1', 'L1_gnn_fc_w2', 'L1_gnn_lin2_w00', 'L1_gnn_lin2_w01',
          'L1_gnn_lin2_w10', 'L1_gnn_lin2_w11', 'L1_ffn_W1', 'L1_ffn_b1', 'L1_ffn_Wg', 'L1_ffn_bg', 'L1_ffn_Wd',
          'L1_ffn_bd']


def build(nc, inputs, out, stop=99):
    k = Kept()
    (k.x, k.src, k.dst, k.edge_attr_4, k.edge_attr_8, k.node_vec1, k.L0_gnn_eps, k.L0_gnn_W1, k.L0_gnn_b1,
     k.L0_gnn_W2, k.L0_gnn_b2, k.L0_gnn_gamma, k.L0_gnn_beta, k.L0_ffn_gate_w, k.L0_ffn_gate_b, k.L0_ffn_w1,
     k.L0_ffn_b1, k.L0_ffn_w2, k.L0_ffn_b2, k.L0_ffn_gamma, k.L0_ffn_beta, k.L1_gnn_sc_w0, k.L1_gnn_sc_w1,
     k.L1_gnn_lin1_w0, k.L1_gnn_lin1_w1, k.L1_gnn_fc_w1, k.L1_gnn_fc_w2, k.L1_gnn_lin2_w00, k.L1_gnn_lin2_w01,
     k.L1_gnn_lin2_w10, k.L1_gnn_lin2_w11, k.L1_ffn_W1, k.L1_ffn_b1, k.L1_ffn_Wg, k.L1_ffn_bg, k.L1_ffn_Wd,
     k.L1_ffn_bd) = inputs
    Phase.spent.clear()
    with ExitStack() as ctx:
        def sb(name, shape, dt=F32):
            return ctx.enter_context(nc.sbuf_tensor(name, shape, dt))

        k.x_sb = sb("x_sb", [128, T, D])
        k.xn_sb = sb("xn_sb", [128, T, D])
        k.ident = sb("ident", [128, 128])
        k.below = sb("below", [128, VALS])
        k.tri = sb("tri", [128, 128], BF16)
        k.ones = sb("ones", [128, 128], BF16)
        k.onesf = sb("onesf", [128, 128])
        k.iota = sb("iota", [128, N])
        k.cols = sb("cols", [128, VEC_ROWS])
        k.gate_b = sb("gate_b", [128, 16])
        k.bg = sb("bg", [128, 8])
        k.gamma = sb("gamma", [128, D])
        k.beta = sb("beta", [128, D])
        k.eps = sb("eps", [128, 1])
        k.eps5 = sb("eps5", [128, 1])
        k.node_a = sb("node_a", [128, T])
        k.block_start = sb("block_start", [128, NEB], I32)
        k.block_tile = sb("block_tile", [128, NEB], I32)

        def dram(name, shape, dt=F32):
            return nc.dram_tensor(name, shape, dt, kind="Internal").ap()

        k.xn_dram = dram("xn_dram", [N, D])
        k.recs = dram("recs", [E + EB, REC])
        k.out = out
        k.y_dram = dram("y_dram", [N, D])

        load_inputs(nc, k)
        first_norm(nc, k)
        sort_edges(nc, k)
        with nc.sbuf_tensor("agg0", [128, T, D], F32) as k.agg:
            sum_neighbours(nc, k)
            gin_mlp(nc, k)
        if stop <= 1:
            return
        with ExitStack() as held:
            m = Experts(nc, held, "ffn0", 16, 2, 512, True)
            route_first(nc, k, m)
            pick_slots(nc, k, m)
            send_rows(nc, k, m)
            run_experts(nc, k, m, k.L0_ffn_w1, k.L0_ffn_w2, FFN0_B1, ACT.Relu)
            combine(nc, k, m, k.L0_ffn_b2, norm=True)
        if stop <= 2:
            return
        edge_table(nc, k)
        with nc.sbuf_tensor("agg1", [128, T, 2 * D], F32) as k.agg:
            sum_messages(nc, k)
            update_nodes(nc, k)
        if stop <= 3:
            return
        with ExitStack() as held:
            m = Experts(nc, held, "ffn1", 8, 1, 1024, False)
            route_second(nc, k, m)
            pick_slots(nc, k, m)
            send_rows(nc, k, m)
            run_experts(nc, k, m, k.L1_ffn_W1, k.L1_ffn_Wd, FFN1_B1, ACT.Gelu)
            combine(nc, k, m, k.L1_ffn_bd, norm=False)


def kernel(**inputs):
    import numpy as _np
    import concourse.bacc as _bacc
    from concourse import mybir as _mybir
    from concourse.bass_utils import run_bass_kernel_spmd as _run

    nc = _bacc.Bacc("TRN2", target_bir_lowering=False, num_devices=1)
    arrays, aps = {}, []
    for name in _NAMES:
        a = _np.ascontiguousarray(inputs[name])
        arrays[f"in_{name}"] = a
        aps.append(nc.dram_tensor(f"in_{name}", a.shape, _mybir.dt.from_np(a.dtype), kind="ExternalInput").ap())
    out = nc.dram_tensor("out_0", (N, D), F32, kind="ExternalOutput").ap()
    build(nc, aps, out)
    r = _run(nc, [arrays], core_ids=[0])
    return r.results[0]["out_0"]
```

```python
from contextlib import ExitStack
import math

import concourse.bass as bass
from concourse import mybir

N, D = 3125, 256
E = 53125
P = 125
T = N // P
G = 5
NG = T // G
W = G * P
CUTS = [(0, 313), (313, W)]

EC = E // P
ER = 25
EG = EC // ER
REC = 16
DST, SRC = 12, 13
EB = 256
NEB = (E + T * (EB - 1)) // EB
SLOTS = 8
NEB = -(-NEB // SLOTS) * SLOTS

TOK = 128
EPS = 1e-5
MAGIC = 12582912.0
VALS = 128 * 6 + 800
OFF = 128 * 6

MUL = 64
INV_MUL = 1.0 / math.sqrt(MUL)
SILU_NORM = 1.679
C_S, C_X = math.sin(math.pi / 8.0), math.cos(math.pi / 8.0)

F32, BF16, I32, U32 = mybir.dt.float32, mybir.dt.bfloat16, mybir.dt.int32, mybir.dt.uint32
ALU, ACT, AX = mybir.AluOpType, mybir.ActivationFunctionType, mybir.AxisListType
ds = bass.ds

GNN_B1, GNN_B2, GNN_GAMMA, GNN_BETA, FFN0_B1, FFN1_B1 = 0, 4, 6, 8, 10, 74
VEC_ROWS = 82


class Kept:
    pass


class Phase:

    spent = []

    def __init__(self, nc, name):
        self.nc, self.name, self.ctx, self.taken = nc, name, ExitStack(), []

    def __enter__(self):
        self.ctx.__enter__()
        return self

    def __exit__(self, *what):
        self.ctx.__exit__(*what)
        self.spent += self.taken
        if what[0] is None and len(self.spent) > 70:
            self.nc.clear_and_free_semaphores(list(self.spent))
            self.nc.all_engine_barrier()
            self.spent.clear()

    def sb(self, name, shape, dt=F32):
        return self.ctx.enter_context(self.nc.sbuf_tensor(f"{self.name}_{name}", shape, dt))

    def ps(self, name, shape, dt=F32):
        return self.ctx.enter_context(self.nc.psum_tensor(f"{self.name}_ps_{name}", shape, dt))

    def sem(self, name):
        self.taken.append(self.nc.alloc_semaphore(f"{self.name}_{name}"))
        return self.taken[-1]

    def sems(self, name, n):
        return [self.sem(f"{name}{j}") for j in range(n)]


def load_inputs(nc, k):
    with Phase(nc, "load") as ph:
        rows = ph.sb("rows", [VEC_ROWS, 128])
        iota_i = ph.sb("iota_i", [128, N], I32)
        ps_cols = ph.ps("cols", [128, 128])
        loaded, zeroed, made = ph.sem("loaded"), ph.sem("zeroed"), ph.sem("made")
        cols_ready, copied = ph.sem("cols_ready"), ph.sem("copied")
        block = ph.ctx.enter_context(nc.Block())
        count = 0

        @block.sync
        def _(sp):
            nonlocal count

            def load(dst, src):
                nonlocal count
                sp.dma_start(dst, src).then_inc(loaded, 16)
                count += 16

            def vec(row, a):
                n = a.shape[-1] // 128 if len(a.shape) == 1 else a.shape[0] * a.shape[1] // 128
                src = a.rearrange("(r c) -> r c", c=128) if len(a.shape) == 1 else a.rearrange("e (r c) -> (e r) c", c=128)
                load(rows[row:row + n, :], src)

            vec(GNN_B1, k.L0_gnn_b1)
            vec(GNN_B2, k.L0_gnn_b2)
            vec(GNN_GAMMA, k.L0_gnn_gamma)
            vec(GNN_BETA, k.L0_gnn_beta)
            vec(FFN0_B1, k.L0_ffn_b1)
            vec(FFN1_B1, k.L1_ffn_b1)
            load(k.x_sb[0:P, :, :], k.x.rearrange("(t p) d -> p t d", p=P))
            load(k.gate_b[:, :], k.L0_ffn_gate_b.partition_broadcast(128))
            load(k.bg[:, :], k.L1_ffn_bg.partition_broadcast(128))
            load(k.gamma[:, :], k.L0_ffn_gamma.partition_broadcast(128))
            load(k.beta[:, :], k.L0_ffn_beta.partition_broadcast(128))
            load(k.eps[:, :], k.L0_gnn_eps.partition_broadcast(128))
            with nc.allow_non_contiguous_dma(reason="3125 single words, once"):
                load(k.node_a[0:P, :], k.node_vec1.rearrange("(t p) o -> p (t o)", p=P))
            sp.wait_ge(loaded, count)

        @block.gpsimd
        def _(pool):
            pool.memset(k.ident[:, :], 0.0).then_inc(zeroed, 1)
            pool.memset(k.below[:, :], 1.0).then_inc(zeroed, 1)
            pool.memset(k.tri[:, :], 1.0).then_inc(zeroed, 1)
            pool.memset(k.ones[:, :], 1.0).then_inc(made, 1)
            pool.memset(k.onesf[:, :], 1.0).then_inc(made, 1)
            pool.iota(iota_i[:, :], pattern=[[1, N]], base=0, channel_multiplier=0).then_inc(made, 1)
            pool.wait_ge(zeroed, 3)
            pool.affine_select(out=k.ident[:, :], in_=k.ident[:, :], compare_op=ALU.not_equal, fill=1.0, base=0,
                               pattern=[[-1, 128]], channel_multiplier=1).then_inc(made, 1)
            pool.affine_select(out=k.below[:, :], in_=k.below[:, :], compare_op=ALU.is_gt, fill=0.0, base=-OFF,
                               pattern=[[1, VALS]], channel_multiplier=-1).then_inc(made, 1)
            pool.affine_select(out=k.tri[:, :], in_=k.tri[:, :], compare_op=ALU.is_gt, fill=0.0, base=0,
                               pattern=[[1, 128]], channel_multiplier=-1).then_inc(made, 1)

        @block.tensor
        def _(pe):
            pe.wait_ge(loaded, count)
            pe.wait_ge(made, 6)
            pe.transpose(ps_cols[:, 0:VEC_ROWS], rows[:, :], k.ident[0:VEC_ROWS, 0:VEC_ROWS]).then_inc(cols_ready, 1)

        @block.vector
        def _(dve):
            dve.memset(k.eps5[:, :], EPS).then_inc(copied, 1)
            dve.wait_ge(cols_ready, 1)
            dve.tensor_copy(k.cols[:, :], ps_cols[:, 0:VEC_ROWS]).then_inc(copied, 1)
            dve.wait_ge(made, 6)
            dve.tensor_copy(k.iota[:, :], iota_i[:, :]).then_inc(copied, 1)
            dve.wait_ge(loaded, count)
            dve.tensor_scalar(k.eps[:, :], k.eps[:, :], 1.0, None, ALU.add).then_inc(copied, 1)


def pass_on(eng, gate):
    eng.sem_inc(gate, 1)


class RowNorm:

    def __init__(self, ph):
        self.stats, self.mv = ph.sb("ln_stats", [128, T, 6]), ph.sb("ln_mv", [128, T, 2])
        self.std, self.rstd = ph.sb("ln_std", [128, T]), ph.sb("ln_rstd", [128, T])
        self.stats_done, self.mv_done = ph.sem("ln_stats_done"), ph.sem("ln_mv_done")
        self.std_done, self.rstd_done = ph.sem("ln_std_done"), ph.sem("ln_rstd_done")
        self.out_done = ph.sem("ln_out_done")


def norm_stats(dve, k, ln):
    with dve.Fori(0, NG) as i:
        for j in range(G):
            dve.bn_stats(row(ln.stats, i * G + j), row(k.x_sb, i * G + j)).then_inc(ln.stats_done, 1)
    dve.wait_ge(ln.stats_done, T)
    for t in range(T):
        dve.bn_aggr(ln.mv[0:P, t, :], ln.stats[0:P, t, :]).then_inc(ln.mv_done, 1)
    dve.wait_ge(ln.std_done, 1)
    dve.reciprocal(ln.rstd[0:P, :], ln.std[0:P, :]).then_inc(ln.rstd_done, 1)
    dve.wait_ge(ln.mv_done, T)
    dve.wait_ge(ln.rstd_done, 1)


def norm_root(act, k, ln):
    act.wait_ge(ln.mv_done, T)
    act.activation(ln.std[0:P, :], ln.mv[0:P, :, 1], ACT.Sqrt, bias=k.eps5[0:P, 0:1]).then_inc(ln.std_done, 1)


def norm_tile(dve, k, ln, tile, target):
    dve.tensor_scalar(target, row(k.x_sb, tile), row(ln.mv, tile, 0, 1), ln.rstd[0:P, ds(tile, 1)],
                      ALU.subtract, ALU.mult).then_inc(ln.out_done, 1)


class GroupNorm:

    def __init__(self, ph):
        self.stats, self.mv = ph.sb("ln_stats", [128, G, 6]), ph.sb("ln_mv", [128, G, 2])
        self.std, self.rstd = ph.sb("ln_std", [128, G]), ph.sb("ln_rstd", [128, G])
        self.stats_done, self.mv_done = ph.sem("ln_stats_done"), ph.sem("ln_mv_done")
        self.std_done, self.rstd_done = ph.sem("ln_std_done"), ph.sem("ln_rstd_done")
        self.out_done, self.gate = ph.sem("ln_out_done"), ph.sem("ln_gate")


def group_stats(dve, k, ln, i, first=False):
    for j in range(G):
        dve.bn_stats(ln.stats[0:P, j, :], row(k.x_sb, i * G + j)).then_inc(ln.stats_done, 1)
    dve.wait_ge(ln.stats_done, i * G + G)
    if not first:
        dve.wait_ge(ln.out_done, i * G)
    pass_on(dve, ln.gate)
    for j in range(G):
        dve.bn_aggr(ln.mv[0:P, j, :], ln.stats[0:P, j, :]).then_inc(ln.mv_done, 1)


def group_root(act, k, ln, i):
    act.wait_ge(ln.mv_done, i * G + G)
    act.activation(ln.std[0:P, :], ln.mv[0:P, :, 1], ACT.Sqrt, bias=k.eps5[0:P, 0:1]).then_inc(ln.std_done, 1)


def group_rstd(dve, ln, i):
    dve.wait_ge(ln.std_done, i + 1)
    dve.reciprocal(ln.rstd[0:P, :], ln.std[0:P, :]).then_inc(ln.rstd_done, 1)
    dve.wait_ge(ln.mv_done, i * G + G)
    dve.wait_ge(ln.rstd_done, i + 1)


def group_tile(dve, k, ln, i, j, target):
    dve.tensor_scalar(target, row(k.x_sb, i * G + j), ln.mv[0:P, j, 0:1], ln.rstd[0:P, j:j + 1],
                      ALU.subtract, ALU.mult).then_inc(ln.out_done, 1)


def first_norm(nc, k):
    with Phase(nc, "norm0") as ph:
        ln = RowNorm(ph)
        stored, gate = ph.sem("stored"), ph.sem("gate")
        block = ph.ctx.enter_context(nc.Block())

        @block.vector
        def _(dve):
            norm_stats(dve, k, ln)
            with dve.Fori(0, NG) as i:
                for j in range(G):
                    norm_tile(dve, k, ln, i * G + j, row(k.xn_sb, i * G + j))

        @block.scalar
        def _(act):
            norm_root(act, k, ln)

        @block.sync
        def _(sp):
            with sp.Fori(0, NG) as i:
                sp.wait_ge(ln.out_done, i * G + G)
                pass_on(sp, gate)
                sp.dma_start(k.xn_dram[ds(i * W, W), :].rearrange("(j p) d -> p j d", p=P), k.xn_sb[0:P, ds(i * G, G), :])\
                  .then_inc(stored, 16)
            sp.wait_ge(stored, 16 * NG)


def sort_edges(nc, k):
    with ExitStack() as held:
        def sb(name, shape, dt=F32):
            return held.enter_context(nc.sbuf_tensor(f"edges_{name}", shape, dt))

        e = Kept()
        e.rec = sb("rec", [128, EC, REC])
        e.onehot = sb("onehot", [128, ER, T, EG], BF16)
        e.cum = sb("cum", [128, ER + 1, T * EG], BF16)
        e.base = sb("base", [128, T * EG])
        e.unsorted = sb("unsorted", [128, 1], I32)
        count_edges(nc, k, e)
        place_edges(nc, k, e)


def count_edges(nc, k, e):
    BG = T * EG
    chunks = [(c, min(128, BG - c)) for c in range(0, BG, 128)]
    with Phase(nc, "count") as ph:
        dst_i, next_i, src_i = ph.sb("dst_i", [128, EC], I32), ph.sb("next_i", [128, EC], I32), ph.sb("src_i", [128, EC], I32)
        ea4, ea8 = ph.sb("ea4", [128, EC, 4]), ph.sb("ea8", [128, EC, 8])
        dst_f, next_f = ph.sb("dst_f", [128, EC]), ph.sb("next_f", [128, EC])
        tile_y, tile_f = ph.sb("tile_y", [128, EC]), ph.sb("tile_f", [128, EC])
        falls = ph.sb("falls", [128, 1])
        totals = ph.sb("totals", [128, len(chunks)])
        totals_b = ph.sb("totals_b", [128, len(chunks), 128])
        ps_tot = ph.ps("tot", [128, len(chunks)])
        ps_base = ph.ps("base", [128, BG])
        ps_falls = ph.ps("falls", [128, 1])

        dst_in, next_in, other_in = ph.sem("dst_in"), ph.sem("next_in"), ph.sem("other_in")
        step = ph.sem("step")
        next_set, falls_made, falls_sum = ph.sem("next_set"), ph.sem("falls_made"), ph.sem("falls_sum")
        cum_ready, tot_ready, totb_ready, base_ready = (ph.sem(f"{x}_ready") for x in ("cum", "tot", "totb", "base"))
        fields = ph.sem("fields")
        block = ph.ctx.enter_context(nc.Block())

        @block.sync
        def _(sp):
            sp.dma_start(dst_i[0:P, :], k.dst.rearrange("(p c) -> p c", p=P)).then_inc(dst_in, 16)
            sp.wait_ge(next_set, 1)
            last = (P - 1) * EC
            sp.dma_start(next_i[0:P - 1, :], k.dst[1:last + 1].rearrange("(p c) -> p c", c=EC)).then_inc(next_in, 16)
            sp.dma_start(next_i[P - 1:P, 0:EC - 1], k.dst[last + 1:E].rearrange("(p c) -> p c", p=1)).then_inc(next_in, 16)

        @block.scalar
        def _(act):
            act.dma_start(src_i[0:P, :], k.src.rearrange("(p c) -> p c", p=P)).then_inc(other_in, 16)
            act.dma_start(ea4[0:P, :, :], k.edge_attr_4.rearrange("(p c) w -> p c w", p=P)).then_inc(other_in, 16)
            act.dma_start(ea8[0:P, :, :], k.edge_attr_8.rearrange("(p c) w -> p c w", p=P)).then_inc(other_in, 16)
            act.wait_ge(other_in, 48)
            act.activation(e.rec[0:P, :, 0:8], ea8[0:P, :, :], ACT.Copy).then_inc(fields, 1)
            act.activation(e.rec[0:P, :, 8:12], ea4[0:P, :, :], ACT.Copy).then_inc(fields, 1)

        @block.gpsimd
        def _(pool):
            pool.memset(next_i[:, :], N).then_inc(next_set, 1)
            pool.memset(e.rec[0:P, :, SRC + 1:REC], 0.0).then_inc(fields, 1)

        @block.tensor
        def _(pe):
            pe.wait_ge(falls_made, 1)
            pe.matmul(ps_falls[:, :], k.onesf[0:P, :], falls[0:P, :], start=True, stop=True).then_inc(falls_sum, 1)
            pe.wait_ge(cum_ready, 1)
            for c, (at, n) in enumerate(chunks):
                last = pe.matmul(ps_tot[0:n, c:c + 1], e.cum[0:P, ER, at:at + n], k.ones[0:P, 0:1], start=True, stop=True)
            last.then_inc(tot_ready, 1)
            pe.wait_ge(totb_ready, len(chunks))
            for c, (at, n) in enumerate(chunks):
                last = pe.matmul(ps_base[:, :], totals_b[0:n, c, :], k.below[0:n, OFF - at:OFF - at + BG],
                                 start=(c == 0), stop=(c == len(chunks) - 1))
            last.then_inc(base_ready, 1)

        @block.vector
        def _(dve):
            done = [0]

            def chain(ins):
                done[0] += 1
                ins.then_inc(step, 1)
                dve.wait_ge(step, done[0])

            dve.wait_ge(dst_in, 16)
            chain(dve.tensor_copy(dst_f[0:P, :], dst_i[0:P, :]))
            chain(dve.tensor_scalar(tile_y[0:P, :], dst_f[0:P, :], 1.0 / P, 0.5 / P - 0.5, ALU.mult, ALU.add))
            chain(dve.tensor_scalar(tile_f[0:P, :], tile_y[0:P, :], MAGIC, None, ALU.add))
            chain(dve.tensor_scalar(tile_f[0:P, :], tile_f[0:P, :], MAGIC, None, ALU.subtract))
            view = tile_f[0:P, :].rearrange("p (g r) -> p r g", r=ER)
            chain(dve.memset(e.cum[0:P, 0, :], 0.0))
            for r in range(ER):
                dve.tensor_tensor(e.onehot[0:P, r, :, :], view[:, r, :].unsqueeze(1).to_broadcast([P, T, EG]),
                                  k.iota[0:P, 0:T].unsqueeze(2).to_broadcast([P, T, EG]), ALU.is_equal).then_inc(step, 1)
            done[0] += ER
            dve.wait_ge(next_in, 32)
            chain(dve.tensor_copy(next_f[0:P, :], next_i[0:P, :]))
            chain(dve.tensor_tensor(next_f[0:P, :], dst_f[0:P, :], next_f[0:P, :], ALU.is_gt))
            dve.tensor_reduce(falls[0:P, :], next_f[0:P, :], AX.X, ALU.add).then_inc(falls_made, 1)
            for r in range(ER):
                chain(dve.tensor_tensor(e.cum[0:P, r + 1, :], e.cum[0:P, r, :],
                                        e.onehot[0:P, r, :, :].rearrange("p t g -> p (t g)"), ALU.add))
            dve.sem_inc(cum_ready, 1)
            dve.wait_ge(falls_sum, 1)
            dve.tensor_copy(e.unsorted[:, :], ps_falls[:, :])
            dve.wait_ge(tot_ready, 1)
            for c, (at, n) in enumerate(chunks):
                chain(dve.tensor_copy(totals[0:n, c:c + 1], ps_tot[0:n, c:c + 1]))
                dve.tensor_copy(totals_b[0:n, c, :], totals[0:n, c:c + 1].to_broadcast([n, 128])).then_inc(totb_ready, 1)
            dve.tensor_copy(e.rec[0:P, :, DST], dst_f[0:P, :]).then_inc(fields, 1)
            dve.wait_ge(other_in, 48)
            dve.tensor_copy(e.rec[0:P, :, SRC].bitcast(I32), src_i[0:P, :]).then_inc(fields, 1)
            dve.wait_ge(base_ready, 1)
            dve.tensor_copy(e.base[:, :], ps_base[:, :])


def place_edges(nc, k, e):
    BG = T * EG
    with Phase(nc, "place") as ph:
        tail = ph.sb("tail", [128, 2 * REC])
        sel = ph.sb("sel", [128, 2, BG])
        pos_f, pos_i = ph.sb("pos_f", [128, EG, ER]), ph.sb("pos_i", [128, EC], I32)
        row_st, idx_st = ph.sb("row_st", [128, G, REC]), ph.sb("idx_st", [128, G], I32)
        start_b, count_b = ph.sb("start_b", [128, T + 1]), ph.sb("count_b", [128, T])
        blk_y, blk_n = ph.sb("blk_y", [128, T]), ph.sb("blk_n", [128, T])
        blk_end = ph.sb("blk_end", [128, 2, T])
        shift, dshift = ph.sb("shift", [128, T]), ph.sb("dshift", [128, T])
        NC = -(-NEB // 128)
        number, cmp = ph.sb("number", [128, NC]), ph.sb("cmp", [128, NC, T])
        blk_f, blk_s, blk_t = ph.sb("blk_f", [128, NC]), ph.sb("blk_s", [128, NC]), ph.sb("blk_t", [128, 2, NC])
        ps_number, ps_table = ph.ps("number", [128, NC]), ph.ps("table", [1, 2, NC * 128])
        number_ready, columns_made, table_ready = ph.sem("number_ready"), ph.sem("columns_made"), ph.sem("table_ready")
        ps_rank = [ph.ps(f"rank{s}", [128, BG]) for s in range(2)]
        step, rank_step = ph.sem("step"), ph.sem("rank_step")
        rank_ready, rank_read, staged = ph.sem("rank_ready"), ph.sem("rank_read"), ph.sem("staged")
        scattered = ph.sems("scattered", G)
        tail_made, stored, tail_stored, gate = ph.sem("tail_made"), ph.sem("stored"), ph.sem("tail_stored"), ph.sem("gate")
        block = ph.ctx.enter_context(nc.Block())

        @block.sync
        def _(sp):
            unsorted = sp.value_load(e.unsorted[0:1, 0:1], min_val=0, max_val=E)
            with sp.If(unsorted == 0):
                sp.dma_start(k.recs[0:E, :].rearrange("(p c) w -> p c w", p=P), e.rec[0:P, :, :]).then_inc(stored, 16)
                sp.wait_ge(stored, 16)
            sp.wait_ge(tail_made, 2)
            sp.dma_start(k.recs[E:E + EB, :].rearrange("(p u) w -> p (u w)", u=2), tail[:, :]).then_inc(tail_stored, 16)
            sp.wait_ge(tail_stored, 16)

        @block.tensor
        def _(pe):
            for c in range(NC):
                last = pe.matmul(ps_number[:, c:c + 1], k.iota[0:1, c * 128:(c + 1) * 128], k.onesf[0:1, 0:1], start=True, stop=True)
            last.then_inc(number_ready, 1)
            unsorted = pe.value_load(e.unsorted[0:1, 0:1], min_val=0, max_val=E)
            with pe.If(unsorted != 0):
                for r in range(ER):
                    if r >= 2:
                        pe.wait_ge(rank_read, r - 1)
                    pe.matmul(ps_rank[r % 2][0:P, :], k.onesf[0:1, 0:P], e.base[0:1, :], start=True, stop=False)
                    pe.matmul(ps_rank[r % 2][0:P, :], k.tri[0:P, 0:P], e.onehot[0:P, r, :, :].rearrange("p t g -> p (t g)"),
                              start=False, stop=False)
                    pe.matmul(ps_rank[r % 2][0:P, :], k.ones[0:P, 0:P], e.cum[0:P, r, :], start=False,
                              stop=True).then_inc(rank_ready, 1)
            pe.wait_ge(columns_made, 2)
            for q in range(2):
                for c in range(NC):
                    last = pe.matmul(ps_table[:, q, c * 128:(c + 1) * 128], blk_t[:, q, c:c + 1], k.ident[:, :], start=True, stop=True)
            last.then_inc(table_ready, 1)

        @block.gpsimd
        def _(pool):
            pool.memset(tail[:, :], 0.0).then_inc(tail_made, 1)
            pool.wait_ge(tail_made, 1)
            pool.memset(tail[:, :].rearrange("p (u w) -> p u w", w=REC)[:, :, DST], -1.0).then_inc(tail_made, 1)
            unsorted = pool.value_load(e.unsorted[0:1, 0:1], min_val=0, max_val=E)
            with pool.If(unsorted != 0):
                with pool.Fori(0, EC // G) as i:
                    for j in range(G):
                        pool.wait_ge(staged, i * 2 * G + 2 * j + 2)
                        pass_on(pool, gate)
                        pool.indirect_dma_start(k.recs, bass.IndirectOffsetOnAxis(ap=idx_st[0:P, j:j + 1].bitcast(U32), axis=0),
                                                row_st[0:P, j, :], None).then_inc(scattered[j], 16)
                for j in range(G):
                    pool.wait_ge(scattered[j], (EC // G) * 16)

        @block.vector
        def _(dve):
            unsorted = dve.value_load(e.unsorted[0:1, 0:1], min_val=0, max_val=E)
            with dve.If(unsorted != 0):
                for r in range(ER):
                    dve.wait_ge(rank_ready, r + 1)
                    s = sel[0:P, r % 2, :]
                    dve.tensor_tensor(s, ps_rank[r % 2][0:P, :], e.onehot[0:P, r, :, :].rearrange("p t g -> p (t g)"), ALU.mult)\
                       .then_inc(rank_read, 1)
                    dve.wait_ge(rank_read, r + 1)
                    dve.tensor_reduce(pos_f[0:P, :, r], s.rearrange("p (t g) -> p g t", g=EG), AX.X, ALU.add).then_inc(rank_step, 1)
                dve.wait_ge(rank_step, ER)
                dve.tensor_copy(pos_i[0:P, :], pos_f[0:P, :, :].rearrange("p g r -> p (g r)")).then_inc(rank_step, 1)
                dve.wait_ge(rank_step, ER + 1)

                def stage(i, first=False):
                    for j in range(G):
                        if not first:
                            dve.wait_ge(scattered[j], i * 16)
                            pass_on(dve, gate)
                        dve.tensor_copy(row_st[0:P, j, :], row(e.rec, i * G + j)).then_inc(staged, 1)
                        dve.tensor_copy(idx_st[0:P, j:j + 1], pos_i[0:P, ds(i * G + j, 1)]).then_inc(staged, 1)

                stage(0, first=True)
                with dve.Fori(1, EC // G) as i:
                    stage(i)

            done = [0]

            def chain(ins):
                done[0] += 1
                ins.then_inc(step, 1)
                dve.wait_ge(step, done[0])

            first = e.base[:, :].rearrange("p (t g) -> p t g", g=EG)[:, :, 0]
            chain(dve.tensor_copy(start_b[:, 0:T], first))
            chain(dve.memset(start_b[:, T:T + 1], float(E)))
            chain(dve.tensor_tensor(count_b[:, :], start_b[:, 1:T + 1], start_b[:, 0:T], ALU.subtract))
            chain(dve.tensor_scalar(blk_y[:, :], count_b[:, :], 1.0 / EB, (EB - 1) / EB - 0.5 + 0.5 / EB, ALU.mult, ALU.add))
            chain(dve.tensor_scalar(blk_y[:, :], blk_y[:, :], MAGIC, None, ALU.add))
            chain(dve.tensor_scalar(blk_n[:, :], blk_y[:, :], MAGIC, None, ALU.subtract))
            chain(dve.tensor_copy(blk_end[:, 0, :], blk_n[:, :]))
            side, gap = 0, 1
            while gap < T:
                chain(dve.tensor_copy(blk_end[:, 1 - side, 0:gap], blk_end[:, side, 0:gap]))
                chain(dve.tensor_tensor(blk_end[:, 1 - side, gap:T], blk_end[:, side, gap:T], blk_end[:, side, 0:T - gap], ALU.add))
                side, gap = 1 - side, 2 * gap
            end = blk_end[:, side, :]
            chain(dve.tensor_tensor(shift[:, :], end, blk_n[:, :], ALU.subtract))
            chain(dve.scalar_tensor_tensor(shift[:, :], shift[:, :], float(-EB), start_b[:, 0:T], ALU.mult, ALU.add))
            chain(dve.memset(dshift[:, :], 0.0))
            chain(dve.tensor_tensor(dshift[:, 0:T - 1], shift[:, 1:T], shift[:, 0:T - 1], ALU.subtract))
            dve.wait_ge(number_ready, 1)
            chain(dve.tensor_copy(number[:, :], ps_number[:, :]))
            chain(dve.tensor_tensor(cmp[:, :, :], number[:, :].unsqueeze(2).to_broadcast([128, NC, T]),
                                    end.unsqueeze(1).to_broadcast([128, NC, T]), ALU.is_ge))
            chain(dve.tensor_reduce(blk_f[:, :], cmp[:, :, :], AX.X, ALU.add))
            chain(dve.tensor_tensor(cmp[:, :, :], cmp[:, :, :], dshift[:, :].unsqueeze(1).to_broadcast([128, NC, T]), ALU.mult))
            chain(dve.tensor_reduce(blk_s[:, :], cmp[:, :, :], AX.X, ALU.add))
            chain(dve.scalar_tensor_tensor(blk_s[:, :], number[:, :], float(EB), blk_s[:, :], ALU.mult, ALU.add))
            dve.tensor_scalar(blk_t[:, 0, :], blk_s[:, :], float(E), None, ALU.min).then_inc(columns_made, 1)
            dve.tensor_scalar(blk_t[:, 1, :], blk_f[:, :], float(T - 1), None, ALU.min).then_inc(columns_made, 1)
            dve.wait_ge(table_ready, 1)
            dve.tensor_copy(k.block_start[0:1, :], ps_table[:, 0, 0:NEB])
            dve.tensor_copy(k.block_tile[0:1, :], ps_table[:, 1, 0:NEB])


def row(buf, at, lo=0, hi=None, parts=P):
    return buf[0:parts, ds(at, 1), lo:hi].rearrange("p o d -> p (o d)")


def node_ids(k, tile):
    return k.iota[:, ds(tile * P, P)].unsqueeze(1).to_broadcast([128, 2, P])


def sum_neighbours(nc, k):
    with Phase(nc, "sum") as ph:
        rec = [ph.sb(f"rec{s}", [128, 2, REC]) for s in range(SLOTS)]
        got = [[ph.sb(f"got{s}{u}", [128, D]) for u in range(2)] for s in range(SLOTS)]
        onehot = [ph.sb(f"onehot{s}", [128, 2, P]) for s in range(SLOTS)]
        ps_sum = [ph.ps(f"sum{s}", [128, D]) for s in range(SLOTS)]
        rec_in, got_in = ph.sems("rec_in", SLOTS), ph.sems("got_in", SLOTS)
        summed, added = ph.sem("summed"), ph.sem("added")
        masked, gate = ph.sem("masked"), ph.sem("gate")
        block = ph.ctx.enter_context(nc.Block())

        @block.sync
        def _(sp):
            sp.sem_inc(summed, SLOTS)
            with sp.Fori(0, NEB // SLOTS) as i:
                for s in range(SLOTS):
                    n = i * SLOTS + s
                    start = sp.value_load(k.block_start[0:1, ds(n, 1)], min_val=0, max_val=E)
                    sp.wait_ge(summed, n + 1)
                    pass_on(sp, gate)
                    sp.dma_start(rec[s][:, :, :], k.recs[ds(start, EB), :].rearrange("(p u) w -> p u w", u=2))\
                      .then_inc(rec_in[s], 16)

        @block.gpsimd
        def _(pool):
            with pool.Fori(0, NEB // SLOTS) as i:
                for s in range(SLOTS):
                    pool.wait_ge(rec_in[s], i * 16 + 16)
                    pass_on(pool, gate)
                    for u in range(2):
                        pool.indirect_dma_start(
                            got[s][u][:, :], None, k.xn_dram,
                            bass.IndirectOffsetOnAxis(ap=rec[s][:, u, SRC:SRC + 1].bitcast(U32), axis=0)).then_inc(got_in[s], 16)

        @block.tensor
        def _(pe):
            with pe.Fori(0, NEB // SLOTS) as i:
                for s in range(SLOTS):
                    n = i * SLOTS + s
                    pe.wait_ge(added, n + 1)
                    pe.wait_ge(masked, n + 1)
                    pe.wait_ge(got_in[s], i * 32 + 32)
                    for u in range(2):
                        last = pe.matmul(ps_sum[s][0:P, :], onehot[s][:, u, :], got[s][u][:, :], start=(u == 0), stop=(u == 1))
                    last.then_inc(summed, 1)

        @block.vector
        def _(dve):
            dve.memset(k.agg[:, :, 0:D], 0.0).then_inc(added, SLOTS)

            def tile_of(n):
                return dve.value_load(k.block_tile[0:1, ds(n, 1)], min_val=0, max_val=T - 1)

            def add_sum(n, s, tile):
                dve.wait_ge(summed, n + 1 + SLOTS)
                dve.wait_ge(added, n + SLOTS)
                dve.tensor_tensor(row(k.agg, tile, 0, D), ps_sum[s][0:P, :], row(k.agg, tile, 0, D), ALU.add)\
                   .then_inc(added, 1)

            def turn(i, first=False):
                tile_before = None if first else tile_of(i * SLOTS - 1)
                for s in range(SLOTS):
                    n = i * SLOTS + s
                    tile = tile_of(n)
                    dve.wait_ge(rec_in[s], i * 16 + 16)
                    dve.tensor_tensor(onehot[s][:, :, :], node_ids(k, tile), rec[s][:, :, DST:DST + 1].to_broadcast([128, 2, P]),
                                      ALU.is_equal).then_inc(masked, 1)
                    if not first or s >= 1:
                        add_sum(n - 1, (s - 1) % SLOTS, tile_before)
                    tile_before = tile

            turn(0, first=True)
            with dve.Fori(1, NEB // SLOTS) as i:
                turn(i)
            add_sum(NEB - 1, SLOTS - 1, tile_of(NEB - 1))


def gin_mlp(nc, k):
    HID = 512
    HC = HID // 128
    with Phase(nc, "gin") as ph:
        w1, w2 = ph.sb("w1", [128, 2, HID]), ph.sb("w2", [128, HC, D])
        h = ph.sb("h", [128, G, D])
        h_t = ph.sb("h_t", [128, 2, W])
        hid = ph.sb("hid", [128, HC, W])
        h2 = ph.sb("h2", [128, 2, NG, W])
        stats = ph.sb("stats", [128, 2, 2 * NG, 6])
        mv, std, rstd = ph.sb("mv", [128, 2, 2]), ph.sb("std", [128, 2]), ph.sb("rstd", [128, 2])
        scale, shift = ph.sb("scale", [128, 2]), ph.sb("shift", [128, 2])
        bn = ph.sb("bn", [128, G, 2, P])
        ps_t = [ph.ps(f"t{s}", [128, 2, 128]) for s in range(2)]
        ps_h = [ph.ps(f"h{s}", [128, 512]) for s in range(4)]
        ps_o = [ph.ps(f"o{s}", [128, 512]) for s in range(2)]
        back = ps_h
        zeros, zero_made, zero_stored = ph.sb("zeros", [128, 4, D]), ph.sem("zero_made"), ph.sem("zero_stored")
        w_in = ph.sem("w_in")
        h_made, turned, kept = ph.sem("h_made"), ph.sem("turned"), ph.sem("kept")
        hid_sum, hid_made, out_sum, out_made = ph.sem("hid_sum"), ph.sem("hid_made"), ph.sem("out_sum"), ph.sem("out_made")
        step, bn_std, bn_ready = ph.sem("step"), ph.sem("bn_std"), ph.sem("bn_ready")
        bn_made, bn_turned, x_made, gate = ph.sem("bn_made"), ph.sem("bn_turned"), ph.sem("x_made"), ph.sem("gate")
        block = ph.ctx.enter_context(nc.Block())

        @block.sync
        def _(sp):
            sp.dma_start(w1[:, :, :], k.L0_gnn_W1.rearrange("(c p) h -> p c h", p=128)).then_inc(w_in, 16)
            sp.dma_start(w2[:, :, :], k.L0_gnn_W2.rearrange("(c p) h -> p c h", p=128)).then_inc(w_in, 16)

            sp.wait_ge(zero_made, 1)
            stores = 0
            for rows in (k.rows0, k.rows1):
                for at in range(0, rows.shape[0], 4 * TOK):
                    sp.dma_start(rows[at:at + 4 * TOK, :].rearrange("(p c) d -> p c d", c=4), zeros[:, :, :]).then_inc(zero_stored, 16)
                    stores += 16
            sp.wait_ge(zero_stored, stores)

        @block.gpsimd
        def _(pool):
            pool.memset(zeros[:, :, :], 0.0).then_inc(zero_made, 1)

        @block.vector
        def _(dve):
            def start_rows(i, first=False):
                for j in range(G):
                    if not first:
                        dve.wait_ge(turned, i * G + j - G + 1)
                        pass_on(dve, gate)
                    dve.scalar_tensor_tensor(h[0:P, j, :], row(k.xn_sb, i * G + j), k.eps[0:P, 0:1], row(k.agg, i * G + j, 0, D),
                                             ALU.mult, ALU.add).then_inc(h_made, 1)

            def statistics(i):
                for c, (a, b) in enumerate(CUTS):
                    for m in range(2):
                        dve.wait_ge(out_made, i * 4 + 2 * c + m + 1)
                        pass_on(dve, gate)
                        dve.bn_stats(stats[:, m, ds(i * 2 + c, 1), :].rearrange("p o w -> p (o w)"),
                                     h2[:, m, ds(i, 1), a:b].rearrange("p o w -> p (o w)")).then_inc(step, 1)

            start_rows(0, first=True)
            with dve.Fori(1, NG) as i:
                start_rows(i)
                statistics(i - 1)
            statistics(NG - 1)
            done = [4 * NG]

            def chain(ins):
                done[0] += 1
                ins.then_inc(step, 1)
                dve.wait_ge(step, done[0])

            dve.wait_ge(step, done[0])
            for m in range(2):
                chain(dve.bn_aggr(mv[:, m, :], stats[:, m, :, :].rearrange("p n w -> p (n w)")))
            dve.wait_ge(bn_std, 1)
            chain(dve.reciprocal(rstd[:, :], std[:, :]))
            chain(dve.tensor_tensor(scale[:, :], rstd[:, :], k.cols[:, GNN_GAMMA:GNN_GAMMA + 2], ALU.mult))
            chain(dve.tensor_tensor(shift[:, :], mv[:, :, 0], scale[:, :], ALU.mult))
            dve.tensor_tensor(shift[:, :], k.cols[:, GNN_BETA:GNN_BETA + 2], shift[:, :], ALU.subtract).then_inc(bn_ready, 1)
            with dve.Fori(0, NG) as i:
                for j in range(G):
                    dve.wait_ge(bn_turned, i * G + j + 1)
                    pass_on(dve, gate)
                    dve.tensor_tensor(row(k.x_sb, i * G + j), back[j % 4][0:P, 0:D], row(k.x_sb, i * G + j), ALU.add).then_inc(x_made, 1)

        @block.scalar
        def _(act):
            def keep_turned(i):
                for j in range(G):
                    act.wait_ge(turned, i * G + j + 1)
                    act.activation(h_t[:, :, j * P:(j + 1) * P], ps_t[j % 2][:, :, 0:P], ACT.Copy).then_inc(kept, 1)

            def keep_hidden(i):
                for c, (a, b) in enumerate(CUTS):
                    for m in range(HC):
                        act.wait_ge(hid_sum, i * 2 * HC + c * HC + m + 1)
                        act.activation(hid[:, m, a:b], ps_h[m][:, 0:b - a], ACT.Relu,
                                       bias=k.cols[:, GNN_B1 + m:GNN_B1 + m + 1]).then_inc(hid_made, 1)

            def keep_out(i):
                for c, (a, b) in enumerate(CUTS):
                    for m in range(2):
                        act.wait_ge(out_sum, i * 4 + 2 * c + m + 1)
                        pass_on(act, gate)
                        act.activation(h2[:, m, ds(i, 1), a:b].rearrange("p o w -> p (o w)"), ps_o[m][:, 0:b - a],
                                       ACT.Identity, bias=k.cols[:, GNN_B2 + m:GNN_B2 + m + 1]).then_inc(out_made, 1)

            keep_turned(0)
            keep_hidden(0)
            with act.Fori(1, NG) as i:
                keep_turned(i)
                keep_out(i - 1)
                keep_hidden(i)
            keep_out(NG - 1)
            act.wait_ge(step, 4 * NG + 2)
            act.activation(std[:, :], mv[:, :, 1], ACT.Sqrt, bias=k.eps5[:, 0:1]).then_inc(bn_std, 1)
            act.wait_ge(bn_ready, 1)

            def normalise(i, first=False):
                for j in range(G):
                    if not first:
                        act.wait_ge(bn_turned, i * G + j - G + 1)
                        pass_on(act, gate)
                    for m in range(2):
                        last = act.activation(bn[:, j, m, :], h2[:, m, ds(i, 1), j * P:(j + 1) * P].rearrange("p o w -> p (o w)"),
                                              ACT.Identity, bias=shift[:, m:m + 1], scale=scale[:, m:m + 1])
                    last.then_inc(bn_made, 1)

            normalise(0, first=True)
            with act.Fori(1, NG) as i:
                normalise(i)

        @block.tensor
        def _(pe):
            pe.wait_ge(w_in, 32)

            def transposes(i, first=False):
                for j in range(G):
                    pe.wait_ge(h_made, i * G + j + 1)
                    if not first or j >= 2:
                        pe.wait_ge(kept, i * G + (j - 1 if j >= 2 else 0))
                    for m in range(2):
                        last = pe.transpose(ps_t[j % 2][:, m, 0:P], h[0:P, j, m * 128:(m + 1) * 128], k.ident[0:P, 0:P])
                    last.then_inc(turned, 1)

            def hidden(i):
                pe.wait_ge(kept, i * G + G)
                for c, (a, b) in enumerate(CUTS):
                    for m in range(HC):
                        if c:
                            pe.wait_ge(hid_made, i * 2 * HC + m + 1)
                        for q in range(2):
                            last = pe.matmul(ps_h[m][:, 0:b - a], w1[:, q, m * 128:(m + 1) * 128], h_t[:, q, a:b],
                                             start=(q == 0), stop=(q == 1))
                        last.then_inc(hid_sum, 1)

            def outputs(i, first=False):
                pe.wait_ge(hid_made, i * 2 * HC + 2 * HC)
                for c, (a, b) in enumerate(CUTS):
                    for m in range(2):
                        if c or not first:
                            pe.wait_ge(out_made, i * 4 + 2 * c + m - 1)
                        for q in range(HC):
                            last = pe.matmul(ps_o[m][:, 0:b - a], w2[:, q, m * 128:(m + 1) * 128], hid[:, q, a:b],
                                             start=(q == 0), stop=(q == HC - 1))
                        last.then_inc(out_sum, 1)

            def transposes_back(i, first=False):
                for j in range(G):
                    pe.wait_ge(bn_made, i * G + j + 1)
                    if j == 4:
                        pe.wait_ge(x_made, i * G + 1)
                    elif not first:
                        pe.wait_ge(x_made, i * G)
                    for m in range(2):
                        last = pe.transpose(back[j % 4][0:P, m * 128:(m + 1) * 128], bn[:, j, m, :], k.ident[:, :])
                    last.then_inc(bn_turned, 1)

            transposes(0, first=True)
            hidden(0)
            transposes(1)
            outputs(0, first=True)
            hidden(1)
            with pe.Fori(2, NG) as i:
                transposes(i)
                outputs(i - 1)
                hidden(i)
            outputs(NG - 1)
            transposes_back(0, first=True)
            with pe.Fori(1, NG) as i:
                transposes_back(i)


def expert_blocks(n, picks):
    blocks = (N * picks + n * (TOK - 1)) // TOK
    return blocks + -blocks % 4


class Experts:

    def __init__(self, nc, ctx, name, rows, n, picks, hid, own_w1):
        self.name, self.n, self.picks, self.hid, self.own_w1 = name, n, picks, hid, own_w1
        self.cols = T * picks
        self.blocks = expert_blocks(n, picks)

        def sb(what, shape, dt=F32):
            return ctx.enter_context(nc.sbuf_tensor(f"{name}_{what}", shape, dt))

        self.onehot = sb("onehot", [128, n, self.cols], BF16)
        self.prob = sb("prob", [128, self.cols])
        self.slot_i = sb("slot_i", [128, self.cols], I32)
        self.block_expert = sb("block_expert", [128, self.blocks], I32)
        self.rows = rows
        self.results = nc.dram_tensor(f"{name}_results", [self.blocks * TOK, D], F32, kind="Internal").ap()


def pick_slots(nc, k, m):
    n, cols = m.n, m.cols
    width = n * cols
    cuts = [(a, min(a + 400, width)) for a in range(0, width, 400)]
    chunks = [(c, min(128, width - c)) for c in range(0, width, 128)]
    with Phase(nc, f"{m.name}_slots") as ph:
        totals = ph.sb("totals", [128, len(chunks)])
        totals_b = ph.sb("totals_b", [128, len(chunks), 128])
        base, rank = ph.sb("base", [128, n, cols]), ph.sb("rank", [128, n, cols])
        start_e, count_e = ph.sb("start_e", [128, n + 1]), ph.sb("count_e", [128, n])
        blk_n, blk_end = ph.sb("blk_n", [128, n]), ph.sb("blk_end", [128, 2, n])
        pad = ph.sb("pad", [128, n])
        cmp, blk_f = ph.sb("cmp", [128, m.blocks, n]), ph.sb("blk_f", [128, m.blocks])
        slot_f = ph.sb("slot_f", [128, cols])
        ps_tot = ph.ps("tot", [128, len(chunks)])
        ps_base = [ph.ps(f"base{c}", [128, 400]) for c in range(len(cuts))]
        ps_rank = [ph.ps(f"rank{c}", [128, 400]) for c in range(len(cuts))]
        tot_ready, totb_ready, base_ready, rank_ready = (ph.sem(f"{x}_ready") for x in ("tot", "totb", "base", "rank"))
        step = ph.sem("step")
        block = ph.ctx.enter_context(nc.Block())
        flat = m.onehot[:, :, :].rearrange("p e c -> p (e c)")

        @block.tensor
        def _(pe):
            for c, (at, w) in enumerate(chunks):
                last = pe.matmul(ps_tot[0:w, c:c + 1], flat[0:P, at:at + w], k.ones[0:P, 0:1], start=True, stop=True)
            last.then_inc(tot_ready, 1)
            for c, (a, b) in enumerate(cuts):
                last = pe.matmul(ps_rank[c][0:P, 0:b - a], k.tri[0:P, 0:P], flat[0:P, a:b], start=True, stop=True)
            last.then_inc(rank_ready, 1)
            pe.wait_ge(totb_ready, len(chunks))
            for c, (a, b) in enumerate(cuts):
                for q, (at, w) in enumerate(chunks):
                    last = pe.matmul(ps_base[c][:, 0:b - a], totals_b[0:w, q, :], k.below[0:w, OFF - at + a:OFF - at + b],
                                     start=(q == 0), stop=(q == len(chunks) - 1))
            last.then_inc(base_ready, 1)

        @block.vector
        def _(dve):
            done = [0]

            def chain(ins):
                done[0] += 1
                ins.then_inc(step, 1)
                dve.wait_ge(step, done[0])

            dve.wait_ge(tot_ready, 1)
            for c, (at, w) in enumerate(chunks):
                chain(dve.tensor_copy(totals[0:w, c:c + 1], ps_tot[0:w, c:c + 1]))
                dve.tensor_copy(totals_b[0:w, c, :], totals[0:w, c:c + 1].to_broadcast([w, 128])).then_inc(totb_ready, 1)
            dve.wait_ge(base_ready, 1)
            flat_base, flat_rank = (x[:, :, :].rearrange("p e c -> p (e c)") for x in (base, rank))
            for c, (a, b) in enumerate(cuts):
                chain(dve.tensor_copy(flat_base[:, a:b], ps_base[c][:, 0:b - a]))
            chain(dve.tensor_copy(start_e[:, 0:n], base[:, :, 0]))
            chain(dve.memset(start_e[:, n:n + 1], float(N * m.picks)))
            chain(dve.tensor_tensor(count_e[:, :], start_e[:, 1:n + 1], start_e[:, 0:n], ALU.subtract))
            chain(dve.tensor_scalar(blk_n[:, :], count_e[:, :], 1.0 / TOK, (TOK - 1) / TOK - 0.5 + 0.5 / TOK, ALU.mult, ALU.add))
            chain(dve.tensor_scalar(blk_n[:, :], blk_n[:, :], MAGIC, None, ALU.add))
            chain(dve.tensor_scalar(blk_n[:, :], blk_n[:, :], MAGIC, None, ALU.subtract))
            chain(dve.tensor_copy(blk_end[:, 0, :], blk_n[:, :]))
            side, gap = 0, 1
            while gap < n:
                chain(dve.tensor_copy(blk_end[:, 1 - side, 0:gap], blk_end[:, side, 0:gap]))
                chain(dve.tensor_tensor(blk_end[:, 1 - side, gap:n], blk_end[:, side, gap:n], blk_end[:, side, 0:n - gap], ALU.add))
                side, gap = 1 - side, 2 * gap
            end = blk_end[:, side, :]
            chain(dve.tensor_tensor(pad[:, :], end, blk_n[:, :], ALU.subtract))
            chain(dve.scalar_tensor_tensor(pad[:, :], pad[:, :], float(TOK), start_e[:, 0:n], ALU.mult, ALU.subtract))
            chain(dve.tensor_tensor(base[:, :, :], base[:, :, :], pad[:, :].unsqueeze(2).to_broadcast([128, n, cols]), ALU.add))
            dve.wait_ge(rank_ready, 1)
            for c, (a, b) in enumerate(cuts):
                chain(dve.tensor_tensor(flat_rank[0:P, a:b], ps_rank[c][0:P, 0:b - a], flat_base[0:P, a:b], ALU.add))
            chain(dve.tensor_tensor(flat_rank[0:P, :], flat_rank[0:P, :], flat[0:P, :], ALU.mult))
            chain(dve.tensor_reduce(slot_f[0:P, :], rank[0:P, :, :].rearrange("p e c -> p c e"), AX.X, ALU.add))
            chain(dve.tensor_copy(m.slot_i[0:P, :], slot_f[0:P, :]))
            chain(dve.tensor_tensor(cmp[:, :, :], k.iota[:, 0:m.blocks].unsqueeze(2).to_broadcast([128, m.blocks, n]),
                                    end.unsqueeze(1).to_broadcast([128, m.blocks, n]), ALU.is_ge))
            chain(dve.tensor_reduce(blk_f[:, :], cmp[:, :, :], AX.X, ALU.add))
            chain(dve.tensor_scalar(blk_f[:, :], blk_f[:, :], float(n - 1), None, ALU.min))
            chain(dve.tensor_copy(m.block_expert[:, :], blk_f[:, :]))


def send_rows(nc, k, m, bias_dram, base, target, beta=None):
    K = m.picks
    with Phase(nc, f"{m.name}_send") as ph:
        bias = ph.sb("bias", [m.n, D])
        mix, mix_w = ph.sb("mix", [128, G, m.n, K]), ph.sb("mix_w", [128, G, m.n])
        mix_t = ph.sb("mix_t", [m.n, G, P])
        ps_m = [ph.ps(f"m{b}", [128, 128]) for b in range(2)]
        ps_b = [ph.ps(f"b{j}", [128, D]) for j in range(G)]
        gate, bias_in, sent = ph.sem("gate"), ph.sem("bias_in"), ph.sem("sent")
        mix_made, mixed, mix_turned, mix_kept, bias_sum, based = (
            ph.sem(x) for x in ("mix_made", "mixed", "mix_turned", "mix_kept", "bias_sum", "based"))
        block = ph.ctx.enter_context(nc.Block())

        @block.sync
        def _(sp):
            sp.dma_start(bias[:, :], bias_dram).then_inc(bias_in, 16)

        @block.vector
        def _(dve):
            def add_biases(i):
                for j in range(G):
                    dve.wait_ge(bias_sum, i * G + j + 1)
                    pass_on(dve, gate)
                    dve.tensor_tensor(row(target, i * G + j), ps_b[j][0:P, :], row(base, i * G + j), ALU.add).then_inc(based, 1)

            def turn(i, first=False):
                if not first:
                    dve.wait_ge(mix_turned, i * G)
                for j in range(G):
                    cols = ds((i * G + j) * K, K)
                    dve.tensor_tensor(mix[0:P, j, :, :], m.onehot[0:P, :, cols],
                                      m.prob[0:P, cols].unsqueeze(1).to_broadcast([P, m.n, K]), ALU.mult).then_inc(mix_made, 1)
                dve.wait_ge(mix_made, i * G + G)
                pass_on(dve, gate)
                for j in range(G):
                    dve.tensor_reduce(mix_w[0:P, j, :], mix[0:P, j, :, :], AX.X, ALU.add).then_inc(mixed, 1)
                if beta is not None:
                    group = k.x_sb[0:P, ds(i * G, G), :]
                    dve.tensor_tensor(group, group, beta[0:P, :].unsqueeze(1).to_broadcast([P, G, D]), ALU.add)
                if not first:
                    add_biases(i - 1)

            turn(0, first=True)
            with dve.Fori(1, NG) as i:
                turn(i)
            add_biases(NG - 1)

        @block.scalar
        def _(act):
            with act.Fori(0, NG) as i:
                for j in range(G):
                    act.wait_ge(mix_turned, i * G + j + 1)
                    pass_on(act, gate)
                    act.activation(mix_t[:, j, :], ps_m[j % 2][0:m.n, 0:P], ACT.Copy).then_inc(mix_kept, 1)

        @block.tensor
        def _(pe):
            pe.wait_ge(bias_in, 16)

            def tiles(i, first=False):
                for j in range(G):
                    pe.wait_ge(mixed, i * G + j + 1)
                    if not first or j >= 2:
                        pe.wait_ge(mix_kept, i * G + (j - 1 if j else 0))
                    pe.transpose(ps_m[j % 2][0:m.n, 0:P], mix_w[0:P, j, :], k.ident[0:P, 0:P]).then_inc(mix_turned, 1)
                for j in range(G):
                    pe.wait_ge(mix_kept, i * G + j + 1)
                    if not first:
                        pe.wait_ge(based, i * G + j - G + 1)
                    pe.matmul(ps_b[j][0:P, :], mix_t[:, j, :], bias[:, :], start=True, stop=True).then_inc(bias_sum, 1)

            tiles(0, first=True)
            with pe.Fori(1, NG) as i:
                tiles(i)

        @block.gpsimd
        def _(pool):
            for t in range(T):
                for q in range(K):
                    pool.indirect_dma_start(
                        m.rows, bass.IndirectOffsetOnAxis(ap=m.slot_i[0:P, t * K + q:t * K + q + 1].bitcast(U32), axis=0),
                        k.xn_sb[0:P, t, :], None).then_inc(sent, 16)
            pool.wait_ge(sent, T * K * 16)


def run_experts(nc, k, m, w1_dram, w2_dram, bias_row, function):
    HC = m.hid // 128
    S = 4
    with Phase(nc, f"{m.name}_run") as ph:
        n_w1 = S if m.own_w1 else 1
        w1 = [ph.sb(f"w1_{s}", [128, 2, m.hid]) for s in range(n_w1)]
        w2 = [ph.sb(f"w2_{s}", [128, HC, D]) for s in range(S)]
        rows = [ph.sb(f"rows{s}", [128, D]) for s in range(S)]
        rows_t = [ph.sb(f"rows_t{b}", [128, 2, TOK]) for b in range(2)]
        hid = [ph.sb(f"hid{b}", [128, HC, TOK]) for b in range(2)]
        res = [ph.sb(f"res{s}", [128, D]) for s in range(S)]
        HB = HC // 4
        ps_t = [ph.ps(f"t{b}", [128, 2, TOK]) for b in range(2)]
        ps_h = [[ph.ps(f"h{b}{c}", [128, 4, TOK]) for c in range(HB)] for b in range(2)]
        ps_r = [ph.ps(f"r{b}", [128, D]) for b in range(2)]
        w1_in, w2_in, rows_in, stored = (ph.sems(x, S) for x in ("w1_in", "w2_in", "rows_in", "stored"))
        turned, kept, hid_sum, hid_made, res_sum, res_made = (
            ph.sem(x) for x in ("turned", "kept", "hid_sum", "hid_made", "res_sum", "res_made"))
        gate = ph.sem("gate")
        block = ph.ctx.enter_context(nc.Block())
        turns = m.blocks // S

        @block.sync
        def _(sp):
            if not m.own_w1:
                sp.dma_start(w1[0][:, :, :], w1_dram.rearrange("(c p) h -> p c h", p=128)).then_inc(w1_in[0], 16)

            def turn(i, first=False):
                for s in range(S):
                    n = i * S + s
                    e = sp.value_load(m.block_expert[0:1, ds(n, 1)], min_val=0, max_val=m.n - 1)
                    if not first:
                        sp.wait_ge(res_sum, n - S + 1)
                        pass_on(sp, gate)
                    sp.dma_start(rows[s][:, :], m.rows[ds(n * TOK, TOK), :]).then_inc(rows_in[s], 16)
                    if m.own_w1:
                        sp.dma_start(w1[s][:, :, :], w1_dram[ds(e, 1), :, :].rearrange("o (c p) h -> p (o c) h", p=128))\
                          .then_inc(w1_in[s], 16)
                    sp.dma_start(w2[s][:, :, :], w2_dram[ds(e, 1), :, :].rearrange("o (c p) h -> p (o c) h", p=128))\
                      .then_inc(w2_in[s], 16)

            turn(0, first=True)
            with sp.Fori(1, turns) as i:
                turn(i)

        @block.tensor
        def _(pe):
            if not m.own_w1:
                pe.wait_ge(w1_in[0], 16)

            def landed(sems, i, s):
                pe.wait_ge(sems[s % S], i * 16 + (16 if s >= 0 else 0))

            def hidden(n, i, s, b, banks_used=True):
                pe.wait_ge(kept, n + 1)
                if m.own_w1:
                    landed(w1_in, i, s)
                if banks_used:
                    pe.wait_ge(hid_made, n - 1)
                for c in range(HC):
                    for q in range(2):
                        last = pe.matmul(ps_h[b][c // 4][:, c % 4, :], w1[s % n_w1][:, q, c * 128:(c + 1) * 128],
                                         rows_t[b][:, q, :], start=(q == 0), stop=(q == 1))
                    if c % 4 == 3:
                        last.then_inc(hid_sum, 1)

            def result(n, i, s, b, bank_used=True):
                landed(w2_in, i, s)
                pe.wait_ge(hid_made, n + 1)
                if bank_used:
                    pe.wait_ge(res_made, n - 1)
                for c in range(HC):
                    last = pe.matmul(ps_r[b][:, :], hid[b][:, c, :], w2[s % S][:, c, :], start=(c == 0), stop=(c == HC - 1))
                last.then_inc(res_sum, 1)

            def turn(i, first=False):
                for s in range(S):
                    n, b = i * S + s, s % 2
                    if not first or s >= 1:
                        hidden(n - 1, i, s - 1, 1 - b, banks_used=not first or s >= 3)
                    landed(rows_in, i, s)
                    if not first or s >= 2:
                        pe.wait_ge(kept, n - 1)
                    for q in range(2):
                        last = pe.transpose(ps_t[b][:, q, :], rows[s][:, q * 128:(q + 1) * 128], k.ident[:, :])
                    last.then_inc(turned, 1)
                    if not first or s >= 2:
                        result(n - 2, i, s - 2, b, bank_used=not first)

            turn(0, first=True)
            with pe.Fori(1, turns) as i:
                turn(i)
            hidden(m.blocks - 1, turns - 1, S - 1, 1)
            result(m.blocks - 2, turns - 1, S - 2, 0)
            result(m.blocks - 1, turns - 1, S - 1, 1)

        @block.scalar
        def _(act):
            def turn(i, first=False):
                for s in range(S):
                    n, b = i * S + s, s % 2
                    e = act.value_load(m.block_expert[0:1, ds(n, 1)], min_val=0, max_val=m.n - 1) if m.own_w1 else 0
                    if not first or s >= 2:
                        act.wait_ge(res_sum, n - 1)
                    for c in range(HC):
                        if c % 4 == 0:
                            act.wait_ge(hid_sum, n * HB + c // 4 + 1)
                            pass_on(act, gate)
                        last = act.activation(hid[b][:, c, :], ps_h[b][c // 4][:, c % 4, :], function,
                                              bias=k.cols[:, ds(bias_row + c + e * HC, 1)] if m.own_w1 else
                                              k.cols[:, bias_row + c:bias_row + c + 1])
                    last.then_inc(hid_made, 1)

            turn(0, first=True)
            with act.Fori(1, turns) as i:
                turn(i)

        @block.vector
        def _(dve):
            def finish(n, i, s, b, slot_used=True):
                dve.wait_ge(res_sum, n + 1)
                if slot_used:
                    dve.wait_ge(stored[s % S], i * 16 - (16 if s < 0 else 0))
                dve.tensor_copy(res[s % S][:, :], ps_r[b][:, :]).then_inc(res_made, 1)

            def turn(i, first=False, second=False):
                for s in range(S):
                    n, b = i * S + s, s % 2
                    dve.wait_ge(turned, n + 1)
                    dve.tensor_copy(rows_t[b][:, :, :], ps_t[b][:, :, :]).then_inc(kept, 1)
                    if not first or s >= 2:
                        finish(n - 2, i, s - 2, b, slot_used=not first and not (second and s < 2))

            turn(0, first=True)
            turn(1, second=True)
            with dve.Fori(2, turns) as i:
                turn(i)
            finish(m.blocks - 2, turns - 1, S - 2, 0)
            finish(m.blocks - 1, turns - 1, S - 1, 1)

        @block.gpsimd
        def _(pool):
            with pool.Fori(0, turns) as i:
                for s in range(S):
                    n = i * S + s
                    pool.wait_ge(res_made, n + 1)
                    pass_on(pool, gate)
                    pool.dma_start(m.results[ds(n * TOK, TOK), :], res[s][:, :]).then_inc(stored[s], 16)
            for s in range(S):
                pool.wait_ge(stored[s], 16 * turns)


def best_of(dve, chain, logit, best, score, place, onehot, n, iota_down):
    wide = [P, T, n]
    chain(dve.tensor_reduce(best, logit, AX.X, ALU.max))
    chain(dve.tensor_tensor(score, logit, best.unsqueeze(2).to_broadcast(wide), ALU.is_equal))
    chain(dve.tensor_tensor(score, score, iota_down.unsqueeze(1).to_broadcast(wide), ALU.mult))
    chain(dve.tensor_reduce(place, score, AX.X, ALU.max))
    chain(dve.tensor_tensor(onehot, iota_down.unsqueeze(1).to_broadcast(wide), place.unsqueeze(2).to_broadcast(wide), ALU.is_equal))


def make_iota_down(dve, chain, k, down, n):
    chain(dve.tensor_scalar(down, k.iota[0:P, 0:n], -1.0, float(n), ALU.mult, ALU.add))


def route_first(nc, k, m):
    with Phase(nc, "route0") as ph:
        ln = GroupNorm(ph)
        gw = ph.sb("gw", [128, 2, m.n])
        xs, x_t = ph.sb("xs", [128, G, D]), ph.sb("x_t", [128, G, 2, P])
        logit, score = ph.sb("logit", [128, T, m.n]), ph.sb("score", [128, T, m.n])
        first, rest, down = ph.sb("first", [128, T, m.n]), ph.sb("rest", [128, T, m.n]), ph.sb("down", [128, m.n])
        best, place = ph.sb("best", [128, 2, T]), ph.sb("place", [128, T])
        diff, ratio, den = ph.sb("diff", [128, T]), ph.sb("ratio", [128, T]), ph.sb("den", [128, T])
        ps_t = [ph.ps(f"t{s}", [128, 2, 128]) for s in range(4)]
        ps_l = ph.ps("l", [128, G, m.n])
        w_in, turned, kept, logit_sum, logit_made = (ph.sem(x) for x in ("w_in", "turned", "kept", "logit_sum", "logit_made"))
        spread, step, diff_made, ratio_made = ph.sem("spread"), ph.sem("step"), ph.sem("diff_made"), ph.sem("ratio_made")
        gate = ph.sem("gate")
        block = ph.ctx.enter_context(nc.Block())

        @block.sync
        def _(sp):
            sp.dma_start(gw[:, :, :], k.L0_ffn_gate_w.rearrange("(c p) e -> p c e", p=128)).then_inc(w_in, 16)

        @block.vector
        def _(dve):
            def group(i, first_turn=False, last=False):
                group_rstd(dve, ln, i)
                for j in range(G):
                    if not first_turn:
                        dve.wait_ge(turned, i * G + j - G + 1)
                        dve.wait_ge(spread, i * G + j - G + 1)
                    group_tile(dve, k, ln, i, j, xs[0:P, j, :])
                if not last:
                    group_stats(dve, k, ln, i + 1)
                if not first_turn:
                    logits(i - 1)

            def logits(i):
                dve.wait_ge(logit_sum, i * G + G)
                dve.tensor_tensor(logit[0:P, ds(i * G, G), :], ps_l[0:P, :, :],
                                  k.gate_b[0:P, :].unsqueeze(1).to_broadcast([P, G, m.n]), ALU.add).then_inc(logit_made, 1)

            group_stats(dve, k, ln, 0, first=True)
            group(0, first_turn=True)
            with dve.Fori(1, NG - 1) as i:
                group(i)
            group(NG - 1, last=True)
            logits(NG - 1)

            done = [0]

            def chain(ins):
                done[0] += 1
                ins.then_inc(step, 1)
                dve.wait_ge(step, done[0])

            dve.wait_ge(logit_made, NG)
            make_iota_down(dve, chain, k, down[0:P, :], m.n)
            picks = m.onehot[0:P, :, :].rearrange("p e (t q) -> p q t e", q=2)
            best_of(dve, chain, logit[0:P, :, :], best[0:P, 0, :], score[0:P, :, :], place[0:P, :], first[0:P, :, :], m.n, down[0:P, :])
            chain(dve.tensor_copy(picks[:, 0, :, :], first[0:P, :, :]))
            chain(dve.scalar_tensor_tensor(rest[0:P, :, :], first[0:P, :, :], -3.0e38, logit[0:P, :, :], ALU.mult, ALU.add))
            best_of(dve, chain, rest[0:P, :, :], best[0:P, 1, :], score[0:P, :, :], place[0:P, :], picks[:, 1, :, :], m.n, down[0:P, :])
            dve.tensor_tensor(diff[0:P, :], best[0:P, 1, :], best[0:P, 0, :], ALU.subtract).then_inc(diff_made, 1)
            dve.wait_ge(ratio_made, 1)
            chain(dve.tensor_scalar(den[0:P, :], ratio[0:P, :], 1.0, None, ALU.add))
            chain(dve.reciprocal(den[0:P, :], den[0:P, :]))
            prob = m.prob[0:P, :].rearrange("p (t q) -> p t q", q=2)
            chain(dve.tensor_copy(prob[:, :, 0], den[0:P, :]))
            chain(dve.tensor_tensor(prob[:, :, 1], den[0:P, :], ratio[0:P, :], ALU.mult))

        @block.scalar
        def _(act):
            group_root(act, k, ln, 0)

            def tiles(i, first_turn=False, last=False):
                for j in range(G):
                    act.wait_ge(ln.out_done, i * G + j + 1)
                    pass_on(act, gate)
                    act.activation(row(k.xn_sb, i * G + j), xs[0:P, j, :], ACT.Copy).then_inc(spread, 1)
                    act.wait_ge(turned, i * G + j + 1)
                    if not first_turn:
                        act.wait_ge(logit_sum, i * G + j - G + 1)
                    act.activation(x_t[:, j, :, :], ps_t[j % 4][:, :, 0:P], ACT.Copy).then_inc(kept, 1)
                    if j == G - 1 and not last:
                        group_root(act, k, ln, i + 1)

            tiles(0, first_turn=True)
            with act.Fori(1, NG - 1) as i:
                tiles(i)
            tiles(NG - 1, last=True)
            act.wait_ge(diff_made, 1)
            act.activation(ratio[0:P, :], diff[0:P, :], ACT.Exp).then_inc(ratio_made, 1)

        @block.tensor
        def _(pe):
            pe.wait_ge(w_in, 16)

            def logits(i, first_turn=False):
                if not first_turn:
                    pe.wait_ge(logit_made, i)
                for j in range(G):
                    pe.wait_ge(kept, i * G + j + 1)
                    for q in range(2):
                        last = pe.matmul(ps_l[0:P, j, :], x_t[:, j, q, :], gw[:, q, :], start=(q == 0), stop=(q == 1))
                    last.then_inc(logit_sum, 1)

            def transposes(i, first_turn=False):
                for j in range(G):
                    pe.wait_ge(ln.out_done, i * G + j + 1)
                    if j == 4:
                        pe.wait_ge(kept, i * G + 1)
                    elif not first_turn:
                        pe.wait_ge(kept, i * G)
                    for q in range(2):
                        last = pe.transpose(ps_t[j % 4][:, q, 0:P], xs[0:P, j, q * 128:(q + 1) * 128], k.ident[0:P, 0:P])
                    last.then_inc(turned, 1)

            transposes(0, first_turn=True)
            logits(0, first_turn=True)
            with pe.Fori(1, NG) as i:
                transposes(i)
                logits(i)


def gather_results(pool, m, i, idx_made, idx_st, got, got_in, gate):
    for j in range(G):
        pool.wait_ge(idx_made, i * G + j + 1)
        pass_on(pool, gate)
        for q in range(m.picks):
            pool.indirect_dma_start(got[0:P, j, q, :], None, m.results,
                                    bass.IndirectOffsetOnAxis(ap=idx_st[0:P, j, q:q + 1].bitcast(U32), axis=0))\
                .then_inc(got_in[j], 16)


def combine_first(nc, k, m):
    K = m.picks
    with Phase(nc, f"{m.name}_combine") as ph:
        idx_st, got = ph.sb("idx_st", [128, G, K], I32), ph.sb("got", [128, G, K, D])
        stats, mv = ph.sb("stats", [128, G, 6]), ph.sb("mv", [128, G, 2])
        std, rstd, shift = ph.sb("std", [128, G]), ph.sb("rstd", [128, G]), ph.sb("shift", [128, G])
        zn = ph.sb("zn", [128, G, D])
        got_in = ph.sems("got_in", G)
        idx_made, z_made, stats_done, mv_done, std_done, rstd_done, shift_done, zn_made, scaled, gate = (
            ph.sem(x) for x in ("idx_made", "z_made", "stats_done", "mv_done", "std_done", "rstd_done", "shift_done", "zn_made",
                                "scaled", "gate"))
        block = ph.ctx.enter_context(nc.Block())

        @block.gpsimd
        def _(pool):
            with pool.Fori(0, NG) as i:
                gather_results(pool, m, i, idx_made, idx_st, got, got_in, gate)

        @block.vector
        def _(dve):
            def indices(i, j):
                dve.tensor_copy(idx_st[0:P, j, :], m.slot_i[0:P, ds((i * G + j) * K, K)]).then_inc(idx_made, 1)

            def finish(i):
                group = k.x_sb[0:P, ds(i * G, G), :]
                dve.wait_ge(zn_made, i * G + G)
                dve.tensor_tensor(zn[0:P, :, :], zn[0:P, :, :], k.gamma[0:P, :].unsqueeze(1).to_broadcast([P, G, D]), ALU.mult)\
                   .then_inc(scaled, 1)
                dve.wait_ge(scaled, i * 2 + 1)
                dve.tensor_tensor(group, zn[0:P, :, :], group, ALU.add).then_inc(scaled, 1)

            def turn(i, first=False, last=False):
                for j in range(G):
                    z = row(k.z, i * G + j)
                    dve.wait_ge(got_in[j], (i + 1) * 16 * K)
                    for q in range(K):
                        ins = dve.scalar_tensor_tensor(z, got[0:P, j, q, :], m.prob[0:P, ds((i * G + j) * K + q, 1)], z, ALU.mult, ALU.add)
                        ins.then_inc(z_made, 1)
                        dve.wait_ge(z_made, (i * G + j) * K + q + 1)
                    if not last:
                        indices(i + 1, j)
                    dve.bn_stats(stats[0:P, j, :], z).then_inc(stats_done, 1)
                if not first:
                    finish(i - 1)
                dve.wait_ge(stats_done, i * G + G)
                pass_on(dve, gate)
                for j in range(G):
                    dve.bn_aggr(mv[0:P, j, :], stats[0:P, j, :]).then_inc(mv_done, 1)
                dve.wait_ge(std_done, i + 1)
                dve.reciprocal(rstd[0:P, :], std[0:P, :]).then_inc(rstd_done, 1)
                dve.wait_ge(rstd_done, i + 1)
                dve.scalar_tensor_tensor(shift[0:P, :], mv[0:P, :, 0], -1.0, rstd[0:P, :], ALU.mult, ALU.mult).then_inc(shift_done, 1)

            for j in range(G):
                indices(0, j)
            turn(0, first=True)
            with dve.Fori(1, NG - 1) as i:
                turn(i)
            turn(NG - 1, last=True)
            finish(NG - 1)

        @block.scalar
        def _(act):
            def turn(i, first=False):
                act.wait_ge(mv_done, i * G + G)
                act.activation(std[0:P, :], mv[0:P, :, 1], ACT.Sqrt, bias=k.eps5[0:P, 0:1]).then_inc(std_done, 1)
                act.wait_ge(shift_done, i + 1)
                if not first:
                    act.wait_ge(scaled, i * 2)
                pass_on(act, gate)
                for j in range(G):
                    act.activation(zn[0:P, j, :], row(k.z, i * G + j), ACT.Identity, bias=shift[0:P, j:j + 1],
                                   scale=rstd[0:P, j:j + 1]).then_inc(zn_made, 1)

            turn(0, first=True)
            with act.Fori(1, NG) as i:
                turn(i)


def combine_second(nc, k, m):
    with Phase(nc, f"{m.name}_combine") as ph:
        idx_st, got = ph.sb("idx_st", [128, G, 1], I32), ph.sb("got", [128, G, 1, D])
        got_in = ph.sems("got_in", G)
        idx_made, x_made, stored, gate = (ph.sem(x) for x in ("idx_made", "x_made", "stored", "gate"))
        block = ph.ctx.enter_context(nc.Block())

        @block.gpsimd
        def _(pool):
            with pool.Fori(0, NG) as i:
                gather_results(pool, m, i, idx_made, idx_st, got, got_in, gate)

        @block.vector
        def _(dve):
            def indices(i, j):
                dve.tensor_copy(idx_st[0:P, j, :], m.slot_i[0:P, ds(i * G + j, 1)]).then_inc(idx_made, 1)

            def add(i, j):
                x = row(k.x_sb, i * G + j)
                dve.wait_ge(got_in[j], (i + 1) * 16)
                dve.scalar_tensor_tensor(x, got[0:P, j, 0, :], m.prob[0:P, ds(i * G + j, 1)], x, ALU.mult, ALU.add).then_inc(x_made, 1)
                dve.wait_ge(x_made, i * G + j + 1)

            for j in range(G):
                indices(0, j)
            with dve.Fori(0, NG - 1) as i:
                for j in range(G):
                    add(i, j)
                    pass_on(dve, gate)
                    indices(i + 1, j)
            for j in range(G):
                add(NG - 1, j)

        @block.sync
        def _(sp):
            with sp.Fori(0, NG) as i:
                sp.wait_ge(x_made, i * G + G)
                pass_on(sp, gate)
                sp.dma_start(k.out[ds(i * W, W), :].rearrange("(j p) d -> p j d", p=P), k.x_sb[0:P, ds(i * G, G), :]).then_inc(stored, 16)
            sp.wait_ge(stored, 16 * NG)


def vectors_apart(ap):
    return ap[:, MUL:D].rearrange("p (u c) -> p c u", c=3)


def edge_table(nc, k):
    with Phase(nc, "table") as ph:
        ln = GroupNorm(ph)
        raw = ph.sb("raw", [128, 2, 2, 128])
        w = ph.sb("w", [128, 2, 2, 128])
        xs, xq, x_t = ph.sb("xs", [128, G, D]), ph.sb("xq", [128, G, D]), ph.sb("x_t", [128, G, 2, P])
        y = ph.sb("y", [128, G, D])
        ps_t = [ph.ps(f"t{s}", [128, 2, 128]) for s in range(4)]
        ps_y = [ph.ps(f"y{s}", [128, D]) for s in range(2)]
        ps_s = [ph.ps(f"s{s}", [128, D]) for s in range(2)]
        raw_zero, raw_in, w_made = ph.sem("raw_zero"), ph.sem("raw_in"), ph.sem("w_made")
        apart, turned, kept, made, y_made, added = (ph.sem(x) for x in ("apart", "turned", "kept", "made", "y_made", "added"))
        stored, gate = ph.sem("stored"), ph.sem("gate")
        block = ph.ctx.enter_context(nc.Block())

        @block.gpsimd
        def _(pool):
            pool.memset(raw[:, :, :, :], 0.0).then_inc(raw_zero, 1)

        @block.sync
        def _(sp):
            sp.wait_ge(raw_zero, 1)
            for which, (w0, w1) in enumerate([(k.L1_gnn_lin1_w0, k.L1_gnn_lin1_w1), (k.L1_gnn_sc_w0, k.L1_gnn_sc_w1)]):
                sp.dma_start(raw[0:MUL, which, 0, 0:MUL], w0).then_inc(raw_in, 16)
                sp.dma_start(raw[MUL:128, which, 0, MUL:128], w1).then_inc(raw_in, 16)
                sp.dma_start(raw[0:MUL, which, 1, 0:MUL], w1).then_inc(raw_in, 16)
                sp.dma_start(raw[MUL:128, which, 1, MUL:128], w1).then_inc(raw_in, 16)
            with sp.Fori(0, NG) as i:
                sp.wait_ge(y_made, i * G + G)
                pass_on(sp, gate)
                sp.dma_start(k.y_dram[ds(i * W, W), :].rearrange("(j p) d -> p j d", p=P), y[0:P, :, :]).then_inc(stored, 16)
                sp.wait_ge(stored, i * 16 + 16)
                pass_on(sp, gate)

        @block.vector
        def _(dve):
            dve.wait_ge(raw_in, 128)
            dve.tensor_scalar(w[:, 0, :, :], raw[:, 0, :, :], INV_MUL, None, ALU.mult).then_inc(w_made, 1)
            dve.tensor_scalar(w[:, 1, :, :], raw[:, 1, :, :], INV_MUL * C_S, None, ALU.mult).then_inc(w_made, 1)
            def normalise(i, first=False, last=False):
                group_rstd(dve, ln, i)
                for j in range(G):
                    if not first:
                        dve.wait_ge(apart, (i * G + j - G) * 2 + 2)
                    group_tile(dve, k, ln, i, j, xs[0:P, j, :])
                if not last:
                    group_stats(dve, k, ln, i + 1)

            def add_self(i):
                for j in range(G):
                    dve.wait_ge(made, i * G + j + 1)
                    pass_on(dve, gate)
                    x, a = row(k.x_sb, i * G + j), k.node_a[0:P, ds(i * G + j, 1)]
                    dve.scalar_tensor_tensor(x[:, 0:MUL], ps_s[j % 2][0:P, 0:MUL], a, x[:, 0:MUL], ALU.mult, ALU.add).then_inc(added, 1)
                    dve.scalar_tensor_tensor(vectors_apart(x), ps_s[j % 2][0:P, MUL:D].rearrange("p (c u) -> p c u", c=3), a,
                                             vectors_apart(x), ALU.mult, ALU.add).then_inc(added, 1)

            group_stats(dve, k, ln, 0, first=True)
            normalise(0, first=True)
            with dve.Fori(1, NG - 1) as i:
                normalise(i)
                add_self(i - 1)
            normalise(NG - 1, last=True)
            add_self(NG - 2)
            add_self(NG - 1)

        @block.scalar
        def _(act):
            group_root(act, k, ln, 0)

            def take_apart(i, first=False):
                for j in range(G):
                    act.wait_ge(ln.out_done, i * G + j + 1)
                    if not first:
                        act.wait_ge(turned, i * G + j - G + 1)
                    act.activation(xq[0:P, j, 0:MUL], xs[0:P, j, 0:MUL], ACT.Copy).then_inc(apart, 1)
                    act.activation(xq[0:P, j, MUL:D].rearrange("p (c u) -> p c u", c=3), vectors_apart(xs[0:P, j, :]), ACT.Copy)\
                       .then_inc(apart, 1)

            def keep_turned(i):
                for j in range(G):
                    act.wait_ge(turned, i * G + j + 1)
                    act.activation(x_t[:, j, :, :], ps_t[j % 4][:, :, 0:P], ACT.Copy).then_inc(kept, 1)

            def scale_rows(i, first=False):
                for j in range(G):
                    act.wait_ge(made, i * G + j + 1)
                    if not first:
                        act.wait_ge(stored, i * 16)
                    pass_on(act, gate)
                    act.activation(y[0:P, j, :], ps_y[j % 2][0:P, :], ACT.Copy, scale=k.node_a[0:P, ds(i * G + j, 1)])\
                       .then_inc(y_made, 1)

            take_apart(0, first=True)
            group_root(act, k, ln, 1)
            keep_turned(0)
            take_apart(1)
            group_root(act, k, ln, 2)
            scale_rows(0, first=True)
            with act.Fori(1, NG - 2) as i:
                keep_turned(i)
                take_apart(i + 1)
                group_root(act, k, ln, i + 2)
                scale_rows(i)
            keep_turned(NG - 2)
            take_apart(NG - 1)
            scale_rows(NG - 2)
            keep_turned(NG - 1)
            scale_rows(NG - 1)

        @block.tensor
        def _(pe):
            pe.wait_ge(w_made, 2)

            def transposes(i, first=False):
                for j in range(G):
                    pe.wait_ge(apart, (i * G + j) * 2 + 2)
                    if j == 4:
                        pe.wait_ge(kept, i * G + 1)
                    elif not first:
                        pe.wait_ge(kept, i * G)
                    for q in range(2):
                        last = pe.transpose(ps_t[j % 4][:, q, 0:P], xq[0:P, j, q * 128:(q + 1) * 128], k.ident[0:P, 0:P])
                    last.then_inc(turned, 1)

            def products(i, first=False):
                for j in range(G):
                    pe.wait_ge(kept, i * G + j + 1)
                    if j >= 1 and (not first or j >= 2):
                        pe.wait_ge(y_made, i * G + j - 1)
                        pe.wait_ge(added, (i * G + j - 1) * 2)
                    elif not first:
                        pe.wait_ge(y_made, i * G)
                        pe.wait_ge(added, i * G * 2)
                    for which, ps in enumerate((ps_y, ps_s)):
                        for q in range(2):
                            last = pe.matmul(ps[j % 2][0:P, q * 128:(q + 1) * 128], x_t[:, j, q, :], w[:, which, q, :],
                                             start=True, stop=True)
                    last.then_inc(made, 1)

            transposes(0, first=True)
            products(0, first=True)
            with pe.Fori(1, NG) as i:
                transposes(i)
                products(i)


def sum_messages(nc, k):
    with Phase(nc, "msg") as ph:
        fc1, fc2_raw, fc2 = ph.sb("fc1", [2 * REC, 128]), ph.sb("fc2_raw", [128, D]), ph.sb("fc2", [128, 4, MUL])
        rec = [ph.sb(f"rec{s}", [128, 2, REC]) for s in range(SLOTS)]
        got = [ph.sb(f"got{s}", [128, 2, 4, MUL]) for s in range(SLOTS)]
        onehot = [ph.sb(f"onehot{b}", [128, 2, P]) for b in range(2)]
        onehot_ea0 = [ph.sb(f"onehot_ea0{b}", [128, 2, P]) for b in range(2)]
        attr_t = [ph.sb(f"attr_t{b}", [2 * REC, 128]) for b in range(2)]
        hid = [ph.sb(f"hid{b}", [128, 128]) for b in range(2)]
        part = [ph.sb(f"part{b}", [128, 2, 3, MUL]) for b in range(2)]
        dot = [ph.sb(f"dot{b}", [128, 2, MUL]) for b in range(2)]
        msg = [ph.sb(f"msg{b}", [128, 2, 9, MUL]) for b in range(2)]
        ps_e = [ph.ps(f"e{b}", [128, 512]) for b in range(2)]
        ps_w = [ph.ps(f"w{b}", [128, 2, 8, MUL]) for b in range(2)]
        ps_z = [ph.ps(f"z{b}", [128, 2, D]) for b in range(2)]
        w_in, w_made = ph.sem("w_in"), ph.sem("w_made")
        rec_in, got_in = ph.sems("rec_in", SLOTS), ph.sems("got_in", SLOTS)
        attr_turned, attr_kept, hid_sum, hid_made, w_sum = (
            ph.sem(x) for x in ("attr_turned", "attr_kept", "hid_sum", "hid_made", "w_sum"))
        ea0_made, part_made, masked, msg_step, msg_made, summed, added = (
            ph.sem(x) for x in ("ea0_made", "part_made", "masked", "msg_step", "msg_made", "summed", "added"))
        fc1_zero, cleared, gate = ph.sem("fc1_zero"), ph.sem("cleared"), ph.sem("gate")
        block = ph.ctx.enter_context(nc.Block())
        turns = NEB // SLOTS

        @block.sync
        def _(sp):
            sp.wait_ge(fc1_zero, 1)
            for u in range(2):
                sp.dma_start(fc1[REC * u:REC * u + 8, 64 * u:64 * u + 64], k.L1_gnn_fc_w1).then_inc(w_in, 16)
                sp.dma_start(fc2_raw[64 * u:64 * u + 64, :], k.L1_gnn_fc_w2).then_inc(w_in, 16)

            def turn(i, first=False):
                for s in range(SLOTS):
                    n = i * SLOTS + s
                    start = sp.value_load(k.block_start[0:1, ds(n, 1)], min_val=0, max_val=E)
                    if not first:
                        sp.wait_ge(summed, n - SLOTS + 1)
                        pass_on(sp, gate)
                    sp.dma_start(rec[s][:, :, :], k.recs[ds(start, EB), :].rearrange("(p u) w -> p u w", u=2))\
                      .then_inc(rec_in[s], 16)

            turn(0, first=True)
            with sp.Fori(1, turns) as i:
                turn(i)

        @block.gpsimd
        def _(pool):
            with pool.Fori(0, turns) as i:
                for s in range(SLOTS):
                    pool.wait_ge(rec_in[s], i * 16 + 16)
                    pass_on(pool, gate)
                    for u in range(2):
                        pool.indirect_dma_start(
                            got[s][:, u, :, :].rearrange("p k v -> p (k v)"), None, k.y_dram,
                            bass.IndirectOffsetOnAxis(ap=rec[s][:, u, SRC:SRC + 1].bitcast(U32), axis=0)).then_inc(got_in[s], 16)

        @block.tensor
        def _(pe):
            pe.wait_ge(w_made, 4)

            def weigh(n, b):
                pe.wait_ge(hid_made, n + 1)
                for u in range(2):
                    last = pe.matmul(ps_w[b][:, u, 0:4, :].rearrange("p k v -> p (k v)"), hid[b][64 * u:64 * u + 64, :],
                                     fc2[64 * u:64 * u + 64, :, :].rearrange("p k v -> p (k v)"), start=True, stop=True)
                last.then_inc(w_sum, 1)

            def add_up(n, b):
                pe.wait_ge(ea0_made, 2 * n + 2)
                pe.wait_ge(msg_made, n + 1)
                for h, mask in enumerate((onehot_ea0[b], onehot[b])):
                    for u in range(2):
                        last = pe.matmul(ps_z[b][0:P, h, :], mask[:, u, :],
                                         msg[b][:, u, 4 * h:4 * h + 4, :].rearrange("p k v -> p (k v)"),
                                         start=(u == 0), stop=(u == 1))
                last.then_inc(summed, 1)

            def turn(i, first=False):
                for s in range(SLOTS):
                    n, b = i * SLOTS + s, s % 2
                    pe.wait_ge(rec_in[s], i * 16 + 16)
                    if not first or s >= 2:
                        pe.wait_ge(hid_made, n - 1)
                    pe.transpose(ps_e[b][0:2 * REC, 0:128], rec[s][:, :, :].rearrange("p u w -> p (u w)"), k.ident[:, :])\
                      .then_inc(attr_turned, 1)
                    if not first or s >= 1:
                        if not first or s >= 3:
                            pe.wait_ge(msg_made, n - 2)
                        weigh(n - 1, 1 - b)
                    pe.wait_ge(attr_kept, n + 1)
                    pe.matmul(ps_e[b][:, 128:256], fc1[:, :], attr_t[b][:, :], start=True, stop=True).then_inc(hid_sum, 1)
                    if not first or s >= 2:
                        if not first or s >= 4:
                            pe.wait_ge(added, n - 3)
                        add_up(n - 2, b)

            turn(0, first=True)
            with pe.Fori(1, turns) as i:
                turn(i)
            pe.wait_ge(msg_made, NEB - 2)
            weigh(NEB - 1, 1)
            pe.wait_ge(added, NEB - 3)
            add_up(NEB - 2, 0)
            pe.wait_ge(added, NEB - 2)
            add_up(NEB - 1, 1)

        @block.scalar
        def _(act):
            def scale_parts(n, i, s, b, slot_used=True):
                act.wait_ge(got_in[s % SLOTS], i * 32 + (32 if s >= 0 else 0))
                if slot_used:
                    act.wait_ge(msg_made, n - 1)
                pass_on(act, gate)
                for u in range(2):
                    for c in range(3):
                        last = act.activation(part[b][:, u, c, :], got[s % SLOTS][:, u, 1 + c, :], ACT.Copy,
                                              scale=rec[s % SLOTS][:, u, 9 + c:10 + c])
                last.then_inc(part_made, 1)

            def scale_onehots(n, s, b):
                act.wait_ge(masked, n + 1)
                pass_on(act, gate)
                for u in range(2):
                    act.activation(onehot_ea0[b][:, u, :], onehot[b][:, u, :], ACT.Copy, scale=rec[s % SLOTS][:, u, 8:9])\
                       .then_inc(ea0_made, 1)

            def turn(i, first=False):
                for s in range(SLOTS):
                    n, b = i * SLOTS + s, s % 2
                    act.wait_ge(attr_turned, n + 1)
                    act.activation(attr_t[b][:, :], ps_e[b][0:2 * REC, 0:128], ACT.Copy).then_inc(attr_kept, 1)
                    if not first or s >= 1:
                        scale_parts(n - 1, i, s - 1, 1 - b, slot_used=not first or s >= 3)
                    act.wait_ge(hid_sum, n + 1)
                    if not first or s >= 2:
                        act.wait_ge(w_sum, n - 1)
                    act.activation(hid[b][:, :], ps_e[b][:, 128:256], ACT.Silu, scale=1.0 / math.sqrt(8)).then_inc(hid_made, 1)
                    if not first or s >= 1:
                        scale_onehots(n - 1, s - 1, 1 - b)

            turn(0, first=True)
            with act.Fori(1, turns) as i:
                turn(i)
            scale_parts(NEB - 1, turns - 1, SLOTS - 1, 1)
            scale_onehots(NEB - 1, SLOTS - 1, 1)

        @block.vector
        def _(dve):
            dve.memset(k.agg[:, :, :], 0.0).then_inc(cleared, 1)
            dve.memset(fc1[:, :], 0.0).then_inc(fc1_zero, 1)
            dve.wait_ge(w_in, 64)
            for at, (which, factor) in enumerate([(0, 1.0), (2, 1.0), (1, 1.0 / math.sqrt(3.0)), (3, 1.0)]):
                dve.tensor_scalar(fc2[:, at, :], fc2_raw[:, which * MUL:(which + 1) * MUL], SILU_NORM / 8.0 * factor, None, ALU.mult)\
                   .then_inc(w_made, 1)

            def tile_of(n):
                return dve.value_load(k.block_tile[0:1, ds(n, 1)], min_val=0, max_val=T - 1)

            def add_sum(n, b, tile, any_before=True):
                dve.wait_ge(summed, n + 1)
                if any_before:
                    dve.wait_ge(added, n)
                dve.tensor_tensor(row(k.agg, tile), ps_z[b][0:P, :, :].rearrange("p h v -> p (h v)"), row(k.agg, tile), ALU.add)\
                   .then_inc(added, 1)

            def turn(i, first=False):
                tile_before = None if first else tile_of(i * SLOTS - 1)
                for s in range(SLOTS):
                    n, b = i * SLOTS + s, s % 2
                    tile = tile_of(n)
                    dve.wait_ge(rec_in[s], i * 16 + 16)
                    if not first or s >= 2:
                        dve.wait_ge(summed, n - 1)
                    dve.tensor_tensor(onehot[b][:, :, :], node_ids(k, tile), rec[s][:, :, DST:DST + 1].to_broadcast([128, 2, P]),
                                      ALU.is_equal).then_inc(masked, 1)
                    w, y, m = ps_w[b], got[s], msg[b]
                    ea1 = rec[s][:, :, 9:12].unsqueeze(3).to_broadcast([128, 2, 3, MUL])
                    dve.wait_ge(got_in[s], i * 32 + 32)
                    dve.wait_ge(w_sum, n + 1)
                    dve.tensor_tensor(m[:, :, 0:9:8, :], w[:, :, 0:2, :], y[:, :, 0:1, :].to_broadcast([128, 2, 2, MUL]), ALU.mult)\
                       .then_inc(msg_step, 1)
                    dve.wait_ge(part_made, n + 1)
                    pass_on(dve, gate)
                    dve.tensor_reduce(dot[b][:, :, :], part[b][:, :, :, :].rearrange("p u c v -> p u v c"), AX.X, ALU.add)\
                       .then_inc(msg_step, 1)
                    dve.tensor_tensor(m[:, :, 1:4, :], w[:, :, 3:4, :].to_broadcast([128, 2, 3, MUL]), y[:, :, 1:4, :], ALU.mult)
                    dve.wait_ge(msg_step, n * 2 + 2)
                    dve.tensor_tensor(m[:, :, 5:8, :], m[:, :, 8:9, :].to_broadcast([128, 2, 3, MUL]), ea1, ALU.mult)
                    dve.tensor_tensor(m[:, :, 4, :], w[:, :, 2, :], dot[b][:, :, :], ALU.mult).then_inc(msg_made, 1)
                    if not first or s >= 1:
                        add_sum(n - 1, 1 - b, tile_before, any_before=not first or s >= 2)
                    tile_before = tile

            turn(0, first=True)
            with dve.Fori(1, turns) as i:
                turn(i)
            add_sum(NEB - 1, 1, tile_of(NEB - 1))


def update_nodes(nc, k):
    FACTOR = C_X / math.sqrt(20.0) / math.sqrt(2 * MUL)
    with Phase(nc, "update") as ph:
        raw, w = ph.sb("raw", [128, 4, 128]), ph.sb("w", [128, 4, 128])
        tile = ph.sb("tile", [128, G, 4, 128])
        tile_t = ph.sb("tile_t", [128, G, 4, P])
        ps_t = [ph.ps(f"t{s}", [128, 4, 128]) for s in range(4)]
        ps_o = [ph.ps(f"o{s}", [128, D]) for s in range(4)]
        raw_zero, raw_in, w_made, staged, turned, kept, made, added, gate = (
            ph.sem(x) for x in ("raw_zero", "raw_in", "w_made", "staged", "turned", "kept", "made", "added", "gate"))
        block = ph.ctx.enter_context(nc.Block())

        @block.sync
        def _(sp):
            w00, w01, w10, w11 = k.L1_gnn_lin2_w00, k.L1_gnn_lin2_w01, k.L1_gnn_lin2_w10, k.L1_gnn_lin2_w11
            sp.wait_ge(raw_zero, 1)
            for q, (wa, wb) in enumerate([(w00, w11), (w11, w11), (w01, w10), (w10, w10)]):
                sp.dma_start(raw[0:MUL, q, 0:MUL], wa).then_inc(raw_in, 16)
                sp.dma_start(raw[MUL:128, q, MUL:128], wb).then_inc(raw_in, 16)

        @block.vector
        def _(dve):
            dve.memset(raw[:, :, :], 0.0).then_inc(raw_zero, 1)
            dve.wait_ge(raw_in, 128)
            dve.tensor_scalar(w[:, :, :], raw[:, :, :], FACTOR, None, ALU.mult).then_inc(w_made, 1)

            def stage(i, j, first=False):
                if not first:
                    dve.wait_ge(turned, i * G + j - G + 1)
                    pass_on(dve, gate)
                dve.tensor_copy(tile[0:P, j, :, :].rearrange("p k v -> p (k v)"), row(k.agg, i * G + j)).then_inc(staged, 1)

            def add(i, j):
                dve.wait_ge(made, i * G + j + 1)
                pass_on(dve, gate)
                x, a = row(k.x_sb, i * G + j), k.node_a[0:P, ds(i * G + j, 1)]
                dve.scalar_tensor_tensor(x[:, 0:MUL], ps_o[j % 4][0:P, 0:MUL], a, x[:, 0:MUL], ALU.mult, ALU.add).then_inc(added, 1)
                dve.scalar_tensor_tensor(vectors_apart(x), ps_o[j % 4][0:P, MUL:D].rearrange("p (c u) -> p c u", c=3), a,
                                         vectors_apart(x), ALU.mult, ALU.add).then_inc(added, 1)

            for j in range(G):
                stage(0, j, first=True)
            for j in range(G):
                stage(1, j)
            with dve.Fori(1, NG - 1) as i:
                for j in range(G):
                    stage(i + 1, j)
                    add(i - 1, j)
            for i in (NG - 2, NG - 1):
                for j in range(G):
                    add(i, j)

        @block.scalar
        def _(act):
            def keep_turned(i, j, first=False):
                act.wait_ge(turned, i * G + j + 1)
                if not first:
                    act.wait_ge(made, i * G + j - G + 1)
                act.activation(tile_t[:, j, :, :], ps_t[j % 4][:, :, 0:P], ACT.Copy).then_inc(kept, 1)

            for j in range(G):
                keep_turned(0, j, first=True)
            with act.Fori(1, NG) as i:
                for j in range(G):
                    keep_turned(i, j)

        @block.tensor
        def _(pe):
            pe.wait_ge(w_made, 1)

            def transposes(i, j, first=False):
                pe.wait_ge(staged, i * G + j + 1)
                if j == 4:
                    pe.wait_ge(kept, i * G + 1)
                elif not first:
                    pe.wait_ge(kept, i * G)
                for q in range(4):
                    last = pe.transpose(ps_t[j % 4][:, q, 0:P], tile[0:P, j, q, :], k.ident[0:P, 0:P])
                last.then_inc(turned, 1)

            def products(i, j, first=False):
                pe.wait_ge(kept, i * G + j + 1)
                if j == 4:
                    pe.wait_ge(added, i * G * 2 + 2)
                elif not first:
                    pe.wait_ge(added, i * G * 2)
                for h in range(2):
                    for q in (h, h + 2):
                        last = pe.matmul(ps_o[j % 4][0:P, h * 128:(h + 1) * 128], tile_t[:, j, q, :], w[:, q, :],
                                         start=(q == h), stop=(q == h + 2))
                last.then_inc(made, 1)

            for j in range(G):
                transposes(0, j, first=True)
            for j in range(G):
                transposes(1, j)
                products(0, j, first=True)
            with pe.Fori(2, NG) as i:
                for j in range(G):
                    transposes(i, j)
                    products(i - 1, j)
            for j in range(G):
                products(NG - 1, j)


def route_second(nc, k, m):
    HC = m.hid // 128
    with Phase(nc, "route1") as ph:
        ln = GroupNorm(ph)
        w1, wg = ph.sb("w1", [128, 2, m.hid]), ph.sb("wg", [128, HC, m.n])
        xs, x_t, hid = ph.sb("xs", [128, G, D]), ph.sb("x_t", [128, 2, W]), ph.sb("hid", [128, HC, W])
        logit, score, picked = (ph.sb(x, [128, T, m.n]) for x in ("logit", "score", "picked"))
        shifted, expd, down = ph.sb("shifted", [128, T, m.n]), ph.sb("expd", [128, T, m.n]), ph.sb("down", [128, m.n])
        best, place, total = ph.sb("best", [128, T]), ph.sb("place", [128, T]), ph.sb("total", [128, T])
        ps_t = [ph.ps(f"t{s}", [128, 2, 128]) for s in range(2)]
        ps_h = [ph.ps(f"h{s}", [128, 512]) for s in range(4)]
        logit_t = ph.sb("logit_t", [m.n, N])
        ps_l = [ph.ps(f"l{c}", [128, 512]) for c in range(2)]
        w_in, turned, kept, hid_sum, hid_made, logit_sum, logit_made = (
            ph.sem(x) for x in ("w_in", "turned", "kept", "hid_sum", "hid_made", "logit_sum", "logit_made"))
        logits_back = ph.sem("logits_back")
        spread, step, shift_made, exp_made, gate = (ph.sem(x) for x in ("spread", "step", "shift_made", "exp_made", "gate"))
        block = ph.ctx.enter_context(nc.Block())
        H2 = 2 * HC

        @block.sync
        def _(sp):
            sp.dma_start(w1[:, :, :], k.L1_ffn_W1.rearrange("(c p) h -> p c h", p=128)).then_inc(w_in, 16)
            sp.dma_start(wg[:, :, :], k.L1_ffn_Wg.rearrange("(c p) h -> p c h", p=128)).then_inc(w_in, 16)

        @block.vector
        def _(dve):
            def logits(i):
                for c, (a, b) in enumerate(CUTS):
                    dve.wait_ge(logit_sum, 2 * i + c + 1)
                    dve.tensor_copy(logit_t[:, ds(i * W + a, b - a)], ps_l[c][0:m.n, 0:b - a]).then_inc(logit_made, 1)

            def group(i, first_turn=False, last=False):
                group_rstd(dve, ln, i)
                for j in range(G):
                    if not first_turn:
                        dve.wait_ge(turned, i * G + j - G + 1)
                        dve.wait_ge(spread, i * G + j - G + 1)
                    group_tile(dve, k, ln, i, j, xs[0:P, j, :])
                if not last:
                    group_stats(dve, k, ln, i + 1)
                if not first_turn:
                    logits(i - 1)

            group_stats(dve, k, ln, 0, first=True)
            group(0, first_turn=True)
            with dve.Fori(1, NG - 1) as i:
                group(i)
            group(NG - 1, last=True)
            logits(NG - 1)

            done = [0]

            def chain(ins):
                done[0] += 1
                ins.then_inc(step, 1)
                dve.wait_ge(step, done[0])

            dve.wait_ge(logits_back, 1)
            chain(dve.tensor_tensor(logit[0:P, :, :], ps_l[0][0:P, 0:T * m.n].rearrange("p (t e) -> p t e", e=m.n),
                                    k.bg[0:P, :].unsqueeze(1).to_broadcast([P, T, m.n]), ALU.add))
            make_iota_down(dve, chain, k, down[0:P, :], m.n)
            best_of(dve, chain, logit[0:P, :, :], best[0:P, :], score[0:P, :, :], place[0:P, :], picked[0:P, :, :], m.n, down[0:P, :])
            dve.tensor_tensor(shifted[0:P, :, :], logit[0:P, :, :], best[0:P, :].unsqueeze(2).to_broadcast([P, T, m.n]), ALU.subtract)\
               .then_inc(shift_made, 1)
            chain(dve.tensor_copy(m.onehot[0:P, :, :].rearrange("p e t -> p t e"), picked[0:P, :, :]))
            dve.wait_ge(exp_made, 1)
            chain(dve.tensor_reduce(total[0:P, :], expd[0:P, :, :], AX.X, ALU.add))
            chain(dve.reciprocal(m.prob[0:P, :], total[0:P, :]))

        @block.scalar
        def _(act):
            group_root(act, k, ln, 0)

            def group(i, last=False):
                for j in range(G):
                    act.wait_ge(ln.out_done, i * G + j + 1)
                    pass_on(act, gate)
                    act.activation(row(k.xn_sb, i * G + j), xs[0:P, j, :], ACT.Copy).then_inc(spread, 1)
                    act.wait_ge(turned, i * G + j + 1)
                    act.activation(x_t[:, :, j * P:(j + 1) * P], ps_t[j % 2][:, :, 0:P], ACT.Copy).then_inc(kept, 1)
                if not last:
                    group_root(act, k, ln, i + 1)
                for c, (a, b) in enumerate(CUTS):
                    for h in range(HC):
                        act.wait_ge(hid_sum, i * H2 + c * HC + h + 1)
                        act.activation(hid[:, h, a:b], ps_h[h % 4][:, 0:b - a], ACT.Gelu,
                                       bias=k.cols[:, FFN1_B1 + h:FFN1_B1 + h + 1]).then_inc(hid_made, 1)

            with act.Fori(0, NG - 1) as i:
                group(i)
            group(NG - 1, last=True)
            act.wait_ge(shift_made, 1)
            act.activation(expd[0:P, :, :], shifted[0:P, :, :], ACT.Exp).then_inc(exp_made, 1)

        @block.tensor
        def _(pe):
            pe.wait_ge(w_in, 32)
            pe.sem_inc(kept, 2)
            pe.sem_inc(hid_made, 4)

            def logits(i, bank_used=True):
                pe.wait_ge(hid_made, i * H2 + H2 + 4)
                for c, (a, b) in enumerate(CUTS):
                    if bank_used:
                        pe.wait_ge(logit_made, 2 * i + c - 1)
                    for h in range(HC):
                        last = pe.matmul(ps_l[c][0:m.n, 0:b - a], wg[:, h, :], hid[:, h, a:b], start=(h == 0), stop=(h == HC - 1))
                    last.then_inc(logit_sum, 1)

            def transposes(i):
                for j in range(G):
                    pe.wait_ge(ln.out_done, i * G + j + 1)
                    pe.wait_ge(kept, i * G + j + 1)
                    for q in range(2):
                        last = pe.transpose(ps_t[j % 2][:, q, 0:P], xs[0:P, j, q * 128:(q + 1) * 128], k.ident[0:P, 0:P])
                    last.then_inc(turned, 1)

            def hidden(i):
                pe.wait_ge(kept, i * G + G + 2)
                for c, (a, b) in enumerate(CUTS):
                    for h in range(HC):
                        pe.wait_ge(hid_made, i * H2 + c * HC + h + 1)
                        for q in range(2):
                            last = pe.matmul(ps_h[h % 4][:, 0:b - a], w1[:, q, h * 128:(h + 1) * 128], x_t[:, q, a:b],
                                             start=(q == 0), stop=(q == 1))
                        last.then_inc(hid_sum, 1)

            transposes(0)
            hidden(0)
            transposes(1)
            logits(0, bank_used=False)
            hidden(1)
            with pe.Fori(2, NG) as i:
                transposes(i)
                logits(i - 1)
                hidden(i)
            logits(NG - 1)
            pe.wait_ge(logit_made, 2 * NG)
            for t in range(T):
                last = pe.transpose(ps_l[0][0:P, t * m.n:(t + 1) * m.n], logit_t[:, t * P:(t + 1) * P], k.ident[0:m.n, 0:m.n])
            last.then_inc(logits_back, 1)


_NAMES = ['x', 'src', 'dst', 'edge_attr_4', 'edge_attr_8', 'node_vec1', 'L0_gnn_eps', 'L0_gnn_W1', 'L0_gnn_b1',
          'L0_gnn_W2', 'L0_gnn_b2', 'L0_gnn_gamma', 'L0_gnn_beta', 'L0_ffn_gate_w', 'L0_ffn_gate_b', 'L0_ffn_w1',
          'L0_ffn_b1', 'L0_ffn_w2', 'L0_ffn_b2', 'L0_ffn_gamma', 'L0_ffn_beta', 'L1_gnn_sc_w0', 'L1_gnn_sc_w1',
          'L1_gnn_lin1_w0', 'L1_gnn_lin1_w1', 'L1_gnn_fc_w1', 'L1_gnn_fc_w2', 'L1_gnn_lin2_w00', 'L1_gnn_lin2_w01',
          'L1_gnn_lin2_w10', 'L1_gnn_lin2_w11', 'L1_ffn_W1', 'L1_ffn_b1', 'L1_ffn_Wg', 'L1_ffn_bg', 'L1_ffn_Wd',
          'L1_ffn_bd']


def build(nc, inputs, out):
    k = Kept()
    (k.x, k.src, k.dst, k.edge_attr_4, k.edge_attr_8, k.node_vec1, k.L0_gnn_eps, k.L0_gnn_W1, k.L0_gnn_b1,
     k.L0_gnn_W2, k.L0_gnn_b2, k.L0_gnn_gamma, k.L0_gnn_beta, k.L0_ffn_gate_w, k.L0_ffn_gate_b, k.L0_ffn_w1,
     k.L0_ffn_b1, k.L0_ffn_w2, k.L0_ffn_b2, k.L0_ffn_gamma, k.L0_ffn_beta, k.L1_gnn_sc_w0, k.L1_gnn_sc_w1,
     k.L1_gnn_lin1_w0, k.L1_gnn_lin1_w1, k.L1_gnn_fc_w1, k.L1_gnn_fc_w2, k.L1_gnn_lin2_w00, k.L1_gnn_lin2_w01,
     k.L1_gnn_lin2_w10, k.L1_gnn_lin2_w11, k.L1_ffn_W1, k.L1_ffn_b1, k.L1_ffn_Wg, k.L1_ffn_bg, k.L1_ffn_Wd,
     k.L1_ffn_bd) = inputs
    Phase.spent.clear()
    with ExitStack() as ctx:
        def sb(name, shape, dt=F32):
            return ctx.enter_context(nc.sbuf_tensor(name, shape, dt))

        k.x_sb = sb("x_sb", [128, T, D])
        k.xn_sb = sb("xn_sb", [128, T, D])
        k.ident = sb("ident", [128, 128])
        k.below = sb("below", [128, VALS])
        k.tri = sb("tri", [128, 128], BF16)
        k.ones = sb("ones", [128, 128], BF16)
        k.onesf = sb("onesf", [128, 128])
        k.iota = sb("iota", [128, N])
        k.cols = sb("cols", [128, VEC_ROWS])
        k.gate_b = sb("gate_b", [128, 16])
        k.bg = sb("bg", [128, 8])
        k.gamma = sb("gamma", [128, D])
        k.beta = sb("beta", [128, D])
        k.eps = sb("eps", [128, 1])
        k.eps5 = sb("eps5", [128, 1])
        k.node_a = sb("node_a", [128, T])
        k.block_start = sb("block_start", [128, NEB], I32)
        k.block_tile = sb("block_tile", [128, NEB], I32)

        def dram(name, shape, dt=F32):
            return nc.dram_tensor(name, shape, dt, kind="Internal").ap()

        k.xn_dram = dram("xn_dram", [N, D])
        k.recs = dram("recs", [E + EB, REC])
        k.rows0, k.rows1 = dram("ffn0_rows", [expert_blocks(16, 2) * TOK, D]), dram("ffn1_rows", [expert_blocks(8, 1) * TOK, D])
        k.out = out
        k.y_dram = dram("y_dram", [N, D])

        load_inputs(nc, k)
        first_norm(nc, k)
        sort_edges(nc, k)
        with nc.sbuf_tensor("agg0", [128, T, D], F32) as k.agg:
            sum_neighbours(nc, k)
            gin_mlp(nc, k)
        with ExitStack() as held:
            m = Experts(nc, held, "ffn0", k.rows0, 16, 2, 512, True)
            route_first(nc, k, m)
            pick_slots(nc, k, m)
            k.z = held.enter_context(nc.sbuf_tensor("z", [128, T, D], F32))
            send_rows(nc, k, m, k.L0_ffn_b2, k.xn_sb, k.z, k.beta)
            run_experts(nc, k, m, k.L0_ffn_w1, k.L0_ffn_w2, FFN0_B1, ACT.Relu)
            combine_first(nc, k, m)
        edge_table(nc, k)
        with nc.sbuf_tensor("agg1", [128, T, 2 * D], F32) as k.agg:
            sum_messages(nc, k)
            update_nodes(nc, k)
        with ExitStack() as held:
            m = Experts(nc, held, "ffn1", k.rows1, 8, 1, 1024, False)
            route_second(nc, k, m)
            pick_slots(nc, k, m)
            send_rows(nc, k, m, k.L1_ffn_bd, k.x_sb, k.x_sb)
            run_experts(nc, k, m, k.L1_ffn_W1, k.L1_ffn_Wd, FFN1_B1, ACT.Gelu)
            combine_second(nc, k, m)


def kernel(**inputs):
    import numpy as _np
    import concourse.bacc as _bacc
    from concourse import mybir as _mybir
    from concourse.bass_utils import run_bass_kernel_spmd as _run

    nc = _bacc.Bacc("TRN2", target_bir_lowering=False, num_devices=1)
    arrays, aps = {}, []
    for name in _NAMES:
        a = _np.ascontiguousarray(inputs[name])
        arrays[f"in_{name}"] = a
        aps.append(nc.dram_tensor(f"in_{name}", a.shape, _mybir.dt.from_np(a.dtype), kind="ExternalInput").ap())
    out = nc.dram_tensor("out_0", (N, D), F32, kind="ExternalOutput").ap()
    build(nc, aps, out)
    r = _run(nc, [arrays], core_ids=[0])
    return r.results[0]["out_0"]
```
